# Optimizing a Trainium2 kernel written in Bass

```python
import numpy as np
import jax
import jax.numpy as jnp

def _softmax(x, axis=-1):
    return jax.nn.softmax(x, axis=axis)

def _gelu(x):
    return jax.nn.gelu(x, approximate=True)

def _silu(x):
    return jax.nn.silu(x)

def _sigmoid(x):
    return jax.nn.sigmoid(x)

def _layernorm(x, axis=-1, eps=1e-05):
    m = jnp.mean(x, axis=axis, keepdims=True)
    v = jnp.var(x, axis=axis, keepdims=True)
    return (x - m) / jnp.sqrt(v + eps)

def _scatter_add(tgt, idx, src, axis=0):
    return tgt.at[idx].add(src)

def _segment_sum(src, seg, n):
    return jax.ops.segment_sum(src, seg, n)
kernel_name = 'mk_adaln_d1_jaxref_r2_60d3a0'

def setup_inputs(seed: int=0):
    np.random.seed(seed)
    _w = jnp.asarray

    def _L0_attn_setup():
        import jax, jax.numpy as jnp
        import numpy as np
        EMBED_DIM = 512
        NUM_HEADS = 16
        HEAD_DIM = EMBED_DIM // NUM_HEADS

        def _feature_map(x):
            return jax.nn.elu(x) + 1.0

        def _split_heads(x, bsz, seq_len):
            return x.reshape(bsz, seq_len, NUM_HEADS, HEAD_DIM).transpose(0, 2, 1, 3)
        key = jax.random.key(seed)
        ks = jax.random.split(key, 9)
        s = 0.02
        E = EMBED_DIM
        return {'hidden_states': jax.random.normal(ks[0], (4, 2048, E), dtype=jnp.float32), 'Wq': jax.random.normal(ks[1], (E, E), dtype=jnp.float32) * s, 'bq': jnp.zeros((E,), dtype=jnp.float32), 'Wk': jax.random.normal(ks[2], (E, E), dtype=jnp.float32) * s, 'bk': jnp.zeros((E,), dtype=jnp.float32), 'Wv': jax.random.normal(ks[3], (E, E), dtype=jnp.float32) * s, 'bv': jnp.zeros((E,), dtype=jnp.float32), 'Wo': jax.random.normal(ks[4], (E, E), dtype=jnp.float32) * s, 'bo': jnp.zeros((E,), dtype=jnp.float32)}
    _L0_attn_in = _L0_attn_setup()

    def _L0_ffn_setup():
        import jax, jax.numpy as jnp
        import numpy as np
        B, S, H, DV = (4, 2048, 512, 512)
        E, INNER, P, K = (8, 32, 8, 2)

        def _ln(v, g, b, eps=1e-05):
            m = jnp.mean(v, axis=-1, keepdims=True)
            var = jnp.var(v, axis=-1, keepdims=True)
            return (v - m) * jax.lax.rsqrt(var + eps) * g + b
        key = jax.random.key(seed)
        ks = jax.random.split(key, 8)
        sc = lambda d: 1.0 / np.sqrt(d)
        return {'x': jax.random.normal(ks[0], (B, S, H), jnp.float32), 'Wv': jax.random.normal(ks[1], (DV, H), jnp.float32) * sc(H), 'bv': jnp.zeros((DV,), jnp.float32), 'Wg': jax.random.normal(ks[2], (E, DV), jnp.float32) * sc(DV), 'bg': jnp.zeros((E,), jnp.float32), 'Wp': jax.random.normal(ks[3], (E, P, DV), jnp.float32) * sc(DV), 'alpha': jnp.zeros((), jnp.float32), 'g_r': jnp.ones((E,), jnp.float32), 'b_r': jnp.zeros((E,), jnp.float32), 'g_c': jnp.ones((E,), jnp.float32), 'b_c': jnp.zeros((E,), jnp.float32), 'W1': jax.random.normal(ks[4], (E, INNER, DV), jnp.float32) * sc(DV), 'b1': jnp.zeros((E, INNER), jnp.float32), 'W2': jax.random.normal(ks[5], (E, DV, INNER), jnp.float32) * sc(INNER), 'b2': jnp.zeros((E, DV), jnp.float32)}
    _L0_ffn_in = _L0_ffn_setup()
    _L0_c = _w((lambda *s: np.random.randn(*s).astype(np.float32) * 0.05)(1, 512))
    _L0_wmod = _w((lambda *s: np.random.randn(*s).astype(np.float32) * 0.05)(512, 6 * 512) * 512 ** (-0.5))
    _d = {'L0_attn_hidden_states': _L0_attn_in['hidden_states'], 'L0_attn_Wq': _L0_attn_in['Wq'], 'L0_attn_bq': _L0_attn_in['bq'], 'L0_attn_Wk': _L0_attn_in['Wk'], 'L0_attn_bk': _L0_attn_in['bk'], 'L0_attn_Wv': _L0_attn_in['Wv'], 'L0_attn_bv': _L0_attn_in['bv'], 'L0_attn_Wo': _L0_attn_in['Wo'], 'L0_attn_bo': _L0_attn_in['bo'], 'L0_ffn_Wv': _L0_ffn_in['Wv'], 'L0_ffn_bv': _L0_ffn_in['bv'], 'L0_ffn_Wg': _L0_ffn_in['Wg'], 'L0_ffn_bg': _L0_ffn_in['bg'], 'L0_ffn_Wp': _L0_ffn_in['Wp'], 'L0_ffn_alpha': _L0_ffn_in['alpha'], 'L0_ffn_g_r': _L0_ffn_in['g_r'], 'L0_ffn_b_r': _L0_ffn_in['b_r'], 'L0_ffn_g_c': _L0_ffn_in['g_c'], 'L0_ffn_b_c': _L0_ffn_in['b_c'], 'L0_ffn_W1': _L0_ffn_in['W1'], 'L0_ffn_b1': _L0_ffn_in['b1'], 'L0_ffn_W2': _L0_ffn_in['W2'], 'L0_ffn_b2': _L0_ffn_in['b2'], 'L0_c': _L0_c, 'L0_wmod': _L0_wmod}
    _x0 = _d['L0_attn_hidden_states']
    _d['L0_attn_hidden_states'] = jax.random.normal(jax.random.fold_in(jax.random.key(seed), 1), (1, 8192, 512), dtype=_x0.dtype)
    del _x0
    return _d

def reference(L0_attn_hidden_states, L0_attn_Wq, L0_attn_bq, L0_attn_Wk, L0_attn_bk, L0_attn_Wv, L0_attn_bv, L0_attn_Wo, L0_attn_bo, L0_ffn_Wv, L0_ffn_bv, L0_ffn_Wg, L0_ffn_bg, L0_ffn_Wp, L0_ffn_alpha, L0_ffn_g_r, L0_ffn_b_r, L0_ffn_g_c, L0_ffn_b_c, L0_ffn_W1, L0_ffn_b1, L0_ffn_W2, L0_ffn_b2, L0_c, L0_wmod):

    def _L0_attn_ref(hidden_states, Wq, bq, Wk, bk, Wv, bv, Wo, bo):
        import jax, jax.numpy as jnp
        import numpy as np
        EMBED_DIM = 512
        NUM_HEADS = 16
        HEAD_DIM = EMBED_DIM // NUM_HEADS

        def _feature_map(x):
            return jax.nn.elu(x) + 1.0

        def _split_heads(x, bsz, seq_len):
            return x.reshape(bsz, seq_len, NUM_HEADS, HEAD_DIM).transpose(0, 2, 1, 3)
        bsz, tgt_len, _ = hidden_states.shape
        q = _feature_map(hidden_states @ Wq.T + bq)
        k = _feature_map(hidden_states @ Wk.T + bk)
        v = hidden_states @ Wv.T + bv
        q = _split_heads(q, bsz, tgt_len)
        k = _split_heads(k, bsz, tgt_len)
        v = _split_heads(v, bsz, tgt_len)
        KV = jnp.einsum('bhsd,bhsm->bhmd', k, v)
        Z = 1.0 / (jnp.einsum('bhsd,bhd->bhs', q, k.sum(axis=2)) + 1e-06)
        attn = jnp.einsum('bhsd,bhmd,bhs->bshm', q, KV, Z)
        attn = attn.reshape(bsz, tgt_len, EMBED_DIM)
        return attn @ Wo.T + bo

    def _L0_ffn_ref(x, Wv, bv, Wg, bg, Wp, alpha, g_r, b_r, g_c, b_c, W1, b1, W2, b2):
        import jax, jax.numpy as jnp
        import numpy as np
        B, S, H, DV = (4, 2048, 512, 512)
        E, INNER, P, K = (8, 32, 8, 2)

        def _ln(v, g, b, eps=1e-05):
            m = jnp.mean(v, axis=-1, keepdims=True)
            var = jnp.var(v, axis=-1, keepdims=True)
            return (v - m) * jax.lax.rsqrt(var + eps) * g + b
        V = jnp.einsum('bsh,dh->bsd', x, Wv) + bv
        Vf = V.reshape(-1, DV)
        r = Vf @ Wg.T + bg
        pv = jnp.einsum('epd,nd->nep', Wp, Vf)
        c = jnp.sqrt(jnp.sum(pv * pv, axis=-1)) / np.sqrt(P)
        s = _ln(r, g_r, b_r) + jax.nn.sigmoid(alpha) * _ln(c, g_c, b_c)
        topv, sel = jax.lax.top_k(s, K)
        w = jax.nn.softmax(topv, axis=-1)
        delta = jnp.zeros_like(Vf)
        for e in range(E):
            h = jax.nn.silu(Vf @ W1[e].T + b1[e])
            out = h @ W2[e].T + b2[e]
            we = jnp.sum(jnp.where(sel == e, w, 0.0), axis=-1)
            delta = delta + out * we[:, None]
        return (Vf + delta).reshape(V.shape)
    x = L0_attn_hidden_states
    mod = (_silu(L0_c) @ L0_wmod).reshape(L0_c.shape[0], 6, 1, -1)
    sa, ca, ga, sb, cb, gb = (mod[:, 0], mod[:, 1], mod[:, 2], mod[:, 3], mod[:, 4], mod[:, 5])
    ga = (2 * (ga >= 0) - 1) * jnp.maximum(jnp.abs(ga), 0.25)
    gb = (2 * (gb >= 0) - 1) * jnp.maximum(jnp.abs(gb), 0.25)
    h = _layernorm(x, axis=-1) * (1 + ca) + sa
    x = x + ga * _L0_attn_ref(h, L0_attn_Wq, L0_attn_bq, L0_attn_Wk, L0_attn_bk, L0_attn_Wv, L0_attn_bv, L0_attn_Wo, L0_attn_bo)
    h = _layernorm(x, axis=-1) * (1 + cb) + sb
    x = x + gb * _L0_ffn_ref(h, L0_ffn_Wv, L0_ffn_bv, L0_ffn_Wg, L0_ffn_bg, L0_ffn_Wp, L0_ffn_alpha, L0_ffn_g_r, L0_ffn_b_r, L0_ffn_g_c, L0_ffn_b_c, L0_ffn_W1, L0_ffn_b1, L0_ffn_W2, L0_ffn_b2)
    return x

_drawn_inputs = setup_inputs


def setup_inputs(seed=0):
    import zlib

    import numpy as np

    out = dict(_drawn_inputs(seed))
    spreads = {'L0_attn_bq': (0.0, 2.0),
     'L0_attn_bk': (0.0, 2.0),
     'L0_attn_bv': (0.0, 0.56),
     'L0_attn_bo': (0.0, 0.294),
     'L0_ffn_bv': (0.0, 0.1),
     'L0_ffn_bg': (0.0, 0.404),
     'L0_ffn_g_r': (1.0, 0.548),
     'L0_ffn_b_r': (0.0, 0.344),
     'L0_ffn_g_c': (1.0, 0.6),
     'L0_ffn_b_c': (0.0, 0.485),
     'L0_ffn_b1': (0.0, 0.689),
     'L0_ffn_b2': (0.0, 0.431)}
    factors = {'L0_attn_Wq': 21.946, 'L0_attn_Wk': 8.0, 'L0_attn_Wv': 8.0, 'L0_attn_Wo': 4.293}
    for name, (base, spread) in spreads.items():
        noise = np.random.default_rng([zlib.crc32(name.encode()), seed]).standard_normal(out[name].shape)
        drawn = base * np.exp(spread * noise) if base else spread * noise
        out[name] = jnp.asarray(drawn.astype(out[name].dtype))
    for name, factor in factors.items():
        out[name] = (out[name] * factor).astype(out[name].dtype)
    return out
```

```python
from contextlib import ExitStack

import concourse.bass as bass
from concourse import mybir

ALU = mybir.AluOpType
ACT = mybir.ActivationFunctionType
AX = mybir.AxisListType
F32 = mybir.dt.float32
F32R = mybir.dt.float32r

P = 128
D = 512
KB = D // P
HEADS = 16
DH = D // HEADS
E = 8
INNER = 32
PD = 8
HID = E * INNER
PV = E * PD
C = HID + PV + E
EPS = 1e-5
SENTINEL = -3.0e38
TAKEN = -3.3e38
LATE_LOADS = 23


def f32(ap):
    return ap.bitcast(F32)


def wait_count(eng, sem, n):
    if not isinstance(n, int) or n > 0:
        eng.wait_ge(sem, n)


def sweep(eng, step, first, last, loop_from, loop_to):
    for i in range(first, loop_from):
        step(i, i % 2)
    with eng.Fori(loop_from, loop_to, 2) as v:
        step(v, 0)
        step(v + 1, 1)
    for i in range(loop_to + 1, last + 1):
        step(i, i % 2)


def live(t, tiles):
    return not isinstance(t, int) or 0 <= t < tiles


def landed(t, slot):
    return (t - slot) * 8 + 16


def build(nc, x, Wq, bq, Wk, bk, Wv, bv, Wo, bo, fWv, fbv, Wg, bg, Wp, alpha, g_r, b_r, g_c, b_c,
          W1, b1, W2, b2, c, wmod, out):
    T = x.shape[1] // P
    assert T % 2 == 0 and T > 16
    LOOP_A = (4, T - 5)
    LOOP_B = (6, T - 5)
    xt = x.rearrange("a (t p) d -> (a t p) d", p=P)
    ot = out.rearrange("a (t p) d -> (a t p) d", p=P)
    q_dram = nc.dram_tensor("q_scratch", [T * P, D], F32, kind="Internal").ap()

    def rows(i):
        return bass.ds(i * P, P)

    ctx = ExitStack()
    with ctx:
        def sb(name, shape, dt=F32, stack=ctx):
            return stack.enter_context(nc.sbuf_tensor(name, shape, dt))

        def sem(name):
            return ctx.enter_context(nc.semaphore(name))

        ps = ctx.enter_context(nc.psum_tensor("ps", [P, 8, D], F32))

        ident = sb("ident", [P, P])
        headmask = sb("headmask", [P, P])
        ones = sb("ones", [P, P])
        neg_half = sb("neg_half", [P, 8])
        half = sb("half", [P, 8])
        raw_v = sb("raw_v", [P, KB, D])
        raw_o = sb("raw_o", [P, KB, D])
        raw_fv = sb("raw_fv", [P, KB, D])
        raw_cat = sb("raw_cat", [P, 3, D])
        raw_w2 = sb("raw_w2", [P, KB, E, INNER])
        bv_row = sb("bv_row", [P, D])
        bo_ga = sb("bo_ga", [P, D])
        fbv_row = sb("fbv_row", [P, D])
        fbv_col = sb("fbv_col", [P, KB])
        b2raw = sb("b2raw", [P, D])
        bcat = sb("bcat", [P, C])
        rt = sb("rt", [P, 5, E])
        al = sb("al", [P, 4])
        sa_col = sb("sa_col", [P, KB])
        ca1_col = sb("ca1_col", [P, KB])
        diag_out = sb("diag_out", [P, P])
        acc_v = sb("acc_v", [P, D])
        ks_acc = sb("ks_acc", [P, D])
        mod2 = sb("mod2", [P, 4, D])
        xin = sb("xin", [P, 2, D])
        stats = sb("stats", [P, 2, 6])
        mv = sb("mv", [P, 2, 2])
        veps = sb("veps", [P, 2])
        rstd = sb("rstd", [P, 2])
        xn = sb("xn", [P, 2, D])
        xT_hi = sb("xT_hi", [P, 2, D], F32R)
        xT_lo = sb("xT_lo", [P, 2, D], F32R)

        early = ExitStack()
        wk_hi = sb("wk_hi", [P, KB, D], F32R, early)
        wk_lo = sb("wk_lo", [P, KB, D], F32R, early)
        wq_hi = sb("wq_hi", [P, KB, D], F32R, early)
        wq_lo = sb("wq_lo", [P, KB, D], F32R, early)
        raw_k = sb("raw_k", [P, KB, D], F32, early)
        raw_q = sb("raw_q", [P, KB, D], F32, early)
        wm_a = sb("wm_a", [P, KB, 2 * D], F32, early)
        wm_b = sb("wm_b", [P, 4 * D], F32, early)
        bk_row = sb("bk_row", [P, D], F32, early)
        bq_row = sb("bq_row", [P, D], F32, early)
        c_col = sb("c_col", [P, 3, KB], F32, early)
        mod1 = sb("mod1", [P, 2 * D], F32, early)
        acc_k = sb("acc_k", [P, D], F32, early)
        acc_q = sb("acc_q", [P, D], F32, early)
        xn_hi = sb("xn_hi", [P, 2, D], F32R, early)
        xn_lo = sb("xn_lo", [P, 2, D], F32R, early)
        zk = sb("zk", [P, 2, D], F32, early)
        exp_k = sb("exp_k", [P, 2, D], F32, early)
        neg_k = sb("neg_k", [P, 2, D], F32, early)
        kf = sb("kf", [P, 2, D], F32, early)
        k_hi = sb("k_hi", [P, 2, D], F32R, early)
        k_lo = sb("k_lo", [P, 2, D], F32R, early)
        zq = sb("zq", [P, 2, D], F32, early)
        exp_q = sb("exp_q", [P, 2, D], F32, early)
        neg_q = sb("neg_q", [P, 2, D], F32, early)
        qf = sb("qf", [P, 2, D], F32, early)
        early.close()

        late = ExitStack()
        g_hi = sb("g_hi", [P, KB, D], F32R, late)
        g_lo = sb("g_lo", [P, KB, D], F32R, late)
        v_hi = sb("v_hi", [P, KB, D], F32R, late)
        v_lo = sb("v_lo", [P, KB, D], F32R, late)
        c_hi = sb("c_hi", [P, KB, C], F32R, late)
        c_lo = sb("c_lo", [P, KB, C], F32R, late)
        w2_hi = sb("w2_hi", [P, 2, D], F32R, late)
        w2_lo = sb("w2_lo", [P, 2, D], F32R, late)
        b2st = sb("b2st", [P, D], F32R, late)
        ks_row = sb("ks_row", [P, D], F32, late)
        q_in = sb("q_in", [P, 2, D], F32, late)
        qks = sb("qks", [P, 2, D], F32, late)
        den = sb("den", [P, 2, HEADS], F32, late)
        den_eps = sb("den_eps", [P, 2, HEADS], F32, late)
        zr = sb("zr", [P, 2, HEADS], F32, late)
        qz = sb("qz", [P, 2, D], F32, late)
        qT_hi = sb("qT_hi", [P, 2, D], F32R, late)
        qT_lo = sb("qT_lo", [P, 2, D], F32R, late)
        xb = sb("xb", [P, 2, D], F32, late)
        x1 = sb("x1", [P, 4 * D], F32, late)
        zf = sb("zf", [P, 2, C], F32, late)
        sq = sb("sq", [P, 2, PV], F32, late)
        th = sb("th", [P, 2, HID], F32, late)
        hz = sb("hz", [P, 2, HID], F32, late)
        c2 = sb("c2", [P, 2, E], F32, late)
        cn = sb("cn", [P, 2, E], F32, late)
        cs = sb("cs", [P, 2, E], F32, late)
        cmean = sb("cmean", [P, 2], F32, late)
        cc = sb("cc", [P, 2, E], F32, late)
        rsq = sb("rsq", [P, 2, 2, E], F32, late)
        rve = sb("rve", [P, 2, 2], F32, late)
        rrs = sb("rrs", [P, 2, 2], F32, late)
        s1 = sb("s1", [P, 2, E], F32, late)
        s2 = sb("s2", [P, 2, E], F32, late)
        s3 = sb("s3", [P, 2, E], F32, late)
        sx = sb("sx", [P, 2, 16], F32, late)
        m8 = sb("m8", [P, 2, 8], F32, late)
        top = sb("top", [P, 2, 8], F32, late)
        marked = sb("marked", [P, 2, 16], F32, late)
        mask = sb("mask", [P, 2, E], F32, late)
        sm = sb("sm", [P, 2, E], F32, late)
        ex = sb("ex", [P, 2, E], F32, late)
        wn = sb("wn", [P, 2, E], F32, late)
        wsum = sb("wsum", [P, 2], F32, late)
        winv = sb("winv", [P, 2], F32, late)
        wt = sb("wt", [P, 2, E], F32, late)
        aw = sb("aw", [P, 2, 3 * P], F32, late)
        aT_hi = sb("aT_hi", [P, 2, 3 * P], F32R, late)
        aT_lo = sb("aT_lo", [P, 2, 2 * P], F32R, late)
        out_t = sb("out_t", [P, 2, D], F32, late)
        wvT = sb("wvT", [P, KB, D], F32, late)
        mt = [qks[:, 0, :], qks[:, 1, :], xb[:, 0, :], xb[:, 1, :]]
        bvp_col = sb("bvp_col", [P, KB], F32, late)
        kvm = sb("kvm", [P, KB, P], F32, late)
        kv_tmp = sb("kv_tmp", [P, P], F32, late)
        woT = raw_v
        acc_fv = sb("acc_fv", [P, D], F32, late)
        acc_c = sb("acc_c", [P, C], F32, late)
        bf_row = sb("bf_row", [P, C], F32, late)
        wtmp = sb("wtmp", [P, 2, D], F32, late)
        catT = raw_o[:, :, 0:C]
        sb_col = sb("sb_col", [P, KB], F32, late)
        cb1_col = sb("cb1_col", [P, KB], F32, late)
        small = sb("small", [P, 2], F32, late)
        late.close()

        c_in = sem("c_in")
        wk_in = sem("wk_in")
        wq_in = sem("wq_in")
        wma_in = [sem(f"wma_in{b}") for b in range(KB)]
        wmb_in = [sem(f"wmb_in{b}") for b in range(KB)]
        bias_in = sem("bias_in")
        late_in = sem("late_in")
        b2_zeroed = sem("b2_zeroed")
        pool_const = sem("pool_const")
        pool_step = sem("pool_step")
        dve_const = sem("dve_const")
        dve_step = sem("dve_step")
        c_exp = sem("c_exp")
        al_exp = sem("al_exp")
        mod1_done = sem("mod1_done")
        mod2_kb_done = sem("mod2_kb_done")
        prep_psum = sem("prep_psum")
        prep_hi = sem("prep_hi")
        prep_taken = sem("prep_taken")
        prep_tmp = sem("prep_tmp")
        weights_ready = sem("weights_ready")
        x_in = [sem("x_in0"), sem("x_in1")]
        stats_done = sem("stats_done")
        mv_done = sem("mv_done")
        veps_done = sem("veps_done")
        rstd_done = sem("rstd_done")
        xn_done = sem("xn_done")
        xnh_done = sem("xnh_done")
        xnl_done = sem("xnl_done")
        xT_psum = sem("xT_psum")
        xTh_done = sem("xTh_done")
        xTl_done = sem("xTl_done")
        k_psum = sem("k_psum")
        zk_done = sem("zk_done")
        rk_done = sem("rk_done")
        ek_done = sem("ek_done")
        kf_done = sem("kf_done")
        kh_done = sem("kh_done")
        kl_done = sem("kl_done")
        ks_done = sem("ks_done")
        m_done = sem("m_done")
        q_psum = sem("q_psum")
        zq_done = sem("zq_done")
        rq_done = sem("rq_done")
        eq_done = sem("eq_done")
        qf_done = sem("qf_done")
        q_out = [sem("q_out0"), sem("q_out1")]
        bx_in = [sem("bx_in0"), sem("bx_in1")]
        q_back = [sem("q_back0"), sem("q_back1")]
        qks_done = sem("qks_done")
        den_done = sem("den_done")
        deneps_done = sem("deneps_done")
        zr_done = sem("zr_done")
        qz_done = sem("qz_done")
        xb_done = sem("xb_done")
        qT_psum = sem("qT_psum")
        qTh_done = sem("qTh_done")
        qTl_done = sem("qTl_done")
        o_psum = sem("o_psum")
        x1_done = sem("x1_done")
        bstats_done = sem("bstats_done")
        bmv_done = sem("bmv_done")
        bveps_done = sem("bveps_done")
        brstd_done = sem("brstd_done")
        x2_done = sem("x2_done")
        x2T_psum = sem("x2T_psum")
        x2Th_done = sem("x2Th_done")
        x2Tl_done = sem("x2Tl_done")
        f_psum = sem("f_psum")
        zf_done = sem("zf_done")
        sq_done = sem("sq_done")
        th_done = sem("th_done")
        hz_done = sem("hz_done")
        c2_done = sem("c2_done")
        cn_done = sem("cn_done")
        cs_done = sem("cs_done")
        cm_done = sem("cm_done")
        cc_done = sem("cc_done")
        rve_done = sem("rve_done")
        rrs_done = sem("rrs_done")
        s1_done = sem("s1_done")
        s2_done = sem("s2_done")
        s3_done = sem("s3_done")
        sx_done = sem("sx_done")
        m8_done = sem("m8_done")
        sm_done = sem("sm_done")
        top_done = sem("top_done")
        ex_done = sem("ex_done")
        marked_done = sem("marked_done")
        mask_done = sem("mask_done")
        wn_done = sem("wn_done")
        winv_done = sem("winv_done")
        wt_done = sem("wt_done")
        wth_done = sem("wth_done")
        aw_done = sem("aw_done")
        aT_psum = sem("aT_psum")
        aTh_done = sem("aTh_done")
        aTl_done = sem("aTl_done")
        y_v_done = sem("y_v_done")
        y_psum = sem("y_psum")
        fin_done = sem("fin_done")
        stored = [sem("stored0"), sem("stored1")]

        def slot4(i):
            return bass.ds(i % 4 * D, D)

        def bank_xT(s): return ps[:, 4 + s, :]
        bank_k, bank_q = ps[:, 6, :], ps[:, 7, :]
        bank_qT, bank_o, bank_f, bank_x2T = ps[:, 4, :], ps[:, 5, :], ps[:, 6, :], ps[:, 7, :]
        bank_aT = ps[:, 0, :]
        def bank_y(s): return ps[:, 1 + s, :]

        JOBS = (
            ["k0", "k1", "k2", "k3", "sa", "ca", "q0", "q1", "q2", "q3", "bk", "bq"]
            + ["ks", "ga", "sb", "cb", "gb", "v0", "v1", "v2", "v3", "o0", "o1", "o2", "o3", "bv",
               "kv", "g0", "g1", "g2", "g3", "fv0", "fv1", "fv2", "fv3", "cat0", "cat1", "cat2",
               "cat3", "u0", "u1", "u2", "u3", "bc", "bfv", "w20", "w21"])
        BANK = {}
        for n, j in enumerate(JOBS):
            BANK[j] = n % 8 if n < 12 else 4 + (n - 12) % 4
        JOB = {j: n for n, j in enumerate(JOBS)}
        TAKE = {j: n for n, j in enumerate(["sa", "ca", *[j for j in JOBS if j not in ("sa", "ca")]])}
        EARLY_JOBS = 12

        def bank(j):
            return ps[:, BANK[j], :]

        def bank_free(eng, j):
            before = [TAKE[k] for k in JOBS[:JOB[j]] if BANK[k] == BANK[j]]
            if before:
                eng.wait_ge(prep_taken, max(before) + 1)

        HI_JOBS = ["k0", "k1", "k2", "k3", "q0", "q1", "q2", "q3", "g0", "g1", "g2", "g3",
                   "fv0", "fv1", "fv2", "fv3", "u0", "u1", "u2", "u3", "w20", "w21"]
        HI = {j: n for n, j in enumerate(HI_JOBS)}
        TMP_JOBS = [j for j in HI_JOBS if j[0] in "gfw"]
        TMP = {j: n for n, j in enumerate(TMP_JOBS)}

        block = ctx.enter_context(nc.Block())

        @block.sync
        def _(sp):
            sp.dma_start(c_col[:, 0, :], c.rearrange("a (p b) -> p (a b)", p=P)).then_inc(c_in, 16)
            sp.dma_start(xin[:, 0, :], xt[rows(0), :]).then_inc(x_in[0], 16)
            sp.dma_start(raw_k[:], Wk.rearrange("(r p) f -> p r f", p=P)).then_inc(wk_in, 16)
            wm = wmod.rearrange("(p b) n -> p b n", p=P)
            for b in range(KB):
                sp.dma_start(wm_a[:, b, :], wm[:, b, 0:2 * D]).then_inc(wma_in[b], 16)
            sp.dma_start(raw_q[:], Wq.rearrange("(r p) f -> p r f", p=P)).then_inc(wq_in, 16)
            sp.dma_start(xin[:, 1, :], xt[rows(1), :]).then_inc(x_in[1], 16)
            for row, src in ((bk_row, bk), (bq_row, bq)):
                sp.dma_start(row[:], src.rearrange("(a n) -> a n", a=1).to_broadcast([P, D])).then_inc(bias_in, 16)
            sp.dma_start(wm_b[:], wm[:, 0, 2 * D:6 * D]).then_inc(wmb_in[0], 16)
            def step(i, s):
                if live(i + 4, T):
                    wait_count(sp, xn_done, i + 3)
                    sp.dma_start(xin[:, s, :], xt[rows(i + 4), :]).then_inc(x_in[s], 16)
                if live(i - 1, T):
                    sp.wait_ge(qf_done, i)
                    sp.dma_start(q_dram[rows(i - 1), :], qf[:, 1 - s, :]).then_inc(q_out[1 - s], 16)
                if isinstance(i, int) and 0 < i < KB:
                    sp.wait_ge(mod2_kb_done, i)
                    sp.dma_start(wm_b[:], wm[:, i, 2 * D:6 * D]).then_inc(wmb_in[i], 16)
                if isinstance(i, int) and i == 3:
                    late_loads()

            def late_loads():
                sp.dma_start(raw_v[:], Wv.rearrange("(r p) f -> p r f", p=P)).then_inc(late_in, 16)
                sp.dma_start(raw_o[:], Wo.rearrange("(r p) f -> p r f", p=P)).then_inc(late_in, 16)
                sp.dma_start(raw_fv[:], fWv.rearrange("(r p) f -> p r f", p=P)).then_inc(late_in, 16)
                sp.dma_start(raw_cat[:, 0:2, :], W1.rearrange("(r e) i d -> (e i) r d", r=2)).then_inc(late_in, 16)
                sp.dma_start(raw_cat[0:PV, 2, :], Wp.rearrange("e q d -> (e q) d")).then_inc(late_in, 16)
                sp.dma_start(raw_cat[PV:PV + E, 2, :], Wg).then_inc(late_in, 16)
                for b in range(KB):
                    sp.dma_start(raw_w2[:, b, :, :], W2[:, b * P:(b + 1) * P, :].rearrange("e p i -> p e i")).then_inc(late_in, 16)
                for row, src in ((bv_row, bv), (bo_ga, bo), (fbv_row, fbv)):
                    sp.dma_start(row[:], src.rearrange("(a n) -> a n", a=1).to_broadcast([P, D])).then_inc(late_in, 16)
                sp.dma_start(bcat[:, 0:HID], b1.rearrange("(a e) i -> a (e i)", a=1).to_broadcast([P, HID])).then_inc(late_in, 16)
                sp.dma_start(bcat[:, HID + PV:C], bg.rearrange("(a n) -> a n", a=1).to_broadcast([P, E])).then_inc(late_in, 16)
                for n, src in enumerate((g_r, b_r, g_c, b_c)):
                    sp.dma_start(rt[:, n, :], src.rearrange("(a n) -> a n", a=1).to_broadcast([P, E])).then_inc(late_in, 16)
                sp.dma_start(al[:, 0:1], alpha.to_broadcast([P, 1])).then_inc(late_in, 16)
                sp.wait_ge(b2_zeroed, 1)
                for r in range(3):
                    sp.dma_start(b2raw[32 * r:32 * r + E, :], b2).then_inc(late_in, 16)

            sweep(sp, step, -2, T, *LOOP_A)
            sp.wait_ge(q_out[0], landed(T - 2, 0))
            sp.wait_ge(q_out[1], landed(T - 1, 1))
            sp.wait_ge(xn_done, T)
            sp.wait_ge(m_done, T)
            sp.wait_ge(ks_done, T)

            def step_b(i, s):
                if live(i + 3, T):
                    wait_count(sp, xb_done, i + 2)
                    sp.dma_start(xin[:, 1 - s, :], xt[rows(i + 3), :]).then_inc(bx_in[1 - s], 16)
                if live(i + 4, T):
                    wait_count(sp, qz_done, i + 3)
                    sp.dma_start(q_in[:, s, :], q_dram[rows(i + 4), :]).then_inc(q_back[s], 16)
                if live(i - 3, T):
                    sp.wait_ge(fin_done, i - 2)
                    sp.dma_start(ot[rows(i - 3), :], out_t[:, 1 - s, :]).then_inc(stored[1 - s], 16)

            sweep(sp, step_b, -4, T + 2, *LOOP_B)
            sp.wait_ge(stored[0], landed(T - 2, 0))
            sp.wait_ge(stored[1], landed(T - 1, 1))

        @block.gpsimd
        def _(pool):
            steps = [0]

            def link(ins):
                steps[0] += 1
                ins.then_inc(pool_step, 1)
                pool.wait_ge(pool_step, steps[0])

            link(nc.gpsimd.memset(ident[:], 0.0))
            nc.gpsimd.affine_select(out=ident[:], in_=ident[:], compare_op=ALU.not_equal, fill=1.0,
                                    base=0, pattern=[[-1, P]], channel_multiplier=1).then_inc(pool_const, 1)
            link(nc.gpsimd.memset(headmask[:], 1.0))
            hm = headmask[:].rearrange("p (g d) -> p g d", d=DH)
            link(nc.gpsimd.affine_select(out=hm, in_=hm, compare_op=ALU.is_ge, fill=0.0, base=0,
                                         pattern=[[-DH, P // DH], [0, DH]], channel_multiplier=1))
            nc.gpsimd.affine_select(out=hm, in_=hm, compare_op=ALU.is_ge, fill=0.0, base=DH - 1,
                                    pattern=[[DH, P // DH], [0, DH]], channel_multiplier=-1).then_inc(pool_const, 1)
            link(nc.gpsimd.memset(ks_acc[:], 0.0))
            pool.wait_ge(dve_const, 1)

            def step(i, s):
                if live(i + 2, T):
                    wait_count(pool, veps_done, i + 3)
                    nc.gpsimd.tensor_tensor(rstd[:, s:s + 1], veps[:, s:s + 1], neg_half[:, 0:1],
                                            ALU.pow).then_inc(rstd_done, 1)
                if live(i, T):
                    pool.wait_ge(kf_done, i + 1)
                    wait_count(pool, ks_done, i)
                    nc.gpsimd.tensor_tensor(ks_acc[:], ks_acc[:], kf[:, s, :], ALU.add).then_inc(ks_done, 1)
                if live(i + 1, T):
                    pool.wait_ge(xnh_done, i + 2)
                    pool.wait_ge(xn_done, i + 2)
                    nc.gpsimd.tensor_tensor(xn_lo[:, 1 - s, :], xn[:, 1 - s, :], f32(xn_hi[:, 1 - s, :]),
                                            ALU.subtract).then_inc(xnl_done, 1)

            sweep(pool, step, -2, T - 1, *LOOP_A)

            pool.wait_ge(prep_taken, len(JOBS))
            pool.wait_ge(weights_ready, 1)

            def step_b(i, s):
                if live(i + 2, T):
                    wait_count(pool, zr_done, i + 3)
                    wait_count(pool, q_back[s], landed(i + 2, s))
                    wait_count(pool, qT_psum, i + 1)
                    nc.gpsimd.tensor_tensor(
                        qz[:, s, :].rearrange("p (h d) -> p h d", d=DH),
                        q_in[:, s, :].rearrange("p (h d) -> p h d", d=DH),
                        zr[:, s, :].unsqueeze(2).to_broadcast([P, HEADS, DH]), ALU.mult).then_inc(qz_done, 1)
                if live(i + 1, T):
                    wait_count(pool, bx_in[1 - s], landed(i + 1, 1 - s))
                    wait_count(pool, x1_done, i)
                    nc.gpsimd.tensor_tensor(xb[:, 1 - s, :], xin[:, 1 - s, :], bo_ga[:], ALU.add).then_inc(xb_done, 1)
                if live(i + 3, T):
                    wait_count(pool, q_back[1 - s], landed(i + 3, 1 - s))
                    wait_count(pool, den_done, i + 2)
                    nc.gpsimd.tensor_tensor(qks[:, 1 - s, :], q_in[:, 1 - s, :], ks_row[:], ALU.mult).then_inc(qks_done, 1)
                if live(i, T):
                    pool.wait_ge(bveps_done, i + 1)
                    wait_count(pool, x2_done, i - 1)
                    nc.gpsimd.tensor_tensor(rstd[:, s:s + 1], veps[:, s:s + 1], neg_half[:, 0:1],
                                            ALU.pow).then_inc(brstd_done, 1)
                if live(i - 1, T):
                    pool.wait_ge(c2_done, i)
                    wait_count(pool, cc_done, i - 2)
                    nc.gpsimd.tensor_tensor(cn[:, 1 - s, :], c2[:, 1 - s, :], half[:], ALU.pow).then_inc(cn_done, 1)
                    pool.wait_ge(rve_done, i)
                    wait_count(pool, s2_done, i - 2)
                    nc.gpsimd.tensor_tensor(rrs[:, 1 - s, :], rve[:, 1 - s, :], neg_half[:, 0:2],
                                            ALU.pow).then_inc(rrs_done, 1)

            sweep(pool, step_b, -3, T, *LOOP_B)

        @block.scalar
        def _(act):
            act.wait_ge(c_in, 16)
            nc.scalar.activation(c_col[:, 1, :], c_col[:, 0, :], ACT.Exp, scale=-1.0).then_inc(c_exp, 1)

            def hi_scaled(j, dst, col):
                act.wait_ge(prep_psum, JOB[j] + 1)
                nc.scalar.activation(dst, bank(j)[:, 0:dst.shape[1]], ACT.Copy, scale=col).then_inc(prep_hi, 1)

            act.wait_ge(prep_taken, TAKE["ca"] + 1)
            for b in range(KB):
                hi_scaled(f"k{b}", wk_hi[:, b, :], ca1_col[:, b:b + 1])
            for b in range(KB):
                hi_scaled(f"q{b}", wq_hi[:, b, :], ca1_col[:, b:b + 1])

            def step(i, s):
                if live(i + 1, T):
                    act.wait_ge(xT_psum, i + 2)
                    wait_count(act, xTl_done, i)
                    wait_count(act, q_psum, i)
                    nc.scalar.copy(xT_hi[:, 1 - s, :], bank_xT(1 - s)).then_inc(xTh_done, 1)
                if live(i - 1, T):
                    act.wait_ge(zq_done, i)
                    wait_count(act, qf_done, i - 2)
                    nc.scalar.activation(neg_q[:, 1 - s, :], zq[:, 1 - s, :], ACT.Relu, scale=-1.0).then_inc(rq_done, 1)
                    act.wait_ge(rq_done, i)
                    nc.scalar.activation(exp_q[:, 1 - s, :], neg_q[:, 1 - s, :], ACT.Exp, scale=-1.0).then_inc(eq_done, 1)
                if live(i, T):
                    act.wait_ge(zk_done, i + 1)
                    wait_count(act, kf_done, i - 1)
                    nc.scalar.activation(neg_k[:, s, :], zk[:, s, :], ACT.Relu, scale=-1.0).then_inc(rk_done, 1)
                    act.wait_ge(rk_done, i + 1)
                    nc.scalar.activation(exp_k[:, s, :], neg_k[:, s, :], ACT.Exp, scale=-1.0).then_inc(ek_done, 1)
                    act.wait_ge(kf_done, i + 1)
                    wait_count(act, m_done, i - 1)
                    wait_count(act, kl_done, i - 1)
                    nc.scalar.copy(k_hi[:, s, :], kf[:, s, :]).then_inc(kh_done, 1)
                if live(i + 1, T):
                    act.wait_ge(xn_done, i + 2)
                    wait_count(act, m_done, i)
                    wait_count(act, xnl_done, i)
                    nc.scalar.copy(xn_hi[:, 1 - s, :], xn[:, 1 - s, :]).then_inc(xnh_done, 1)

            sweep(act, step, -1, T, *LOOP_A)

            act.wait_ge(late_in, 16 * LATE_LOADS)
            nc.scalar.activation(al[:, 1:2], al[:, 0:1], ACT.Exp, scale=-1.0).then_inc(al_exp, 1)

            def hi_tmp(j, dst):
                act.wait_ge(prep_tmp, TMP[j] + 1)
                nc.scalar.copy(dst, wtmp[:, TMP[j] % 2, :]).then_inc(prep_hi, 1)

            for b in range(KB):
                hi_tmp(f"g{b}", g_hi[:, b, :])
            for b in range(KB):
                hi_tmp(f"fv{b}", v_hi[:, b, :])
            for b in range(KB):
                hi_scaled(f"u{b}", c_hi[:, b, :], cb1_col[:, b:b + 1])
            for b in range(2):
                hi_tmp(f"w2{b}", w2_hi[:, b, :])

            def step_b(i, s):
                if live(i - 1, T):
                    act.wait_ge(x2T_psum, i)
                    wait_count(act, y_v_done, i - 2)
                    nc.scalar.copy(xT_hi[:, 1 - s, :], bank_x2T).then_inc(x2Th_done, 1)
                if live(i + 1, T):
                    act.wait_ge(qT_psum, i + 2)
                    wait_count(act, o_psum, i)
                    wait_count(act, qTl_done, i)
                    nc.scalar.copy(qT_hi[:, 1 - s, :], bank_qT).then_inc(qTh_done, 1)
                if live(i - 2, T):
                    act.wait_ge(sm_done, i - 1)
                    wait_count(act, wn_done, i - 3)
                    nc.scalar.activation(ex[:, s, :], sm[:, s, :], ACT.Exp).then_inc(ex_done, 1)
                    act.wait_ge(aT_psum, i - 1)
                    wait_count(act, y_psum, i - 3)
                    nc.scalar.copy(aT_hi[:, s, :], bank_aT[:, 0:3 * P]).then_inc(aTh_done, 1)
                if live(i - 1, T):
                    act.wait_ge(zf_done, i)
                    wait_count(act, c2_done, i - 2)
                    nc.scalar.activation(sq[:, 1 - s, :], zf[:, 1 - s, HID:HID + PV], ACT.Square).then_inc(sq_done, 1)
                    wait_count(act, hz_done, i - 2)
                    nc.scalar.activation(th[:, 1 - s, :], zf[:, 1 - s, 0:HID], ACT.Tanh, scale=0.5).then_inc(th_done, 1)

            sweep(act, step_b, -1, T + 1, *LOOP_B)

        @block.vector
        def _(dve):
            steps = [0]

            def link(ins):
                steps[0] += 1
                ins.then_inc(dve_step, 1)
                dve.wait_ge(dve_step, steps[0])

            def wait_apart(sem, n):
                n = n if isinstance(n, int) else dve.snap(n)
                dve.wait_ge(dve_const, 1)
                dve.wait_ge(sem, n)

            nc.vector.memset(neg_half[:], -0.5)
            nc.vector.memset(half[:], 0.5)
            nc.vector.memset(b2raw[:], 0.0).then_inc(b2_zeroed, 1)
            nc.vector.memset(ones[:], 1.0).then_inc(dve_const, 1)

            def statistics(i, s):
                dve.wait_ge(x_in[s], landed(i, s))
                nc.vector.bn_stats(stats[:, s, :], xin[:, s, :]).then_inc(stats_done, 1)
                dve.wait_ge(stats_done, i + 1)

            def mean_var(i, s):
                nc.vector.bn_aggr(mv[:, s, :], stats[:, s, :]).then_inc(mv_done, 1)

            def var_eps(i, s):
                dve.wait_ge(mv_done, i + 1)
                nc.vector.tensor_scalar(veps[:, s:s + 1], mv[:, s, 1:2], EPS, None, ALU.add).then_inc(veps_done, 1)

            def normed(i, s):
                dve.wait_ge(rstd_done, i + 1)
                wait_count(dve, xT_psum, i - 1)
                wait_count(dve, xnh_done, i - 1)
                wait_count(dve, xnl_done, i - 1)
                nc.vector.tensor_scalar(xn[:, s, :], xin[:, s, :], mv[:, s, 0:1], rstd[:, s:s + 1],
                                        ALU.subtract, ALU.mult).then_inc(xn_done, 1)

            statistics(0, 0)
            mean_var(0, 0)
            var_eps(0, 0)
            dve.wait_ge(c_exp, 1)
            link(nc.vector.tensor_scalar(c_col[:, 2, :], c_col[:, 1, :], 1.0, None, ALU.add))
            link(nc.vector.reciprocal(c_col[:, 1, :], c_col[:, 2, :]))
            link(nc.vector.tensor_tensor(c_col[:, 2, :], c_col[:, 0, :], c_col[:, 1, :], ALU.mult))
            normed(0, 0)
            for b in range(KB):
                dve.wait_ge(wma_in[b], 16)
                if b == 0:
                    ins = nc.vector.tensor_scalar(mod1[:], wm_a[:, b, :], c_col[:, 2, b:b + 1], None, ALU.mult)
                else:
                    dve.wait_ge(mod1_done, b)
                    ins = nc.vector.scalar_tensor_tensor(out=mod1[:], in0=wm_a[:, b, :], scalar=c_col[:, 2, b:b + 1],
                                                         in1=mod1[:], op0=ALU.mult, op1=ALU.add)
                ins.then_inc(mod1_done, 1)

            def columns(dst, row, b0=0):
                for b in range(KB):
                    last = nc.vector.tensor_tensor_reduce(out=diag_out[:], in0=ident[:], in1=row[:, b * P:(b + 1) * P],
                                                          scale=1.0, scalar=b0, op0=ALU.mult, op1=ALU.add,
                                                          accum_out=dst[:, b:b + 1])
                    if b < KB - 1:
                        link(last)
                return last

            def full(j):
                dve.wait_ge(prep_psum, JOB[j] + 1)

            taken = [0]

            def taken_by(ins, j):
                assert TAKE[j] == taken[0], j
                taken[0] += 1
                ins.then_inc(prep_taken, 1)
                dve.wait_ge(prep_taken, taken[0])

            dve.wait_ge(pool_const, 1)
            full("ca")
            taken_by(columns(sa_col, bank("sa")), "sa")
            taken_by(columns(ca1_col, bank("ca"), 1.0), "ca")

            def fold(j, acc, col_bias, col_scale, hi, lo, first):
                full(j)
                dve.wait_ge(prep_hi, HI[j] + 1)
                n = acc.shape[1]
                if first:
                    link(nc.vector.tensor_scalar(acc, bank(j)[:, 0:n], col_bias, None, ALU.mult))
                else:
                    link(nc.vector.scalar_tensor_tensor(out=acc, in0=bank(j)[:, 0:n], scalar=col_bias, in1=acc,
                                                        op0=ALU.mult, op1=ALU.add))
                return nc.vector.scalar_tensor_tensor(out=lo, in0=bank(j)[:, 0:n], scalar=col_scale, in1=f32(hi),
                                                      op0=ALU.mult, op1=ALU.subtract)

            for b in range(KB):
                taken_by(fold(f"k{b}", acc_k[:], sa_col[:, b:b + 1], ca1_col[:, b:b + 1], wk_hi[:, b, :],
                              wk_lo[:, b, :], b == 0), f"k{b}")
            for b in range(KB):
                taken_by(fold(f"q{b}", acc_q[:], sa_col[:, b:b + 1], ca1_col[:, b:b + 1], wq_hi[:, b, :],
                              wq_lo[:, b, :], b == 0), f"q{b}")
            statistics(1, 1)
            mean_var(1, 1)
            var_eps(1, 1)
            normed(1, 1)
            dve.wait_ge(bias_in, 32)
            for j, row in (("bk", bk_row), ("bq", bq_row)):
                full(j)
                taken_by(nc.vector.tensor_tensor(row[:], bank(j), row[:], ALU.add), j)

            def step(i, s):
                if live(i - 1, T):
                    dve.wait_ge(q_psum, i)
                    wait_count(dve, eq_done, i - 2)
                    nc.vector.tensor_tensor(zq[:, 1 - s, :], bank_q, bq_row[:], ALU.add).then_inc(zq_done, 1)
                if live(i + 1, T):
                    dve.wait_ge(xTh_done, i + 2)
                    wait_count(dve, q_psum, i)
                    nc.vector.tensor_tensor(xT_lo[:, 1 - s, :], bank_xT(1 - s), f32(xT_hi[:, 1 - s, :]),
                                            ALU.subtract).then_inc(xTl_done, 1)
                ahead = live(i + 2, T) and not (isinstance(i, int) and i + 2 < 2)
                if ahead:
                    statistics(i + 2, s)
                if live(i - 1, T):
                    dve.wait_ge(eq_done, i)
                    wait_count(dve, q_out[1 - s], landed(i - 1, 1 - s) - 16)
                    nc.vector.scalar_tensor_tensor(out=qf[:, 1 - s, :], in0=zq[:, 1 - s, :], scalar=0.0,
                                                   in1=exp_q[:, 1 - s, :], op0=ALU.max, op1=ALU.add).then_inc(qf_done, 1)
                if ahead:
                    mean_var(i + 2, s)
                if live(i, T):
                    dve.wait_ge(k_psum, i + 1)
                    wait_count(dve, ek_done, i - 1)
                    nc.vector.tensor_tensor(zk[:, s, :], bank_k, bk_row[:], ALU.add).then_inc(zk_done, 1)
                if ahead:
                    var_eps(i + 2, s)
                    normed(i + 2, s)
                if live(i, T):
                    dve.wait_ge(ek_done, i + 1)
                    wait_count(dve, kh_done, i - 1)
                    wait_count(dve, ks_done, i - 1)
                    nc.vector.scalar_tensor_tensor(out=kf[:, s, :], in0=zk[:, s, :], scalar=0.0,
                                                   in1=exp_k[:, s, :], op0=ALU.max, op1=ALU.add).then_inc(kf_done, 1)
                    dve.wait_ge(kf_done, i + 1)
                    dve.wait_ge(kh_done, i + 1)
                    wait_count(dve, m_done, i - 1)
                    nc.vector.tensor_tensor(k_lo[:, s, :], kf[:, s, :], f32(k_hi[:, s, :]), ALU.subtract).then_inc(kl_done, 1)
                if isinstance(i, int) and 0 <= i < KB:
                    dve.wait_ge(wmb_in[i], 16)
                    m2 = mod2[:].rearrange("p v n -> p (v n)")
                    if i == 0:
                        ins = nc.vector.tensor_scalar(m2, wm_b[:], c_col[:, 2, 0:1], None, ALU.mult)
                    else:
                        dve.wait_ge(mod2_kb_done, i)
                        ins = nc.vector.scalar_tensor_tensor(out=m2, in0=wm_b[:], scalar=c_col[:, 2, i:i + 1],
                                                             in1=m2, op0=ALU.mult, op1=ALU.add)
                    ins.then_inc(mod2_kb_done, 1)

            sweep(dve, step, -1, T, *LOOP_A)

            dve.wait_ge(late_in, 16 * LATE_LOADS)
            dve.wait_ge(m_done, T)
            dve.wait_ge(ks_done, T)
            dve.wait_ge(q_out[0], landed(T - 2, 0))
            dve.wait_ge(q_out[1], landed(T - 1, 1))
            dve.wait_ge(pool_const, 2)
            nc.vector.memset(f32(b2st[:]), 0.0)
            nc.vector.memset(aw[:], 0.0)
            nc.vector.memset(sx[:], SENTINEL)
            link(nc.vector.memset(top[:], SENTINEL))
            full("ks")
            taken_by(nc.vector.tensor_copy(ks_row[:], bank("ks")), "ks")

            def gate(j, v):
                full(j)
                link(nc.vector.tensor_scalar(wtmp[:, 0, :], bank(j), 0.0, 2.0, ALU.is_ge, ALU.mult))
                link(nc.vector.tensor_scalar(wtmp[:, 0, :], wtmp[:, 0, :], 1.0, None, ALU.subtract))
                taken_by(nc.vector.tensor_tensor(wtmp[:, 1, :], bank(j), wtmp[:, 0, :], ALU.mult), j)
                link(nc.vector.scalar_tensor_tensor(out=mod2[:, v, :], in0=wtmp[:, 1, :], scalar=0.25,
                                                    in1=wtmp[:, 0, :], op0=ALU.max, op1=ALU.mult))

            GA, SB, CB, GB = range(4)
            gate("ga", GA)
            for j, col, b0 in (("sb", sb_col, 0.0), ("cb", cb1_col, 1.0)):
                full(j)
                taken_by(columns(col, bank(j), b0), j)
            gate("gb", GB)
            ga, gb = mod2[:, GA, :], mod2[:, GB, :]
            link(nc.vector.tensor_tensor(bo_ga[:], bo_ga[:], ga, ALU.mult))
            for b in range(KB):
                link(nc.vector.tensor_scalar(mt[b], ps[:, b, :], ca1_col[:, b:b + 1], None, ALU.mult))
            for b in range(KB):
                full(f"v{b}")
                link(nc.vector.tensor_copy(wvT[:, b, :], bank(f"v{b}")))
                if b == 0:
                    ins = nc.vector.tensor_scalar(acc_v[:], bank("v0"), sa_col[:, 0:1], None, ALU.mult)
                else:
                    ins = nc.vector.scalar_tensor_tensor(out=acc_v[:], in0=bank(f"v{b}"), scalar=sa_col[:, b:b + 1],
                                                         in1=acc_v[:], op0=ALU.mult, op1=ALU.add)
                taken_by(ins, f"v{b}")
            for b in range(KB):
                full(f"o{b}")
                taken_by(nc.vector.tensor_copy(woT[:, b, :], bank(f"o{b}")), f"o{b}")
            full("bv")
            taken_by(nc.vector.tensor_tensor(bv_row[:], bank("bv"), bv_row[:], ALU.add), "bv")
            link(columns(bvp_col, bv_row[:]))
            full("kv")
            for b in range(KB):
                blk = slice(b * P, (b + 1) * P)
                link(nc.vector.scalar_tensor_tensor(out=kv_tmp[:], in0=ks_row[:, blk], scalar=bvp_col[:, b:b + 1],
                                                    in1=bank("kv")[:, blk], op0=ALU.mult, op1=ALU.add))
                ins = nc.vector.tensor_tensor(kvm[:, b, :], kv_tmp[:], headmask[:], ALU.mult)
                if b < KB - 1:
                    link(ins)
            taken_by(ins, "kv")

            def split_tmp(j, make, lo, hi, extra=None):
                full(j)
                t = TMP[j]
                make(wtmp[:, t % 2, :]).then_inc(prep_tmp, 1)
                dve.wait_ge(prep_tmp, t + 1)
                dve.wait_ge(prep_hi, HI[j] + 1)
                if extra is not None:
                    link(nc.vector.tensor_tensor(lo, wtmp[:, t % 2, :], f32(hi), ALU.subtract))
                    taken_by(extra(), j)
                else:
                    taken_by(nc.vector.tensor_tensor(lo, wtmp[:, t % 2, :], f32(hi), ALU.subtract), j)

            for b in range(KB):
                j = f"g{b}"
                split_tmp(j, lambda o, j=j: nc.vector.tensor_tensor(o, bank(j), ga, ALU.mult), g_lo[:, b, :], g_hi[:, b, :])
            for b in range(KB):
                j = f"fv{b}"

                def bias_sum(j=j, b=b):
                    if b == 0:
                        return nc.vector.tensor_scalar(acc_fv[:], bank(j), sb_col[:, 0:1], None, ALU.mult)
                    return nc.vector.scalar_tensor_tensor(out=acc_fv[:], in0=bank(j), scalar=sb_col[:, b:b + 1],
                                                          in1=acc_fv[:], op0=ALU.mult, op1=ALU.add)

                split_tmp(j, lambda o, j=j, b=b: nc.vector.scalar_tensor_tensor(
                    out=o, in0=bank(j), scalar=cb1_col[:, b:b + 1], in1=gb, op0=ALU.mult, op1=ALU.mult),
                    v_lo[:, b, :], v_hi[:, b, :], bias_sum)
            link(columns(fbv_col, fbv_row[:]))
            for b in range(KB):
                j = f"cat{b}"
                full(j)
                lg = slice(HID + PV, C)
                link(nc.vector.tensor_copy(catT[:, b, :], bank(j)[:, 0:C]))
                link(nc.vector.tensor_reduce(small[:, 0:1], catT[:, b, lg], AX.X, ALU.add))
                link(nc.vector.tensor_scalar(small[:, 1:2], small[:, 0:1], 1.0 / E, None, ALU.mult))
                link(nc.vector.tensor_scalar(catT[:, b, lg], catT[:, b, lg], small[:, 1:2], None, ALU.subtract))
                if b == 0:
                    ins = nc.vector.tensor_scalar(acc_c[:], catT[:, 0, :], fbv_col[:, 0:1], None, ALU.mult)
                else:
                    ins = nc.vector.scalar_tensor_tensor(out=acc_c[:], in0=catT[:, b, :], scalar=fbv_col[:, b:b + 1],
                                                         in1=acc_c[:], op0=ALU.mult, op1=ALU.add)
                taken_by(ins, j)
            for b in range(KB):
                j = f"u{b}"
                taken_by(fold(j, acc_c[:], sb_col[:, b:b + 1], cb1_col[:, b:b + 1], c_hi[:, b, :], c_lo[:, b, :], False), j)
            lg = slice(HID + PV, C)
            link(nc.vector.memset(bcat[:, HID:HID + PV], 0.0))
            link(nc.vector.tensor_reduce(small[:, 0:1], bcat[:, lg], AX.X, ALU.add))
            link(nc.vector.tensor_scalar(small[:, 1:2], small[:, 0:1], 1.0 / E, None, ALU.mult))
            link(nc.vector.tensor_scalar(bcat[:, lg], bcat[:, lg], small[:, 1:2], None, ALU.subtract))
            full("bc")
            taken_by(nc.vector.tensor_tensor(bf_row[:], bank("bc")[:, 0:C], bcat[:], ALU.add), "bc")
            full("bfv")
            link(nc.vector.tensor_tensor(b2raw[:], b2raw[:], fbv_row[:], ALU.add))
            taken_by(nc.vector.tensor_tensor(b2raw[:], bank("bfv"), b2raw[:], ALU.add), "bfv")
            link(nc.vector.tensor_tensor(b2raw[:], b2raw[:], gb, ALU.mult))
            for r in (0, 64):
                nc.vector.tensor_copy(b2st[r:r + E, :], b2raw[r:r + E, :])
            link(nc.vector.tensor_copy(b2st[32:32 + E, :], b2raw[32:32 + E, :]))
            link(nc.vector.tensor_tensor(b2raw[32:32 + E, :], b2raw[32:32 + E, :], f32(b2st[32:32 + E, :]), ALU.subtract))
            link(nc.vector.tensor_copy(b2st[32:32 + E, :], b2raw[32:32 + E, :]))
            for b in range(2):
                j = f"w2{b}"
                split_tmp(j, lambda o, j=j: nc.vector.scalar_tensor_tensor(
                    out=o, in0=bank(j), scalar=0.5, in1=gb, op0=ALU.mult, op1=ALU.mult), w2_lo[:, b, :], w2_hi[:, b, :])
            dve.wait_ge(al_exp, 1)
            link(nc.vector.tensor_scalar(al[:, 2:3], al[:, 1:2], 1.0, None, ALU.add))
            link(nc.vector.reciprocal(al[:, 3:4], al[:, 2:3]))
            link(nc.vector.tensor_scalar(rt[:, 2, :], rt[:, 2, :], al[:, 3:4], None, ALU.mult))
            link(nc.vector.scalar_tensor_tensor(out=rt[:, 4, :], in0=rt[:, 3, :], scalar=al[:, 3:4], in1=rt[:, 1, :],
                                                op0=ALU.mult, op1=ALU.add))
            nc.vector.tensor_copy(small[:, 0:1], bf_row[:, 0:1]).then_inc(weights_ready, 1)
            gr_row, gc_row, bias_row = rt[:, 0, :], rt[:, 2, :], rt[:, 4, :]

            def denominators(t, s):
                dve.wait_ge(qks_done, t + 1)
                nc.vector.tensor_reduce(den[:, s, :], qks[:, s, :].rearrange("p (h d) -> p h d", d=DH),
                                        AX.X, ALU.add).then_inc(den_done, 1)
                dve.wait_ge(den_done, t + 1)
                nc.vector.tensor_scalar(den_eps[:, s, :], den[:, s, :], 1e-6, None, ALU.add).then_inc(deneps_done, 1)
                dve.wait_ge(deneps_done, t + 1)
                wait_count(dve, qz_done, t - 1)
                nc.vector.reciprocal(zr[:, s, :], den_eps[:, s, :]).then_inc(zr_done, 1)

            def scores(t, s):
                dve.wait_ge(rrs_done, t + 1)
                nc.vector.scalar_tensor_tensor(out=s1[:, s, :], in0=zf[:, s, HID + PV:C], scalar=rrs[:, s, 0:1],
                                               in1=gr_row, op0=ALU.mult, op1=ALU.mult).then_inc(s1_done, 1)
                nc.vector.scalar_tensor_tensor(out=s2[:, s, :], in0=cc[:, s, :], scalar=rrs[:, s, 1:2],
                                               in1=gc_row, op0=ALU.mult, op1=ALU.mult).then_inc(s2_done, 1)
                dve.wait_ge(s1_done, t + 1)
                nc.vector.tensor_tensor(s3[:, s, :], s1[:, s, :], bias_row, ALU.add).then_inc(s3_done, 1)
                dve.wait_ge(s2_done, t + 1)
                dve.wait_ge(s3_done, t + 1)
                nc.vector.tensor_tensor(sx[:, s, 0:E], s2[:, s, :], s3[:, s, :], ALU.add).then_inc(sx_done, 1)
                wait_apart(sx_done, t + 1)
                nc.vector.max(m8[:, s, :], sx[:, s, 0:E]).then_inc(m8_done, 1)
                dve.wait_ge(m8_done, t + 1)
                wait_count(dve, ex_done, t - 1)
                nc.vector.tensor_scalar(sm[:, s, :], sx[:, s, 0:E], m8[:, s, 0:1], None, ALU.subtract).then_inc(sm_done, 1)
                nc.vector.tensor_copy(top[:, s, 0:2], m8[:, s, 0:2]).then_inc(top_done, 1)
                wait_apart(top_done, t + 1)
                nc.vector.match_replace(marked[:, s, 0:14], top[:, s, :], sx[:, s, 0:14], TAKEN).then_inc(marked_done, 1)
                dve.wait_ge(marked_done, t + 1)
                nc.vector.tensor_tensor(mask[:, s, :], marked[:, s, 0:E], sx[:, s, 0:E], ALU.not_equal).then_inc(mask_done, 1)

            def weights(t, s):
                dve.wait_ge(ex_done, t + 1)
                dve.wait_ge(mask_done, t + 1)
                nc.vector.tensor_tensor_reduce(out=wn[:, s, :], in0=ex[:, s, :], in1=mask[:, s, :], scale=1.0,
                                               scalar=0.0, op0=ALU.mult, op1=ALU.add,
                                               accum_out=wsum[:, s:s + 1]).then_inc(wn_done, 1)
                dve.wait_ge(wn_done, t + 1)
                nc.vector.reciprocal(winv[:, s:s + 1], wsum[:, s:s + 1]).then_inc(winv_done, 1)
                dve.wait_ge(winv_done, t + 1)
                nc.vector.tensor_scalar(wt[:, s, :], wn[:, s, :], winv[:, s:s + 1], None, ALU.mult).then_inc(wt_done, 1)
                dve.wait_ge(wt_done, t + 1)
                dve.wait_ge(hz_done, t + 1)
                wait_count(dve, aT_psum, t - 1)
                for col in (2 * P, 2 * P + 32):
                    nc.vector.tensor_copy(aw[:, s, col:col + E].bitcast(F32R), wt[:, s, :]).then_inc(wth_done, 1)
                nc.vector.tensor_tensor(
                    aw[:, s, 0:HID].rearrange("p (e i) -> p e i", i=INNER),
                    hz[:, s, :].rearrange("p (e i) -> p e i", i=INNER),
                    wt[:, s, :].unsqueeze(2).to_broadcast([P, E, INNER]), ALU.mult)
                dve.wait_ge(wth_done, 2 * t + 2)
                nc.vector.tensor_tensor(aw[:, s, 2 * P + 64:2 * P + 64 + E], wt[:, s, :], aw[:, s, 2 * P:2 * P + E],
                                        ALU.subtract).then_inc(aw_done, 1)

            def step_b(i, s):
                if live(i - 1, T):
                    dve.wait_ge(x2Th_done, i)
                    wait_count(dve, y_v_done, i - 2)
                    nc.vector.tensor_tensor(xT_lo[:, 1 - s, :], bank_x2T, f32(xT_hi[:, 1 - s, :]),
                                            ALU.subtract).then_inc(x2Tl_done, 1)
                if live(i + 1, T):
                    dve.wait_ge(qTh_done, i + 2)
                    wait_count(dve, o_psum, i)
                    nc.vector.tensor_tensor(qT_lo[:, 1 - s, :], bank_qT, f32(qT_hi[:, 1 - s, :]),
                                            ALU.subtract).then_inc(qTl_done, 1)
                if live(i - 2, T):
                    scores(i - 2, s)
                if live(i - 3, T):
                    dve.wait_ge(y_psum, i - 2)
                    wait_count(dve, stored[1 - s], landed(i - 3, 1 - s) - 16)
                    nc.vector.tensor_tensor(out_t[:, 1 - s, :], bank_y(1 - s), x1[:, slot4(i - 3)], ALU.add).then_inc(fin_done, 1)
                if live(i - 2, T):
                    weights(i - 2, s)
                if live(i, T):
                    dve.wait_ge(o_psum, i + 1)
                    dve.wait_ge(xb_done, i + 1)
                    nc.vector.tensor_tensor(x1[:, slot4(i)], bank_o, xb[:, s, :], ALU.add).then_inc(x1_done, 1)
                    wait_apart(x1_done, i + 1)
                    nc.vector.bn_stats(stats[:, s, :], x1[:, slot4(i)]).then_inc(bstats_done, 1)
                    wait_apart(bstats_done, i + 1)
                    nc.vector.bn_aggr(mv[:, s, :], stats[:, s, :]).then_inc(bmv_done, 1)
                    dve.wait_ge(bmv_done, i + 1)
                    nc.vector.tensor_scalar(veps[:, s:s + 1], mv[:, s, 1:2], EPS, None, ALU.add).then_inc(bveps_done, 1)
                if live(i - 1, T):
                    dve.wait_ge(f_psum, i)
                    wait_count(dve, sq_done, i - 2)
                    wait_count(dve, th_done, i - 2)
                    nc.vector.tensor_tensor(zf[:, 1 - s, :], bank_f[:, 0:C], bf_row[:], ALU.add).then_inc(zf_done, 1)
                if live(i - 2, T):
                    dve.wait_ge(aTh_done, i - 1)
                    wait_count(dve, y_psum, i - 3)
                    nc.vector.tensor_tensor(aT_lo[:, s, :], bank_aT[:, 0:2 * P], f32(aT_hi[:, s, 0:2 * P]),
                                            ALU.subtract).then_inc(aTl_done, 1)
                if live(i - 1, T):
                    p = 1 - s
                    dve.wait_ge(sq_done, i)
                    wait_count(dve, cn_done, i - 2)
                    nc.vector.tensor_reduce(cs[:, p, :], sq[:, p, :].rearrange("p (e q) -> p e q", q=PD),
                                            AX.X, ALU.add).then_inc(cs_done, 1)
                    dve.wait_ge(cs_done, i)
                    nc.vector.tensor_scalar(c2[:, p, :], cs[:, p, :], 1.0 / PD, None, ALU.mult).then_inc(c2_done, 1)
                if live(i, T):
                    dve.wait_ge(brstd_done, i + 1)
                    wait_count(dve, x2T_psum, i - 1)
                    nc.vector.tensor_scalar(xn[:, s, :], x1[:, slot4(i)], mv[:, s, 0:1], rstd[:, s:s + 1],
                                            ALU.subtract, ALU.mult).then_inc(x2_done, 1)
                if live(i - 1, T):
                    dve.wait_ge(th_done, i)
                    nc.vector.scalar_tensor_tensor(out=hz[:, p, :], in0=th[:, p, :], scalar=1.0, in1=zf[:, p, 0:HID],
                                                   op0=ALU.add, op1=ALU.mult).then_inc(hz_done, 1)
                if live(i + 3, T):
                    denominators(i + 3, 1 - s)
                if live(i - 1, T):
                    dve.wait_ge(cn_done, i)
                    nc.vector.tensor_scalar(cs[:, p, :], cn[:, p, :], 1.0 / E, 0.0, ALU.mult, ALU.add,
                                            accum_out=cmean[:, p:p + 1]).then_inc(cm_done, 1)
                    dve.wait_ge(cm_done, i)
                    nc.vector.tensor_scalar(cc[:, p, :], cn[:, p, :], cmean[:, p:p + 1], None, ALU.subtract).then_inc(cc_done, 1)
                    wait_count(dve, rrs_done, i - 2)
                    lgp = zf[:, p, HID + PV:C]
                    nc.vector.tensor_tensor_reduce(out=rsq[:, p, 0, :], in0=lgp, in1=lgp, scale=1.0 / E, scalar=EPS,
                                                   op0=ALU.mult, op1=ALU.add, accum_out=rve[:, p, 0:1])
                    dve.wait_ge(cc_done, i)
                    nc.vector.tensor_tensor_reduce(out=rsq[:, p, 1, :], in0=cc[:, p, :], in1=cc[:, p, :], scale=1.0 / E,
                                                   scalar=EPS, op0=ALU.mult, op1=ALU.add,
                                                   accum_out=rve[:, p, 1:2]).then_inc(rve_done, 1)

            sweep(dve, step_b, -3, T + 2, *LOOP_B)

        @block.tensor
        def _(pe):
            pe.wait_ge(dve_const, 1)
            pe.wait_ge(pool_const, 1)

            def three(dst, parts, start, stop):
                for n, (ah, al_, bh, bl) in enumerate(parts):
                    s0 = start and n == 0
                    s1_ = stop and n == len(parts) - 1
                    nc.tensor.matmul(dst, ah, bh, start=s0, stop=False)
                    nc.tensor.matmul(dst, ah, bl, start=False, stop=False)
                    last = nc.tensor.matmul(dst, al_, bh, start=False, stop=s1_)
                return last

            def transposes(j, srcs):
                bank_free(pe, j)
                col = 0
                for src in srcs:
                    k = src.shape[0]
                    last = nc.tensor.transpose(bank(j)[:, col:col + k], src, ident[0:k, 0:k])
                    col += k
                last.then_inc(prep_psum, 1)

            def blocks_of(raw, fb):
                return [raw[:, r, fb * P:(fb + 1) * P] for r in range(KB)]

            def sum_rows(j, acc):
                bank_free(pe, j)
                nc.tensor.matmul(bank(j)[:, 0:acc.shape[1]], ones[:], acc, start=True, stop=True).then_inc(prep_psum, 1)

            pe.wait_ge(wk_in, 16)
            for b in range(KB):
                transposes(f"k{b}", blocks_of(raw_k, b))
            pe.wait_ge(mod1_done, KB)
            sum_rows("sa", mod1[:, 0:D])
            sum_rows("ca", mod1[:, D:2 * D])
            pe.wait_ge(wq_in, 16)
            for b in range(KB):
                transposes(f"q{b}", blocks_of(raw_q, b))
            pe.wait_ge(prep_taken, TAKE["q3"] + 1)
            sum_rows("bk", acc_k[:])
            sum_rows("bq", acc_q[:])

            def step(i, s):
                if live(i + 1, T):
                    pe.wait_ge(xn_done, i + 2)
                    wait_count(pe, xTl_done, i)
                    for b in range(KB):
                        blk = slice(b * P, (b + 1) * P)
                        last = nc.tensor.transpose(bank_xT(1 - s)[:, blk], xn[:, 1 - s, blk], ident[:])
                    last.then_inc(xT_psum, 1)
                if live(i, T):
                    if isinstance(i, int) and i == 0:
                        pe.wait_ge(prep_taken, EARLY_JOBS)
                    pe.wait_ge(xTl_done, i + 1)
                    wait_count(pe, zk_done, i)
                    three(bank_k, [(xT_hi[:, s, b * P:(b + 1) * P], xT_lo[:, s, b * P:(b + 1) * P],
                                    wk_hi[:, b, :], wk_lo[:, b, :]) for b in range(KB)], True, True).then_inc(k_psum, 1)
                if live(i - 1, T):
                    p = 1 - s
                    first = isinstance(i, int) and i == 1
                    final = isinstance(i, int) and i == T
                    pe.wait_ge(xnl_done, i)
                    pe.wait_ge(kl_done, i)
                    for b in range(KB):
                        blk = slice(b * P, (b + 1) * P)
                        last = three(ps[:, b, :], [(xn_hi[:, p, blk], xn_lo[:, p, blk], k_hi[:, p, :], k_lo[:, p, :])],
                                     first, final)
                    last.then_inc(m_done, 1)
                if live(i, T):
                    wait_count(pe, zq_done, i)
                    three(bank_q, [(xT_hi[:, s, b * P:(b + 1) * P], xT_lo[:, s, b * P:(b + 1) * P],
                                    wq_hi[:, b, :], wq_lo[:, b, :]) for b in range(KB)], True, True).then_inc(q_psum, 1)

            sweep(pe, step, -1, T, *LOOP_A)

            pe.wait_ge(late_in, 16 * LATE_LOADS)
            pe.wait_ge(zq_done, T)
            pe.wait_ge(ks_done, T)
            sum_rows("ks", ks_acc[:])
            pe.wait_ge(mod2_kb_done, KB)
            for v, j in enumerate(("ga", "sb", "cb", "gb")):
                sum_rows(j, mod2[:, v, :])
            for b in range(KB):
                transposes(f"v{b}", blocks_of(raw_v, b))
            for b in range(KB):
                transposes(f"o{b}", blocks_of(raw_o, b))
            pe.wait_ge(prep_taken, TAKE["v3"] + 1)
            sum_rows("bv", acc_v[:])
            bank_free(pe, "kv")
            pe.wait_ge(prep_taken, TAKE["v3"] + 1)
            for b in range(KB):
                blk = slice(b * P, (b + 1) * P)
                for f in range(KB):
                    last = nc.tensor.matmul(bank("kv")[:, blk], wvT[:, f, blk], mt[f][:, blk], start=(f == 0), stop=(f == KB - 1))
            last.then_inc(prep_psum, 1)
            pe.wait_ge(prep_taken, TAKE["kv"] + 1)
            for b in range(KB):
                bank_free(pe, f"g{b}")
                nc.tensor.matmul(bank(f"g{b}"), kvm[:, b, :], woT[:, b, :], start=True, stop=True).then_inc(prep_psum, 1)
            for b in range(KB):
                transposes(f"fv{b}", blocks_of(raw_fv, b))
            for b in range(KB):
                blk = slice(b * P, (b + 1) * P)
                transposes(f"cat{b}", [raw_cat[:, 0, blk], raw_cat[:, 1, blk], raw_cat[0:PV + E, 2, blk]])
            pe.wait_ge(prep_taken, TAKE["cat3"] + 1)
            for b in range(KB):
                j = f"u{b}"
                bank_free(pe, j)
                for d in range(KB):
                    last = nc.tensor.matmul(bank(j)[:, 0:C], raw_fv[:, d, b * P:(b + 1) * P], catT[:, d, :],
                                            start=(d == 0), stop=(d == KB - 1))
                last.then_inc(prep_psum, 1)
            pe.wait_ge(prep_taken, TAKE["u3"] + 1)
            sum_rows("bc", acc_c[:])
            sum_rows("bfv", acc_fv[:])
            for b in range(2):
                transposes(f"w2{b}", [raw_w2[:, d, 4 * b:4 * b + 4, :].rearrange("p e i -> p (e i)") for d in range(KB)])
            pe.wait_ge(weights_ready, 1)

            def step_b(i, s):
                if live(i + 1, T):
                    pe.wait_ge(qz_done, i + 2)
                    wait_count(pe, qTl_done, i + 1)
                    for b in range(KB):
                        blk = slice(b * P, (b + 1) * P)
                        last = nc.tensor.transpose(bank_qT[:, blk], qz[:, 1 - s, blk], ident[:])
                    last.then_inc(qT_psum, 1)
                if live(i, T):
                    pe.wait_ge(qTl_done, i + 1)
                    wait_count(pe, x1_done, i)
                    three(bank_o, [(qT_hi[:, s, b * P:(b + 1) * P], qT_lo[:, s, b * P:(b + 1) * P],
                                    g_hi[:, b, :], g_lo[:, b, :]) for b in range(KB)], True, True).then_inc(o_psum, 1)
                p = 1 - s
                x2T = [(xT_hi[:, p, b * P:(b + 1) * P], xT_lo[:, p, b * P:(b + 1) * P]) for b in range(KB)]
                if live(i - 1, T):
                    pe.wait_ge(x2Tl_done, i)
                    wait_count(pe, zf_done, i - 1)
                    three(bank_f[:, 0:C], [(*x2T[b], c_hi[:, b, :], c_lo[:, b, :]) for b in range(KB)],
                          True, True).then_inc(f_psum, 1)
                if live(i - 2, T):
                    pe.wait_ge(aw_done, i - 1)
                    wait_count(pe, aTl_done, i - 2)
                    for b in range(3):
                        blk = slice(b * P, (b + 1) * P)
                        last = nc.tensor.transpose(bank_aT[:, blk], aw[:, s, blk], ident[:])
                    last.then_inc(aT_psum, 1)
                if live(i - 1, T):
                    wait_count(pe, fin_done, i - 2)
                    three(bank_y(p), [(*x2T[b], v_hi[:, b, :], v_lo[:, b, :]) for b in range(KB)],
                          True, False).then_inc(y_v_done, 1)
                if live(i - 2, T):
                    pe.wait_ge(aTl_done, i - 1)
                    nc.tensor.matmul(bank_y(s), aT_hi[:, s, 2 * P:3 * P], b2st[:], start=False, stop=False)
                    three(bank_y(s), [(aT_hi[:, s, b * P:(b + 1) * P], aT_lo[:, s, b * P:(b + 1) * P],
                                       w2_hi[:, b, :], w2_lo[:, b, :]) for b in range(2)], False, True).then_inc(y_psum, 1)
                if live(i, T):
                    pe.wait_ge(x2_done, i + 1)
                    wait_count(pe, x2Tl_done, i)
                    for b in range(KB):
                        blk = slice(b * P, (b + 1) * P)
                        last = nc.tensor.transpose(bank_x2T[:, blk], xn[:, s, blk], ident[:])
                    last.then_inc(x2T_psum, 1)

            sweep(pe, step_b, -1, T + 1, *LOOP_B)


_INS = ["L0_attn_hidden_states", "L0_attn_Wq", "L0_attn_bq", "L0_attn_Wk", "L0_attn_bk", "L0_attn_Wv",
        "L0_attn_bv", "L0_attn_Wo", "L0_attn_bo", "L0_ffn_Wv", "L0_ffn_bv", "L0_ffn_Wg", "L0_ffn_bg",
        "L0_ffn_Wp", "L0_ffn_alpha", "L0_ffn_g_r", "L0_ffn_b_r", "L0_ffn_g_c", "L0_ffn_b_c", "L0_ffn_W1",
        "L0_ffn_b1", "L0_ffn_W2", "L0_ffn_b2", "L0_c", "L0_wmod"]


def kernel(**inputs):
    import numpy as _np
    import concourse.bacc as _bacc
    from concourse import mybir as _mybir
    from concourse.bass_utils import run_bass_kernel_spmd as _run

    nc = _bacc.Bacc("TRN2", target_bir_lowering=False, num_devices=1)
    arrays, args = {}, []
    for name in _INS:
        a = _np.ascontiguousarray(inputs[name])
        if name == "L0_ffn_alpha":
            a = a.reshape(1, 1)
        arrays[f"in_{name}_dram"] = a
        args.append(nc.dram_tensor(f"in_{name}_dram", a.shape, _mybir.dt.from_np(a.dtype), kind="ExternalInput").ap())
    shape = inputs["L0_attn_hidden_states"].shape
    args.append(nc.dram_tensor("out_0_dram", shape, _mybir.dt.float32, kind="ExternalOutput").ap())
    build(nc, *args)
    r = _run(nc, [arrays], core_ids=[0])
    return r.results[0]["out_0_dram"]
```

```python
from contextlib import ExitStack

import concourse.bass as bass
from concourse import mybir

ALU = mybir.AluOpType
ACT = mybir.ActivationFunctionType
AX = mybir.AxisListType
F32 = mybir.dt.float32
F32R = mybir.dt.float32r

P = 128
D = 512
KB = D // P
HEADS = 16
DH = D // HEADS
E = 8
INNER = 32
PD = 8
HID = E * INNER
PV = E * PD
C = HID + PV + E
EPS = 1e-5
SENTINEL = -3.0e38
TAKEN = -3.3e38
LATE_LOADS = 23


def f32(ap):
    return ap.bitcast(F32)


def wait_count(eng, sem, n):
    if not isinstance(n, int) or n > 0:
        eng.wait_ge(sem, n)


def sweep(eng, step, first, last, loop_from, loop_to):
    for i in range(first, loop_from):
        step(i, i % 2)
    with eng.Fori(loop_from, loop_to, 2) as v:
        step(v, 0)
        step(v + 1, 1)
    for i in range(loop_to + 1, last + 1):
        step(i, i % 2)


def sweep_pairs(eng, step, first, last, loop_from, loop_to):
    for j in range(first, loop_from):
        step(j)
    with eng.Fori(loop_from, loop_to + 1) as v:
        step(v)
    for j in range(loop_to + 1, last + 1):
        step(j)


def live(t, tiles):
    return not isinstance(t, int) or 0 <= t < tiles


def landed(t, slot):
    return (t - slot) * 8 + 16


def build(nc, x, Wq, bq, Wk, bk, Wv, bv, Wo, bo, fWv, fbv, Wg, bg, Wp, alpha, g_r, b_r, g_c, b_c,
          W1, b1, W2, b2, c, wmod, out):
    T = x.shape[1] // P
    assert T % 2 == 0 and T > 16
    LOOP_A = (4, T - 5)
    J = T // 2
    LOOP_B = (3, J - 3)
    xt = x.rearrange("a (t p) d -> (a t p) d", p=P)
    ot = out.rearrange("a (t p) d -> (a t p) d", p=P)
    q_dram = nc.dram_tensor("q_scratch", [T * P, D], F32, kind="Internal").ap()

    def rows(i):
        return bass.ds(i * P, P)

    ctx = ExitStack()
    with ctx:
        def sb(name, shape, dt=F32, stack=ctx):
            return stack.enter_context(nc.sbuf_tensor(name, shape, dt))

        def sem(name):
            return ctx.enter_context(nc.semaphore(name))

        ps = ctx.enter_context(nc.psum_tensor("ps", [P, 8, D], F32))

        ident = sb("ident", [P, P])
        headmask = sb("headmask", [P, P])
        ones = sb("ones", [P, P])
        neg_half = sb("neg_half", [P, 8])
        half = sb("half", [P, 8])
        raw_v = sb("raw_v", [P, KB, D])
        raw_o = sb("raw_o", [P, KB, D])
        raw_fv = sb("raw_fv", [P, KB, D])
        raw_cat = sb("raw_cat", [P, 3, D])
        raw_w2 = sb("raw_w2", [P, KB, E, INNER])
        bv_row = sb("bv_row", [P, D])
        bo_ga = sb("bo_ga", [P, D])
        fbv_row = sb("fbv_row", [P, D])
        fbv_col = sb("fbv_col", [P, KB])
        b2raw = sb("b2raw", [P, D])
        bcat = sb("bcat", [P, C])
        rt = sb("rt", [P, 5, E])
        al = sb("al", [P, 4])
        sa_col = sb("sa_col", [P, KB])
        ca1_col = sb("ca1_col", [P, KB])
        diag_out = sb("diag_out", [P, P])
        acc_v = sb("acc_v", [P, D])
        ks_acc = sb("ks_acc", [P, D])
        mod2 = sb("mod2", [P, 4, D])
        xin = sb("xin", [P, 2, D])
        stats = sb("stats", [P, 2, 6])
        mv = sb("mv", [P, 2, 2])
        veps = sb("veps", [P, 2])
        rstd = sb("rstd", [P, 2])
        xn = sb("xn", [P, 2, D])
        xT_hi = sb("xT_hi", [P, 2, D], F32R)
        xT_lo = sb("xT_lo", [P, 2, D], F32R)

        early = ExitStack()
        wk_hi = sb("wk_hi", [P, KB, D], F32R, early)
        wk_lo = sb("wk_lo", [P, KB, D], F32R, early)
        wq_hi = sb("wq_hi", [P, KB, D], F32R, early)
        wq_lo = sb("wq_lo", [P, KB, D], F32R, early)
        raw_k = sb("raw_k", [P, KB, D], F32, early)
        raw_q = sb("raw_q", [P, KB, D], F32, early)
        wm_a = sb("wm_a", [P, KB, 2 * D], F32, early)
        wm_b = sb("wm_b", [P, 4 * D], F32, early)
        bk_row = sb("bk_row", [P, D], F32, early)
        bq_row = sb("bq_row", [P, D], F32, early)
        c_col = sb("c_col", [P, 3, KB], F32, early)
        mod1 = sb("mod1", [P, 2 * D], F32, early)
        acc_k = sb("acc_k", [P, D], F32, early)
        acc_q = sb("acc_q", [P, D], F32, early)
        xn_hi = sb("xn_hi", [P, 2, D], F32R, early)
        xn_lo = sb("xn_lo", [P, 2, D], F32R, early)
        zk = sb("zk", [P, 2, D], F32, early)
        exp_k = sb("exp_k", [P, 2, D], F32, early)
        neg_k = sb("neg_k", [P, 2, D], F32, early)
        kf = sb("kf", [P, 2, D], F32, early)
        k_hi = sb("k_hi", [P, 2, D], F32R, early)
        k_lo = sb("k_lo", [P, 2, D], F32R, early)
        zq = sb("zq", [P, 2, D], F32, early)
        exp_q = sb("exp_q", [P, 2, D], F32, early)
        neg_q = sb("neg_q", [P, 2, D], F32, early)
        qf = sb("qf", [P, 2, D], F32, early)
        early.close()

        late = ExitStack()
        g_hi = sb("g_hi", [P, KB, D], F32R, late)
        g_lo = sb("g_lo", [P, KB, D], F32R, late)
        v_hi = sb("v_hi", [P, KB, D], F32R, late)
        v_lo = sb("v_lo", [P, KB, D], F32R, late)
        c_hi = sb("c_hi", [P, KB, C], F32R, late)
        c_lo = sb("c_lo", [P, KB, C], F32R, late)
        w2_hi = sb("w2_hi", [P, 2, D], F32R, late)
        w2_lo = sb("w2_lo", [P, 2, D], F32R, late)
        b2st = sb("b2st", [P, D], F32R, late)
        ks_row = sb("ks_row", [P, D], F32, late)
        q_in = sb("q_in", [P, 2, D], F32, late)
        qks = sb("qks", [P, 2, D], F32, late)
        den = sb("den", [P, 2, HEADS], F32, late)
        den_eps = sb("den_eps", [P, 2, HEADS], F32, late)
        zr = sb("zr", [P, 2, HEADS], F32, late)
        qz = sb("qz", [P, 2, D], F32, late)
        qT_hi = sb("qT_hi", [P, 2, D], F32R, late)
        qT_lo = sb("qT_lo", [P, 2, D], F32R, late)
        xb = sb("xb", [P, 2, D], F32, late)
        x1 = sb("x1", [P, 6 * D], F32, late)
        zf = sb("zf", [P, 2, C + E], F32, late)
        sq = sb("sq", [P, 2, PV], F32, late)
        th = sb("th", [P, 2, HID], F32, late)
        hz = sb("hz", [P, 2, HID], F32, late)
        c2 = sb("c2", [P, 2, E], F32, late)
        cn = sb("cn", [P, 2, E], F32, late)
        csum = sb("csum", [P, 2], F32, late)
        rsq = sb("rsq", [P, 2, 2, E], F32, late)
        rvar = sb("rvar", [P, 4], F32, late)
        rve = sb("rve", [P, 4], F32, late)
        rrs = sb("rrs", [P, 2, 2], F32, late)
        s1 = sb("s1", [P, 2, 2, E], F32, late)
        s2 = sb("s2", [P, 2, 2, E], F32, late)
        s3 = sb("s3", [P, 2, E], F32, late)
        sx = sb("sx", [P, 2, 16], F32, late)
        m8 = sb("m8", [P, 2, 8], F32, late)
        top = sb("top", [P, 2, 8], F32, late)
        marked = sb("marked", [P, 2, 16], F32, late)
        mask = sb("mask", [P, 2, E], F32, late)
        sm = sb("sm", [P, 2, E], F32, late)
        ex = sb("ex", [P, 2, E], F32, late)
        wn = sb("wn", [P, 2, E], F32, late)
        wsum = sb("wsum", [P, 2], F32, late)
        winv = sb("winv", [P, 2], F32, late)
        wt = sb("wt", [P, 2, E], F32, late)
        aw = sb("aw", [P, 2, 3 * P], F32, late)
        aT_hi = sb("aT_hi", [P, 2, 3 * P], F32R, late)
        aT_lo = sb("aT_lo", [P, 2, 2 * P], F32R, late)
        out_t = sb("out_t", [P, 2, D], F32, late)
        wvT = sb("wvT", [P, KB, D], F32, late)
        mt = [qks[:, 0, :], qks[:, 1, :], xb[:, 0, :], xb[:, 1, :]]
        bvp_col = sb("bvp_col", [P, KB], F32, late)
        kvm = sb("kvm", [P, KB, P], F32, late)
        kv_tmp = sb("kv_tmp", [P, P], F32, late)
        woT = raw_v
        acc_fv = sb("acc_fv", [P, D], F32, late)
        acc_c = sb("acc_c", [P, C], F32, late)
        bf_row = sb("bf_row", [P, C], F32, late)
        wtmp = sb("wtmp", [P, 2, D], F32, late)
        catT = raw_o[:, :, 0:C]
        sb_col = sb("sb_col", [P, KB], F32, late)
        cb1_col = sb("cb1_col", [P, KB], F32, late)
        small = sb("small", [P, 2], F32, late)
        late.close()

        c_in = sem("c_in")
        wk_in = sem("wk_in")
        wq_in = sem("wq_in")
        wma_in = [sem(f"wma_in{b}") for b in range(KB)]
        wmb_in = [sem(f"wmb_in{b}") for b in range(KB)]
        bias_in = sem("bias_in")
        late_in = sem("late_in")
        b2_zeroed = sem("b2_zeroed")
        pool_const = sem("pool_const")
        pool_step = sem("pool_step")
        dve_const = sem("dve_const")
        dve_step = sem("dve_step")
        c_exp = sem("c_exp")
        al_exp = sem("al_exp")
        mod1_done = sem("mod1_done")
        mod2_kb_done = sem("mod2_kb_done")
        prep_psum = sem("prep_psum")
        prep_hi = sem("prep_hi")
        prep_taken = sem("prep_taken")
        prep_tmp = sem("prep_tmp")
        weights_ready = sem("weights_ready")
        x_in = [sem("x_in0"), sem("x_in1")]
        stats_done = sem("stats_done")
        mv_done = sem("mv_done")
        veps_done = sem("veps_done")
        rstd_done = sem("rstd_done")
        xn_done = sem("xn_done")
        xnh_done = sem("xnh_done")
        xnl_done = sem("xnl_done")
        xT_psum = sem("xT_psum")
        xTh_done = sem("xTh_done")
        xTl_done = sem("xTl_done")
        k_psum = sem("k_psum")
        zk_done = sem("zk_done")
        rk_done = sem("rk_done")
        ek_done = sem("ek_done")
        kf_done = sem("kf_done")
        kh_done = sem("kh_done")
        kl_done = sem("kl_done")
        ks_done = sem("ks_done")
        m_done = sem("m_done")
        q_psum = sem("q_psum")
        zq_done = sem("zq_done")
        rq_done = sem("rq_done")
        eq_done = sem("eq_done")
        qf_done = sem("qf_done")
        q_out = [sem("q_out0"), sem("q_out1")]
        bx_in = sem("bx_in")
        q_back = sem("q_back")
        qks_done = sem("qks_done")
        den_done = sem("den_done")
        deneps_done = sem("deneps_done")
        zr_done = sem("zr_done")
        qz_done = sem("qz_done")
        xb_done = sem("xb_done")
        bveps_done = sem("bveps_done")
        brstd_done = sem("brstd_done")
        hz_done = sem("hz_done")
        csum_done = sem("csum_done")
        cc_done = sem("cc_done")
        rsq_done = sem("rsq_done")
        rvar_done = sem("rvar_done")
        rve_done = sem("rve_done")
        rrs_done = sem("rrs_done")
        s1_done = sem("s1_done")
        s2_done = sem("s2_done")
        s3_done = sem("s3_done")
        sx_done = sem("sx_done")
        m8_done = sem("m8_done")
        sm_done = sem("sm_done")
        top_done = sem("top_done")
        ex_done = sem("ex_done")
        marked_done = sem("marked_done")
        mask_done = sem("mask_done")
        wn_done = sem("wn_done")
        wsum_done = sem("wsum_done")
        winv_done = sem("winv_done")
        wt_done = sem("wt_done")
        wth_done = sem("wth_done")
        aw_done = sem("aw_done")
        qT_psum = sem("qT_psum")
        qTh_done = sem("qTh_done")
        qTl_done = sem("qTl_done")
        o_psum = sem("o_psum")
        x1_done = sem("x1_done")
        bstats_done = sem("bstats_done")
        bmv_done = sem("bmv_done")
        x2_done = sem("x2_done")
        x2T_psum = sem("x2T_psum")
        x2Th_done = sem("x2Th_done")
        x2Tl_done = sem("x2Tl_done")
        f_psum = sem("f_psum")
        zf_done = sem("zf_done")
        sq_done = sem("sq_done")
        th_done = sem("th_done")
        c2_done = sem("c2_done")
        cn_done = sem("cn_done")
        aT_psum = sem("aT_psum")
        aTh_done = sem("aTh_done")
        aTl_done = sem("aTl_done")
        y_v_done = sem("y_v_done")
        y_psum = sem("y_psum")
        fin_done = sem("fin_done")
        stored = [sem("stored0"), sem("stored1")]

        def x1_of(j, h):
            return x1[:, bass.ds(j % 3 * (2 * D) + h * D, D)]

        def bank_xT(s): return ps[:, 4 + s, :]
        bank_k, bank_q = ps[:, 6, :], ps[:, 7, :]
        bank_qaT, bank_x2T, bank_o, bank_f = ps[:, 4, :], ps[:, 5, :], ps[:, 6, :], ps[:, 7, :]
        def bank_y(h): return ps[:, h, :]

        JOBS = (
            ["k0", "k1", "k2", "k3", "sa", "ca", "q0", "q1", "q2", "q3", "bk", "bq"]
            + ["ks", "ga", "sb", "cb", "gb", "v0", "v1", "v2", "v3", "o0", "o1", "o2", "o3", "bv",
               "kv", "g0", "g1", "g2", "g3", "fv0", "fv1", "fv2", "fv3", "cat0", "cat1", "cat2",
               "cat3", "u0", "u1", "u2", "u3", "bc", "bfv", "w20", "w21"])
        BANK = {}
        for n, j in enumerate(JOBS):
            BANK[j] = n % 8 if n < 12 else 4 + (n - 12) % 4
        JOB = {j: n for n, j in enumerate(JOBS)}
        TAKE = {j: n for n, j in enumerate(["sa", "ca", *[j for j in JOBS if j not in ("sa", "ca")]])}
        EARLY_JOBS = 12

        def bank(j):
            return ps[:, BANK[j], :]

        def bank_free(eng, j):
            before = [TAKE[k] for k in JOBS[:JOB[j]] if BANK[k] == BANK[j]]
            if before:
                eng.wait_ge(prep_taken, max(before) + 1)

        HI_JOBS = ["k0", "k1", "k2", "k3", "q0", "q1", "q2", "q3", "g0", "g1", "g2", "g3",
                   "fv0", "fv1", "fv2", "fv3", "u0", "u1", "u2", "u3", "w20", "w21"]
        HI = {j: n for n, j in enumerate(HI_JOBS)}
        TMP_JOBS = [j for j in HI_JOBS if j[0] in "gfw"]
        TMP = {j: n for n, j in enumerate(TMP_JOBS)}

        block = ctx.enter_context(nc.Block())

        @block.sync
        def _(sp):
            sp.dma_start(c_col[:, 0, :], c.rearrange("a (p b) -> p (a b)", p=P)).then_inc(c_in, 16)
            sp.dma_start(xin[:, 0, :], xt[rows(0), :]).then_inc(x_in[0], 16)
            sp.dma_start(raw_k[:], Wk.rearrange("(r p) f -> p r f", p=P)).then_inc(wk_in, 16)
            wm = wmod.rearrange("(p b) n -> p b n", p=P)
            for b in range(KB):
                sp.dma_start(wm_a[:, b, :], wm[:, b, 0:2 * D]).then_inc(wma_in[b], 16)
            sp.dma_start(raw_q[:], Wq.rearrange("(r p) f -> p r f", p=P)).then_inc(wq_in, 16)
            sp.dma_start(xin[:, 1, :], xt[rows(1), :]).then_inc(x_in[1], 16)
            for row, src in ((bk_row, bk), (bq_row, bq)):
                sp.dma_start(row[:], src.rearrange("(a n) -> a n", a=1).to_broadcast([P, D])).then_inc(bias_in, 16)
            sp.dma_start(wm_b[:], wm[:, 0, 2 * D:6 * D]).then_inc(wmb_in[0], 16)
            def step(i, s):
                if live(i + 4, T):
                    wait_count(sp, xn_done, i + 3)
                    sp.dma_start(xin[:, s, :], xt[rows(i + 4), :]).then_inc(x_in[s], 16)
                if live(i - 1, T):
                    sp.wait_ge(qf_done, i)
                    sp.dma_start(q_dram[rows(i - 1), :], qf[:, 1 - s, :]).then_inc(q_out[1 - s], 16)
                if isinstance(i, int) and 0 < i < KB:
                    sp.wait_ge(mod2_kb_done, i)
                    sp.dma_start(wm_b[:], wm[:, i, 2 * D:6 * D]).then_inc(wmb_in[i], 16)
                if isinstance(i, int) and i == 3:
                    late_loads()

            def late_loads():
                sp.dma_start(raw_v[:], Wv.rearrange("(r p) f -> p r f", p=P)).then_inc(late_in, 16)
                sp.dma_start(raw_o[:], Wo.rearrange("(r p) f -> p r f", p=P)).then_inc(late_in, 16)
                sp.dma_start(raw_fv[:], fWv.rearrange("(r p) f -> p r f", p=P)).then_inc(late_in, 16)
                sp.dma_start(raw_cat[:, 0:2, :], W1.rearrange("(r e) i d -> (e i) r d", r=2)).then_inc(late_in, 16)
                sp.dma_start(raw_cat[0:PV, 2, :], Wp.rearrange("e q d -> (e q) d")).then_inc(late_in, 16)
                sp.dma_start(raw_cat[PV:PV + E, 2, :], Wg).then_inc(late_in, 16)
                for b in range(KB):
                    sp.dma_start(raw_w2[:, b, :, :], W2[:, b * P:(b + 1) * P, :].rearrange("e p i -> p e i")).then_inc(late_in, 16)
                for row, src in ((bv_row, bv), (bo_ga, bo), (fbv_row, fbv)):
                    sp.dma_start(row[:], src.rearrange("(a n) -> a n", a=1).to_broadcast([P, D])).then_inc(late_in, 16)
                sp.dma_start(bcat[:, 0:HID], b1.rearrange("(a e) i -> a (e i)", a=1).to_broadcast([P, HID])).then_inc(late_in, 16)
                sp.dma_start(bcat[:, HID + PV:C], bg.rearrange("(a n) -> a n", a=1).to_broadcast([P, E])).then_inc(late_in, 16)
                for n, src in enumerate((b_r, g_r, g_c, b_c)):
                    sp.dma_start(rt[:, n, :], src.rearrange("(a n) -> a n", a=1).to_broadcast([P, E])).then_inc(late_in, 16)
                sp.dma_start(al[:, 0:1], alpha.to_broadcast([P, 1])).then_inc(late_in, 16)
                sp.wait_ge(b2_zeroed, 1)
                for r in range(3):
                    sp.dma_start(b2raw[32 * r:32 * r + E, :], b2).then_inc(late_in, 16)

            sweep(sp, step, -2, T, *LOOP_A)
            sp.wait_ge(q_out[0], landed(T - 2, 0))
            sp.wait_ge(q_out[1], landed(T - 1, 1))
            sp.wait_ge(xn_done, T)
            sp.wait_ge(m_done, T)
            sp.wait_ge(ks_done, T)

            def pair_rows(j):
                return bass.ds(j * 2 * P, 2 * P)

            def step_b(j):
                if live(j + 2, J):
                    wait_count(sp, qz_done, j + 2)
                    sp.dma_start(q_in[:], q_dram[pair_rows(j + 2), :].rearrange("(h p) d -> p h d", p=P)).then_inc(q_back, 16)
                for h in range(2):
                    if live(j - 2, J):
                        sp.wait_ge(fin_done, 2 * (j - 2) + h + 1)
                        sp.dma_start(ot[rows((j - 2) * 2 + h), :], out_t[:, h, :]).then_inc(stored[h], 16)
                if live(j + 2, J):
                    wait_count(sp, xb_done, j + 2)
                    sp.dma_start(xin[:], xt[pair_rows(j + 2), :].rearrange("(h p) d -> p h d", p=P)).then_inc(bx_in, 16)

            sweep_pairs(sp, step_b, -2, J + 1, *LOOP_B)
            sp.wait_ge(stored[0], landed(T - 2, 0))
            sp.wait_ge(stored[1], landed(T - 1, 1))

        @block.gpsimd
        def _(pool):
            steps = [0]

            def link(ins):
                steps[0] += 1
                ins.then_inc(pool_step, 1)
                pool.wait_ge(pool_step, steps[0])

            link(nc.gpsimd.memset(ident[:], 0.0))
            nc.gpsimd.affine_select(out=ident[:], in_=ident[:], compare_op=ALU.not_equal, fill=1.0,
                                    base=0, pattern=[[-1, P]], channel_multiplier=1).then_inc(pool_const, 1)
            link(nc.gpsimd.memset(headmask[:], 1.0))
            hm = headmask[:].rearrange("p (g d) -> p g d", d=DH)
            link(nc.gpsimd.affine_select(out=hm, in_=hm, compare_op=ALU.is_ge, fill=0.0, base=0,
                                         pattern=[[-DH, P // DH], [0, DH]], channel_multiplier=1))
            nc.gpsimd.affine_select(out=hm, in_=hm, compare_op=ALU.is_ge, fill=0.0, base=DH - 1,
                                    pattern=[[DH, P // DH], [0, DH]], channel_multiplier=-1).then_inc(pool_const, 1)
            link(nc.gpsimd.memset(ks_acc[:], 0.0))
            pool.wait_ge(dve_const, 1)

            def step(i, s):
                if live(i + 2, T):
                    wait_count(pool, veps_done, i + 3)
                    nc.gpsimd.tensor_tensor(rstd[:, s:s + 1], veps[:, s:s + 1], neg_half[:, 0:1],
                                            ALU.pow).then_inc(rstd_done, 1)
                if live(i, T):
                    pool.wait_ge(kf_done, i + 1)
                    wait_count(pool, ks_done, i)
                    nc.gpsimd.tensor_tensor(ks_acc[:], ks_acc[:], kf[:, s, :], ALU.add).then_inc(ks_done, 1)
                if live(i + 1, T):
                    pool.wait_ge(xnh_done, i + 2)
                    pool.wait_ge(xn_done, i + 2)
                    nc.gpsimd.tensor_tensor(xn_lo[:, 1 - s, :], xn[:, 1 - s, :], f32(xn_hi[:, 1 - s, :]),
                                            ALU.subtract).then_inc(xnl_done, 1)

            sweep(pool, step, -2, T - 1, *LOOP_A)

            pool.wait_ge(prep_taken, len(JOBS))
            pool.wait_ge(weights_ready, 1)

            def step_b(j):
                if live(j + 1, J):
                    pool.wait_ge(zr_done, j + 2)
                    wait_count(pool, qT_psum, 2 * j + 2)
                    nc.gpsimd.tensor_tensor(
                        qz[:].rearrange("p h (n d) -> p (h n) d", d=DH),
                        q_in[:].rearrange("p h (n d) -> p (h n) d", d=DH),
                        zr[:].rearrange("p h n -> p (h n)").unsqueeze(2).to_broadcast([P, 2 * HEADS, DH]),
                        ALU.mult).then_inc(qz_done, 1)
                if live(j + 2, J):
                    pool.wait_ge(q_back, 16 * (j + 3))
                    wait_count(pool, den_done, j + 2)
                    nc.gpsimd.tensor_tensor(qks[:], q_in[:], ks_row[:].unsqueeze(1).to_broadcast([P, 2, D]),
                                            ALU.mult).then_inc(qks_done, 1)
                if live(j - 1, J):
                    pool.wait_ge(c2_done, 2 * j - 1)
                    wait_count(pool, cc_done, j - 1)
                    nc.gpsimd.tensor_tensor(cn[:, 0, :], c2[:, 0, :], half[:], ALU.pow).then_inc(cn_done, 1)
                if live(j, J):
                    pool.wait_ge(bveps_done, j + 1)
                    wait_count(pool, x2_done, 2 * j)
                    nc.gpsimd.tensor_tensor(rstd[:], veps[:], neg_half[:, 0:2], ALU.pow).then_inc(brstd_done, 1)
                if live(j - 1, J):
                    pool.wait_ge(c2_done, 2 * j)
                    nc.gpsimd.tensor_tensor(cn[:, 1, :], c2[:, 1, :], half[:], ALU.pow).then_inc(cn_done, 1)
                    pool.wait_ge(rve_done, j)
                    wait_count(pool, s1_done, j - 1)
                    nc.gpsimd.tensor_tensor(rrs[:].rearrange("p h k -> p (h k)"), rve[:], neg_half[:, 0:4],
                                            ALU.pow).then_inc(rrs_done, 1)
                if live(j + 1, J):
                    pool.wait_ge(bx_in, 16 * (j + 2))
                    wait_count(pool, x1_done, 2 * j + 2)
                    nc.gpsimd.tensor_tensor(xb[:], xin[:], bo_ga[:].unsqueeze(1).to_broadcast([P, 2, D]),
                                            ALU.add).then_inc(xb_done, 1)

            sweep_pairs(pool, step_b, -2, J, *LOOP_B)

        @block.scalar
        def _(act):
            act.wait_ge(c_in, 16)
            nc.scalar.activation(c_col[:, 1, :], c_col[:, 0, :], ACT.Exp, scale=-1.0).then_inc(c_exp, 1)

            def hi_scaled(j, dst, col):
                act.wait_ge(prep_psum, JOB[j] + 1)
                nc.scalar.activation(dst, bank(j)[:, 0:dst.shape[1]], ACT.Copy, scale=col).then_inc(prep_hi, 1)

            act.wait_ge(prep_taken, TAKE["ca"] + 1)
            for b in range(KB):
                hi_scaled(f"k{b}", wk_hi[:, b, :], ca1_col[:, b:b + 1])
            for b in range(KB):
                hi_scaled(f"q{b}", wq_hi[:, b, :], ca1_col[:, b:b + 1])

            def step(i, s):
                if live(i + 1, T):
                    act.wait_ge(xT_psum, i + 2)
                    wait_count(act, xTl_done, i)
                    wait_count(act, q_psum, i)
                    nc.scalar.copy(xT_hi[:, 1 - s, :], bank_xT(1 - s)).then_inc(xTh_done, 1)
                if live(i - 1, T):
                    act.wait_ge(zq_done, i)
                    wait_count(act, qf_done, i - 2)
                    nc.scalar.activation(neg_q[:, 1 - s, :], zq[:, 1 - s, :], ACT.Relu, scale=-1.0).then_inc(rq_done, 1)
                    act.wait_ge(rq_done, i)
                    nc.scalar.activation(exp_q[:, 1 - s, :], neg_q[:, 1 - s, :], ACT.Exp, scale=-1.0).then_inc(eq_done, 1)
                if live(i, T):
                    act.wait_ge(zk_done, i + 1)
                    wait_count(act, kf_done, i - 1)
                    nc.scalar.activation(neg_k[:, s, :], zk[:, s, :], ACT.Relu, scale=-1.0).then_inc(rk_done, 1)
                    act.wait_ge(rk_done, i + 1)
                    nc.scalar.activation(exp_k[:, s, :], neg_k[:, s, :], ACT.Exp, scale=-1.0).then_inc(ek_done, 1)
                    act.wait_ge(kf_done, i + 1)
                    wait_count(act, m_done, i - 1)
                    wait_count(act, kl_done, i - 1)
                    nc.scalar.copy(k_hi[:, s, :], kf[:, s, :]).then_inc(kh_done, 1)
                if live(i + 1, T):
                    act.wait_ge(xn_done, i + 2)
                    wait_count(act, m_done, i)
                    wait_count(act, xnl_done, i)
                    nc.scalar.copy(xn_hi[:, 1 - s, :], xn[:, 1 - s, :]).then_inc(xnh_done, 1)

            sweep(act, step, -1, T, *LOOP_A)

            act.wait_ge(late_in, 16 * LATE_LOADS)
            nc.scalar.activation(al[:, 1:2], al[:, 0:1], ACT.Exp, scale=-1.0).then_inc(al_exp, 1)

            def hi_tmp(j, dst):
                act.wait_ge(prep_tmp, TMP[j] + 1)
                nc.scalar.copy(dst, wtmp[:, TMP[j] % 2, :]).then_inc(prep_hi, 1)

            for b in range(KB):
                hi_tmp(f"g{b}", g_hi[:, b, :])
            for b in range(KB):
                hi_tmp(f"fv{b}", v_hi[:, b, :])
            for b in range(KB):
                hi_scaled(f"u{b}", c_hi[:, b, :], cb1_col[:, b:b + 1])
            for b in range(2):
                hi_tmp(f"w2{b}", w2_hi[:, b, :])

            def x2T_high(j, h):
                t = 2 * j + h
                act.wait_ge(x2T_psum, t + 1)
                wait_count(act, y_v_done, t - 1)
                nc.scalar.copy(xT_hi[:, h, :], bank_x2T).then_inc(x2Th_done, 1)

            def qT_high(j, h):
                t = 2 * j + h
                act.wait_ge(qT_psum, t + 1)
                wait_count(act, o_psum, t - 1)
                wait_count(act, qTl_done, t - 1)
                nc.scalar.copy(qT_hi[:, h, :], bank_qaT).then_inc(qTh_done, 1)

            def aT_high(j, h):
                t = 2 * j + h
                act.wait_ge(aT_psum, t + 1)
                wait_count(act, y_psum, t - 1)
                nc.scalar.copy(aT_hi[:, h, :], bank_qaT[:, 0:3 * P]).then_inc(aTh_done, 1)

            def functions(j, h):
                t = 2 * j + h
                act.wait_ge(zf_done, t + 1)
                wait_count(act, c2_done, t - 1)
                nc.scalar.activation(sq[:, h, :], zf[:, h, HID:HID + PV], ACT.Square,
                                     scale=PD ** -0.5).then_inc(sq_done, 1)
                wait_count(act, hz_done, j)
                nc.scalar.activation(th[:, h, :], zf[:, h, 0:HID], ACT.Tanh, scale=0.5).then_inc(th_done, 1)

            def step_b(j):
                if live(j - 1, J):
                    x2T_high(j - 1, 1)
                if live(j - 2, J):
                    aT_high(j - 2, 0)
                if live(j - 1, J):
                    functions(j - 1, 0)
                if live(j - 2, J):
                    aT_high(j - 2, 1)
                if live(j - 1, J):
                    functions(j - 1, 1)
                if live(j + 1, J):
                    qT_high(j + 1, 0)
                if live(j, J):
                    x2T_high(j, 0)
                if live(j + 1, J):
                    qT_high(j + 1, 1)
                if live(j - 1, J):
                    act.wait_ge(sm_done, j)
                    wait_count(act, wn_done, j - 1)
                    nc.scalar.activation(ex[:], sm[:], ACT.Exp).then_inc(ex_done, 1)

            sweep_pairs(act, step_b, -1, J + 1, *LOOP_B)

        @block.vector
        def _(dve):
            steps = [0]

            def link(ins):
                steps[0] += 1
                ins.then_inc(dve_step, 1)
                dve.wait_ge(dve_step, steps[0])

            def wait_apart(sem, n):
                n = n if isinstance(n, int) else dve.snap(n)
                dve.wait_ge(dve_const, 1)
                dve.wait_ge(sem, n)

            nc.vector.memset(neg_half[:], -0.5)
            nc.vector.memset(half[:], 0.5)
            nc.vector.memset(b2raw[:], 0.0).then_inc(b2_zeroed, 1)
            nc.vector.memset(ones[:], 1.0).then_inc(dve_const, 1)

            def statistics(i, s):
                dve.wait_ge(x_in[s], landed(i, s))
                nc.vector.bn_stats(stats[:, s, :], xin[:, s, :]).then_inc(stats_done, 1)
                dve.wait_ge(stats_done, i + 1)

            def mean_var(i, s):
                nc.vector.bn_aggr(mv[:, s, :], stats[:, s, :]).then_inc(mv_done, 1)

            def var_eps(i, s):
                dve.wait_ge(mv_done, i + 1)
                nc.vector.tensor_scalar(veps[:, s:s + 1], mv[:, s, 1:2], EPS, None, ALU.add).then_inc(veps_done, 1)

            def normed(i, s):
                dve.wait_ge(rstd_done, i + 1)
                wait_count(dve, xT_psum, i - 1)
                wait_count(dve, xnh_done, i - 1)
                wait_count(dve, xnl_done, i - 1)
                nc.vector.tensor_scalar(xn[:, s, :], xin[:, s, :], mv[:, s, 0:1], rstd[:, s:s + 1],
                                        ALU.subtract, ALU.mult).then_inc(xn_done, 1)

            statistics(0, 0)
            mean_var(0, 0)
            var_eps(0, 0)
            dve.wait_ge(c_exp, 1)
            link(nc.vector.tensor_scalar(c_col[:, 2, :], c_col[:, 1, :], 1.0, None, ALU.add))
            link(nc.vector.reciprocal(c_col[:, 1, :], c_col[:, 2, :]))
            link(nc.vector.tensor_tensor(c_col[:, 2, :], c_col[:, 0, :], c_col[:, 1, :], ALU.mult))
            normed(0, 0)
            for b in range(KB):
                dve.wait_ge(wma_in[b], 16)
                if b == 0:
                    ins = nc.vector.tensor_scalar(mod1[:], wm_a[:, b, :], c_col[:, 2, b:b + 1], None, ALU.mult)
                else:
                    dve.wait_ge(mod1_done, b)
                    ins = nc.vector.scalar_tensor_tensor(out=mod1[:], in0=wm_a[:, b, :], scalar=c_col[:, 2, b:b + 1],
                                                         in1=mod1[:], op0=ALU.mult, op1=ALU.add)
                ins.then_inc(mod1_done, 1)

            def columns(dst, row, b0=0):
                for b in range(KB):
                    last = nc.vector.tensor_tensor_reduce(out=diag_out[:], in0=ident[:], in1=row[:, b * P:(b + 1) * P],
                                                          scale=1.0, scalar=b0, op0=ALU.mult, op1=ALU.add,
                                                          accum_out=dst[:, b:b + 1])
                    if b < KB - 1:
                        link(last)
                return last

            def full(j):
                dve.wait_ge(prep_psum, JOB[j] + 1)

            taken = [0]

            def taken_by(ins, j):
                assert TAKE[j] == taken[0], j
                taken[0] += 1
                ins.then_inc(prep_taken, 1)
                dve.wait_ge(prep_taken, taken[0])

            dve.wait_ge(pool_const, 1)
            full("ca")
            taken_by(columns(sa_col, bank("sa")), "sa")
            taken_by(columns(ca1_col, bank("ca"), 1.0), "ca")

            def fold(j, acc, col_bias, col_scale, hi, lo, first):
                full(j)
                dve.wait_ge(prep_hi, HI[j] + 1)
                n = acc.shape[1]
                if first:
                    link(nc.vector.tensor_scalar(acc, bank(j)[:, 0:n], col_bias, None, ALU.mult))
                else:
                    link(nc.vector.scalar_tensor_tensor(out=acc, in0=bank(j)[:, 0:n], scalar=col_bias, in1=acc,
                                                        op0=ALU.mult, op1=ALU.add))
                return nc.vector.scalar_tensor_tensor(out=lo, in0=bank(j)[:, 0:n], scalar=col_scale, in1=f32(hi),
                                                      op0=ALU.mult, op1=ALU.subtract)

            for b in range(KB):
                taken_by(fold(f"k{b}", acc_k[:], sa_col[:, b:b + 1], ca1_col[:, b:b + 1], wk_hi[:, b, :],
                              wk_lo[:, b, :], b == 0), f"k{b}")
            for b in range(KB):
                taken_by(fold(f"q{b}", acc_q[:], sa_col[:, b:b + 1], ca1_col[:, b:b + 1], wq_hi[:, b, :],
                              wq_lo[:, b, :], b == 0), f"q{b}")
            statistics(1, 1)
            mean_var(1, 1)
            var_eps(1, 1)
            normed(1, 1)
            dve.wait_ge(bias_in, 32)
            for j, row in (("bk", bk_row), ("bq", bq_row)):
                full(j)
                taken_by(nc.vector.tensor_tensor(row[:], bank(j), row[:], ALU.add), j)

            def step(i, s):
                if live(i - 1, T):
                    dve.wait_ge(q_psum, i)
                    wait_count(dve, eq_done, i - 2)
                    nc.vector.tensor_tensor(zq[:, 1 - s, :], bank_q, bq_row[:], ALU.add).then_inc(zq_done, 1)
                if live(i + 1, T):
                    dve.wait_ge(xTh_done, i + 2)
                    wait_count(dve, q_psum, i)
                    nc.vector.tensor_tensor(xT_lo[:, 1 - s, :], bank_xT(1 - s), f32(xT_hi[:, 1 - s, :]),
                                            ALU.subtract).then_inc(xTl_done, 1)
                ahead = live(i + 2, T) and not (isinstance(i, int) and i + 2 < 2)
                if ahead:
                    statistics(i + 2, s)
                if live(i - 1, T):
                    dve.wait_ge(eq_done, i)
                    wait_count(dve, q_out[1 - s], landed(i - 1, 1 - s) - 16)
                    nc.vector.scalar_tensor_tensor(out=qf[:, 1 - s, :], in0=zq[:, 1 - s, :], scalar=0.0,
                                                   in1=exp_q[:, 1 - s, :], op0=ALU.max, op1=ALU.add).then_inc(qf_done, 1)
                if ahead:
                    mean_var(i + 2, s)
                if live(i, T):
                    dve.wait_ge(k_psum, i + 1)
                    wait_count(dve, ek_done, i - 1)
                    nc.vector.tensor_tensor(zk[:, s, :], bank_k, bk_row[:], ALU.add).then_inc(zk_done, 1)
                if ahead:
                    var_eps(i + 2, s)
                    normed(i + 2, s)
                if live(i, T):
                    dve.wait_ge(ek_done, i + 1)
                    wait_count(dve, kh_done, i - 1)
                    wait_count(dve, ks_done, i - 1)
                    nc.vector.scalar_tensor_tensor(out=kf[:, s, :], in0=zk[:, s, :], scalar=0.0,
                                                   in1=exp_k[:, s, :], op0=ALU.max, op1=ALU.add).then_inc(kf_done, 1)
                    dve.wait_ge(kf_done, i + 1)
                    dve.wait_ge(kh_done, i + 1)
                    wait_count(dve, m_done, i - 1)
                    nc.vector.tensor_tensor(k_lo[:, s, :], kf[:, s, :], f32(k_hi[:, s, :]), ALU.subtract).then_inc(kl_done, 1)
                if isinstance(i, int) and 0 <= i < KB:
                    dve.wait_ge(wmb_in[i], 16)
                    m2 = mod2[:].rearrange("p v n -> p (v n)")
                    if i == 0:
                        ins = nc.vector.tensor_scalar(m2, wm_b[:], c_col[:, 2, 0:1], None, ALU.mult)
                    else:
                        dve.wait_ge(mod2_kb_done, i)
                        ins = nc.vector.scalar_tensor_tensor(out=m2, in0=wm_b[:], scalar=c_col[:, 2, i:i + 1],
                                                             in1=m2, op0=ALU.mult, op1=ALU.add)
                    ins.then_inc(mod2_kb_done, 1)

            sweep(dve, step, -1, T, *LOOP_A)

            dve.wait_ge(late_in, 16 * LATE_LOADS)
            dve.wait_ge(m_done, T)
            dve.wait_ge(ks_done, T)
            dve.wait_ge(q_out[0], landed(T - 2, 0))
            dve.wait_ge(q_out[1], landed(T - 1, 1))
            dve.wait_ge(pool_const, 2)
            nc.vector.memset(f32(b2st[:]), 0.0)
            nc.vector.memset(aw[:], 0.0)
            nc.vector.memset(sx[:], SENTINEL)
            link(nc.vector.memset(top[:], SENTINEL))
            full("ks")
            taken_by(nc.vector.tensor_copy(ks_row[:], bank("ks")), "ks")

            def gate(j, v):
                full(j)
                link(nc.vector.tensor_scalar(wtmp[:, 0, :], bank(j), 0.0, 2.0, ALU.is_ge, ALU.mult))
                link(nc.vector.tensor_scalar(wtmp[:, 0, :], wtmp[:, 0, :], 1.0, None, ALU.subtract))
                taken_by(nc.vector.tensor_tensor(wtmp[:, 1, :], bank(j), wtmp[:, 0, :], ALU.mult), j)
                link(nc.vector.scalar_tensor_tensor(out=mod2[:, v, :], in0=wtmp[:, 1, :], scalar=0.25,
                                                    in1=wtmp[:, 0, :], op0=ALU.max, op1=ALU.mult))

            GA, SB, CB, GB = range(4)
            gate("ga", GA)
            for j, col, b0 in (("sb", sb_col, 0.0), ("cb", cb1_col, 1.0)):
                full(j)
                taken_by(columns(col, bank(j), b0), j)
            gate("gb", GB)
            ga, gb = mod2[:, GA, :], mod2[:, GB, :]
            link(nc.vector.tensor_tensor(bo_ga[:], bo_ga[:], ga, ALU.mult))
            for b in range(KB):
                link(nc.vector.tensor_scalar(mt[b], ps[:, b, :], ca1_col[:, b:b + 1], None, ALU.mult))
            for b in range(KB):
                full(f"v{b}")
                link(nc.vector.tensor_copy(wvT[:, b, :], bank(f"v{b}")))
                if b == 0:
                    ins = nc.vector.tensor_scalar(acc_v[:], bank("v0"), sa_col[:, 0:1], None, ALU.mult)
                else:
                    ins = nc.vector.scalar_tensor_tensor(out=acc_v[:], in0=bank(f"v{b}"), scalar=sa_col[:, b:b + 1],
                                                         in1=acc_v[:], op0=ALU.mult, op1=ALU.add)
                taken_by(ins, f"v{b}")
            for b in range(KB):
                full(f"o{b}")
                taken_by(nc.vector.tensor_copy(woT[:, b, :], bank(f"o{b}")), f"o{b}")
            full("bv")
            taken_by(nc.vector.tensor_tensor(bv_row[:], bank("bv"), bv_row[:], ALU.add), "bv")
            link(columns(bvp_col, bv_row[:]))
            full("kv")
            for b in range(KB):
                blk = slice(b * P, (b + 1) * P)
                link(nc.vector.scalar_tensor_tensor(out=kv_tmp[:], in0=ks_row[:, blk], scalar=bvp_col[:, b:b + 1],
                                                    in1=bank("kv")[:, blk], op0=ALU.mult, op1=ALU.add))
                ins = nc.vector.tensor_tensor(kvm[:, b, :], kv_tmp[:], headmask[:], ALU.mult)
                if b < KB - 1:
                    link(ins)
            taken_by(ins, "kv")

            def split_tmp(j, make, lo, hi, extra=None):
                full(j)
                t = TMP[j]
                make(wtmp[:, t % 2, :]).then_inc(prep_tmp, 1)
                dve.wait_ge(prep_tmp, t + 1)
                dve.wait_ge(prep_hi, HI[j] + 1)
                if extra is not None:
                    link(nc.vector.tensor_tensor(lo, wtmp[:, t % 2, :], f32(hi), ALU.subtract))
                    taken_by(extra(), j)
                else:
                    taken_by(nc.vector.tensor_tensor(lo, wtmp[:, t % 2, :], f32(hi), ALU.subtract), j)

            for b in range(KB):
                j = f"g{b}"
                split_tmp(j, lambda o, j=j: nc.vector.tensor_tensor(o, bank(j), ga, ALU.mult), g_lo[:, b, :], g_hi[:, b, :])
            for b in range(KB):
                j = f"fv{b}"

                def bias_sum(j=j, b=b):
                    if b == 0:
                        return nc.vector.tensor_scalar(acc_fv[:], bank(j), sb_col[:, 0:1], None, ALU.mult)
                    return nc.vector.scalar_tensor_tensor(out=acc_fv[:], in0=bank(j), scalar=sb_col[:, b:b + 1],
                                                          in1=acc_fv[:], op0=ALU.mult, op1=ALU.add)

                split_tmp(j, lambda o, j=j, b=b: nc.vector.scalar_tensor_tensor(
                    out=o, in0=bank(j), scalar=cb1_col[:, b:b + 1], in1=gb, op0=ALU.mult, op1=ALU.mult),
                    v_lo[:, b, :], v_hi[:, b, :], bias_sum)
            link(columns(fbv_col, fbv_row[:]))
            for b in range(KB):
                j = f"cat{b}"
                full(j)
                lg = slice(HID + PV, C)
                link(nc.vector.tensor_copy(catT[:, b, :], bank(j)[:, 0:C]))
                link(nc.vector.tensor_reduce(small[:, 0:1], catT[:, b, lg], AX.X, ALU.add))
                link(nc.vector.tensor_scalar(small[:, 1:2], small[:, 0:1], 1.0 / E, None, ALU.mult))
                link(nc.vector.tensor_scalar(catT[:, b, lg], catT[:, b, lg], small[:, 1:2], None, ALU.subtract))
                if b == 0:
                    ins = nc.vector.tensor_scalar(acc_c[:], catT[:, 0, :], fbv_col[:, 0:1], None, ALU.mult)
                else:
                    ins = nc.vector.scalar_tensor_tensor(out=acc_c[:], in0=catT[:, b, :], scalar=fbv_col[:, b:b + 1],
                                                         in1=acc_c[:], op0=ALU.mult, op1=ALU.add)
                taken_by(ins, j)
            for b in range(KB):
                j = f"u{b}"
                taken_by(fold(j, acc_c[:], sb_col[:, b:b + 1], cb1_col[:, b:b + 1], c_hi[:, b, :], c_lo[:, b, :], False), j)
            lg = slice(HID + PV, C)
            link(nc.vector.memset(bcat[:, HID:HID + PV], 0.0))
            link(nc.vector.tensor_reduce(small[:, 0:1], bcat[:, lg], AX.X, ALU.add))
            link(nc.vector.tensor_scalar(small[:, 1:2], small[:, 0:1], 1.0 / E, None, ALU.mult))
            link(nc.vector.tensor_scalar(bcat[:, lg], bcat[:, lg], small[:, 1:2], None, ALU.subtract))
            full("bc")
            taken_by(nc.vector.tensor_tensor(bf_row[:], bank("bc")[:, 0:C], bcat[:], ALU.add), "bc")
            full("bfv")
            link(nc.vector.tensor_tensor(b2raw[:], b2raw[:], fbv_row[:], ALU.add))
            taken_by(nc.vector.tensor_tensor(b2raw[:], bank("bfv"), b2raw[:], ALU.add), "bfv")
            link(nc.vector.tensor_tensor(b2raw[:], b2raw[:], gb, ALU.mult))
            for r in (0, 64):
                nc.vector.tensor_copy(b2st[r:r + E, :], b2raw[r:r + E, :])
            link(nc.vector.tensor_copy(b2st[32:32 + E, :], b2raw[32:32 + E, :]))
            link(nc.vector.tensor_tensor(b2raw[32:32 + E, :], b2raw[32:32 + E, :], f32(b2st[32:32 + E, :]), ALU.subtract))
            link(nc.vector.tensor_copy(b2st[32:32 + E, :], b2raw[32:32 + E, :]))
            for b in range(2):
                j = f"w2{b}"
                split_tmp(j, lambda o, j=j: nc.vector.scalar_tensor_tensor(
                    out=o, in0=bank(j), scalar=0.5, in1=gb, op0=ALU.mult, op1=ALU.mult), w2_lo[:, b, :], w2_hi[:, b, :])
            dve.wait_ge(al_exp, 1)
            link(nc.vector.tensor_scalar(al[:, 2:3], al[:, 1:2], 1.0, None, ALU.add))
            link(nc.vector.reciprocal(al[:, 3:4], al[:, 2:3]))
            link(nc.vector.tensor_scalar(rt[:, 2, :], rt[:, 2, :], al[:, 3:4], None, ALU.mult))
            link(nc.vector.scalar_tensor_tensor(out=rt[:, 4, :], in0=rt[:, 3, :], scalar=al[:, 3:4], in1=rt[:, 0, :],
                                                op0=ALU.mult, op1=ALU.add))
            nc.vector.tensor_copy(small[:, 0:1], bf_row[:, 0:1]).then_inc(weights_ready, 1)
            g_rows, bias_row = rt[:, 1:3, :].rearrange("p k e -> p (k e)"), rt[:, 4, :]

            def over(ap, shape):
                return ap.unsqueeze(2).to_broadcast(shape)

            def denominators(j):
                dve.wait_ge(qks_done, j + 1)
                nc.vector.tensor_reduce(den[:].rearrange("p h n -> p (h n)"), qks[:].rearrange("p h (n d) -> p (h n) d", d=DH),
                                        AX.X, ALU.add).then_inc(den_done, 1)
                dve.wait_ge(den_done, j + 1)
                nc.vector.tensor_scalar(den_eps[:], den[:], 1e-6, None, ALU.add).then_inc(deneps_done, 1)
                dve.wait_ge(deneps_done, j + 1)
                wait_count(dve, qz_done, j)
                nc.vector.reciprocal(zr[:], den_eps[:]).then_inc(zr_done, 1)

            def residual(j, h):
                t = 2 * j + h
                dve.wait_ge(o_psum, t + 1)
                dve.wait_ge(xb_done, j + 1)
                nc.vector.tensor_tensor(x1_of(j, h), bank_o, xb[:, h, :], ALU.add).then_inc(x1_done, 1)
                wait_apart(x1_done, t + 1)
                nc.vector.bn_stats(stats[:, h, :], x1_of(j, h)).then_inc(bstats_done, 1)

            def moments(j):
                for h in range(2):
                    wait_apart(bstats_done, 2 * j + h + 1)
                    nc.vector.bn_aggr(mv[:, h, :], stats[:, h, :]).then_inc(bmv_done, 1)
                dve.wait_ge(bmv_done, 2 * j + 2)
                nc.vector.tensor_scalar(veps[:], mv[:, :, 1], EPS, None, ALU.add).then_inc(bveps_done, 1)

            def normalised(j, h):
                t = 2 * j + h
                dve.wait_ge(brstd_done, j + 1)
                wait_count(dve, x2T_psum, t - 1)
                nc.vector.tensor_scalar(xn[:, h, :], x1_of(j, h), mv[:, h, 0:1], rstd[:, h:h + 1],
                                        ALU.subtract, ALU.mult).then_inc(x2_done, 1)

            def x2T_low(j, h):
                t = 2 * j + h
                dve.wait_ge(x2Th_done, t + 1)
                nc.vector.tensor_tensor(xT_lo[:, h, :], bank_x2T, f32(xT_hi[:, h, :]), ALU.subtract).then_inc(x2Tl_done, 1)

            def qT_low(j, h):
                t = 2 * j + h
                dve.wait_ge(qTh_done, t + 1)
                nc.vector.tensor_tensor(qT_lo[:, h, :], bank_qaT, f32(qT_hi[:, h, :]), ALU.subtract).then_inc(qTl_done, 1)

            def aT_low(j, h):
                t = 2 * j + h
                dve.wait_ge(aTh_done, t + 1)
                nc.vector.tensor_tensor(aT_lo[:, h, :], bank_qaT[:, 0:2 * P], f32(aT_hi[:, h, 0:2 * P]),
                                        ALU.subtract).then_inc(aTl_done, 1)

            def biased(j, h):
                t = 2 * j + h
                dve.wait_ge(f_psum, t + 1)
                nc.vector.tensor_tensor(zf[:, h, 0:C], bank_f[:, 0:C], bf_row[:], ALU.add).then_inc(zf_done, 1)

            def probes(j, h):
                t = 2 * j + h
                dve.wait_ge(sq_done, t + 1)
                nc.vector.tensor_reduce(c2[:, h, :], sq[:, h, :].rearrange("p (e q) -> p e q", q=PD),
                                        AX.X, ALU.add).then_inc(c2_done, 1)

            def finished(j, h):
                t = 2 * j + h
                dve.wait_ge(y_psum, t + 1)
                wait_count(dve, stored[h], 16 * j)
                nc.vector.tensor_tensor(out_t[:, h, :], bank_y(h),
                                        x1_of(j, h), ALU.add).then_inc(fin_done, 1)

            def gated(j):
                dve.wait_ge(th_done, 2 * j + 2)
                nc.vector.scalar_tensor_tensor(out=hz[:], in0=th[:], scalar=1.0, in1=zf[:, :, 0:HID],
                                               op0=ALU.add, op1=ALU.mult).then_inc(hz_done, 1)

            def variances(j):
                dve.wait_ge(cn_done, 2 * j + 2)
                nc.vector.tensor_reduce(csum[:], cn[:], AX.X, ALU.add).then_inc(csum_done, 1)
                dve.wait_ge(csum_done, j + 1)
                nc.vector.scalar_tensor_tensor(out=zf[:, :, C:C + E], in0=over(csum[:], [P, 2, E]), scalar=-1.0 / E,
                                               in1=cn[:], op0=ALU.mult, op1=ALU.add).then_inc(cc_done, 1)
                dve.wait_ge(cc_done, j + 1)
                rc = zf[:, :, HID + PV:C + E]
                nc.vector.tensor_tensor(rsq[:].rearrange("p h k e -> p h (k e)"), rc, rc, ALU.mult).then_inc(rsq_done, 1)
                dve.wait_ge(rsq_done, j + 1)
                nc.vector.tensor_reduce(rvar[:], rsq[:].rearrange("p h k e -> p (h k) e"), AX.X, ALU.add).then_inc(rvar_done, 1)
                dve.wait_ge(rvar_done, j + 1)
                nc.vector.tensor_scalar(rve[:], rvar[:], 1.0 / E, EPS, ALU.mult, ALU.add).then_inc(rve_done, 1)

            def scores(j):
                dve.wait_ge(rrs_done, j + 1)
                nc.vector.tensor_tensor(s1[:], zf[:, :, HID + PV:C + E].rearrange("p h (k e) -> p h k e", e=E),
                                        rrs[:].unsqueeze(3).to_broadcast([P, 2, 2, E]), ALU.mult).then_inc(s1_done, 1)
                dve.wait_ge(s1_done, j + 1)
                nc.vector.tensor_tensor(s2[:].rearrange("p h k e -> p h (k e)"), s1[:].rearrange("p h k e -> p h (k e)"),
                                        g_rows.unsqueeze(1).to_broadcast([P, 2, 2 * E]), ALU.mult).then_inc(s2_done, 1)
                dve.wait_ge(s2_done, j + 1)
                nc.vector.tensor_tensor(s3[:], s2[:, :, 0, :], s2[:, :, 1, :], ALU.add).then_inc(s3_done, 1)
                dve.wait_ge(s3_done, j + 1)
                nc.vector.tensor_tensor(sx[:, :, 0:E], s3[:], bias_row.unsqueeze(1).to_broadcast([P, 2, E]),
                                        ALU.add).then_inc(sx_done, 1)
                wait_apart(sx_done, j + 1)
                for h in range(2):
                    nc.vector.max(m8[:, h, :], sx[:, h, 0:E]).then_inc(m8_done, 1)
                dve.wait_ge(m8_done, 2 * j + 2)
                nc.vector.tensor_copy(top[:, :, 0:2], m8[:, :, 0:2]).then_inc(top_done, 1)
                nc.vector.tensor_tensor(sm[:], sx[:, :, 0:E], over(m8[:, :, 0], [P, 2, E]), ALU.subtract).then_inc(sm_done, 1)
                wait_apart(top_done, j + 1)
                for h in range(2):
                    nc.vector.match_replace(marked[:, h, 0:14], top[:, h, :], sx[:, h, 0:14], TAKEN).then_inc(marked_done, 1)
                dve.wait_ge(marked_done, 2 * j + 2)
                nc.vector.tensor_tensor(mask[:], marked[:, :, 0:E], sx[:, :, 0:E], ALU.not_equal).then_inc(mask_done, 1)

            def weights(j):
                dve.wait_ge(ex_done, j + 1)
                dve.wait_ge(mask_done, j + 1)
                nc.vector.tensor_tensor(wn[:], ex[:], mask[:], ALU.mult).then_inc(wn_done, 1)
                dve.wait_ge(wn_done, j + 1)
                nc.vector.tensor_reduce(wsum[:], wn[:], AX.X, ALU.add).then_inc(wsum_done, 1)
                dve.wait_ge(wsum_done, j + 1)
                nc.vector.reciprocal(winv[:], wsum[:]).then_inc(winv_done, 1)
                dve.wait_ge(winv_done, j + 1)
                nc.vector.tensor_tensor(wt[:], wn[:], over(winv[:], [P, 2, E]), ALU.mult).then_inc(wt_done, 1)
                dve.wait_ge(wt_done, j + 1)
                dve.wait_ge(hz_done, j + 1)
                wait_count(dve, aT_psum, 2 * j)
                nc.vector.tensor_copy(
                    aw[:, :, 2 * P:2 * P + 64].rearrange("p h (r e) -> p h r e", e=32)[:, :, :, 0:E].bitcast(F32R),
                    wt[:].unsqueeze(2).to_broadcast([P, 2, 2, E])).then_inc(wth_done, 1)
                nc.vector.tensor_tensor(
                    aw[:, :, 0:HID].rearrange("p h (e i) -> p h e i", i=INNER),
                    hz[:].rearrange("p h (e i) -> p h e i", i=INNER),
                    wt[:].unsqueeze(3).to_broadcast([P, 2, E, INNER]), ALU.mult)
                dve.wait_ge(wth_done, j + 1)
                nc.vector.tensor_tensor(aw[:, :, 2 * P + 64:2 * P + 64 + E], wt[:], aw[:, :, 2 * P:2 * P + E],
                                        ALU.subtract).then_inc(aw_done, 1)

            def step_b(j):
                if live(j - 1, J):
                    x2T_low(j - 1, 1)
                if live(j - 2, J):
                    weights(j - 2)
                if live(j, J):
                    residual(j, 0)
                if live(j - 1, J):
                    biased(j - 1, 0)
                if live(j - 2, J):
                    aT_low(j - 2, 0)
                if live(j - 1, J):
                    probes(j - 1, 0)
                if live(j, J):
                    residual(j, 1)
                    moments(j)
                if live(j - 2, J):
                    finished(j - 2, 0)
                    aT_low(j - 2, 1)
                if live(j, J):
                    normalised(j, 0)
                if live(j - 1, J):
                    biased(j - 1, 1)
                    probes(j - 1, 1)
                if live(j, J):
                    normalised(j, 1)
                if live(j - 1, J):
                    gated(j - 1)
                if live(j - 2, J):
                    finished(j - 2, 1)
                if live(j + 1, J):
                    qT_low(j + 1, 0)
                if live(j - 1, J):
                    variances(j - 1)
                if live(j + 2, J):
                    denominators(j + 2)
                if live(j, J):
                    x2T_low(j, 0)
                if live(j - 1, J):
                    scores(j - 1)
                if live(j + 1, J):
                    qT_low(j + 1, 1)

            sweep_pairs(dve, step_b, -2, J + 1, *LOOP_B)

        @block.tensor
        def _(pe):
            pe.wait_ge(dve_const, 1)
            pe.wait_ge(pool_const, 1)

            def three(dst, parts, start, stop):
                for n, (ah, al_, bh, bl) in enumerate(parts):
                    s0 = start and n == 0
                    s1_ = stop and n == len(parts) - 1
                    nc.tensor.matmul(dst, ah, bh, start=s0, stop=False)
                    nc.tensor.matmul(dst, ah, bl, start=False, stop=False)
                    last = nc.tensor.matmul(dst, al_, bh, start=False, stop=s1_)
                return last

            def transposes(j, srcs):
                bank_free(pe, j)
                col = 0
                for src in srcs:
                    k = src.shape[0]
                    last = nc.tensor.transpose(bank(j)[:, col:col + k], src, ident[0:k, 0:k])
                    col += k
                last.then_inc(prep_psum, 1)

            def blocks_of(raw, fb):
                return [raw[:, r, fb * P:(fb + 1) * P] for r in range(KB)]

            def sum_rows(j, acc):
                bank_free(pe, j)
                nc.tensor.matmul(bank(j)[:, 0:acc.shape[1]], ones[:], acc, start=True, stop=True).then_inc(prep_psum, 1)

            pe.wait_ge(wk_in, 16)
            for b in range(KB):
                transposes(f"k{b}", blocks_of(raw_k, b))
            pe.wait_ge(mod1_done, KB)
            sum_rows("sa", mod1[:, 0:D])
            sum_rows("ca", mod1[:, D:2 * D])
            pe.wait_ge(wq_in, 16)
            for b in range(KB):
                transposes(f"q{b}", blocks_of(raw_q, b))
            pe.wait_ge(prep_taken, TAKE["q3"] + 1)
            sum_rows("bk", acc_k[:])
            sum_rows("bq", acc_q[:])

            def step(i, s):
                if live(i + 1, T):
                    pe.wait_ge(xn_done, i + 2)
                    wait_count(pe, xTl_done, i)
                    for b in range(KB):
                        blk = slice(b * P, (b + 1) * P)
                        last = nc.tensor.transpose(bank_xT(1 - s)[:, blk], xn[:, 1 - s, blk], ident[:])
                    last.then_inc(xT_psum, 1)
                if live(i, T):
                    if isinstance(i, int) and i == 0:
                        pe.wait_ge(prep_taken, EARLY_JOBS)
                    pe.wait_ge(xTl_done, i + 1)
                    wait_count(pe, zk_done, i)
                    three(bank_k, [(xT_hi[:, s, b * P:(b + 1) * P], xT_lo[:, s, b * P:(b + 1) * P],
                                    wk_hi[:, b, :], wk_lo[:, b, :]) for b in range(KB)], True, True).then_inc(k_psum, 1)
                if live(i - 1, T):
                    p = 1 - s
                    first = isinstance(i, int) and i == 1
                    final = isinstance(i, int) and i == T
                    pe.wait_ge(xnl_done, i)
                    pe.wait_ge(kl_done, i)
                    for b in range(KB):
                        blk = slice(b * P, (b + 1) * P)
                        last = three(ps[:, b, :], [(xn_hi[:, p, blk], xn_lo[:, p, blk], k_hi[:, p, :], k_lo[:, p, :])],
                                     first, final)
                    last.then_inc(m_done, 1)
                if live(i, T):
                    wait_count(pe, zq_done, i)
                    three(bank_q, [(xT_hi[:, s, b * P:(b + 1) * P], xT_lo[:, s, b * P:(b + 1) * P],
                                    wq_hi[:, b, :], wq_lo[:, b, :]) for b in range(KB)], True, True).then_inc(q_psum, 1)

            sweep(pe, step, -1, T, *LOOP_A)

            pe.wait_ge(late_in, 16 * LATE_LOADS)
            pe.wait_ge(zq_done, T)
            pe.wait_ge(ks_done, T)
            sum_rows("ks", ks_acc[:])
            pe.wait_ge(mod2_kb_done, KB)
            for v, j in enumerate(("ga", "sb", "cb", "gb")):
                sum_rows(j, mod2[:, v, :])
            for b in range(KB):
                transposes(f"v{b}", blocks_of(raw_v, b))
            for b in range(KB):
                transposes(f"o{b}", blocks_of(raw_o, b))
            pe.wait_ge(prep_taken, TAKE["v3"] + 1)
            sum_rows("bv", acc_v[:])
            bank_free(pe, "kv")
            pe.wait_ge(prep_taken, TAKE["v3"] + 1)
            for b in range(KB):
                blk = slice(b * P, (b + 1) * P)
                for f in range(KB):
                    last = nc.tensor.matmul(bank("kv")[:, blk], wvT[:, f, blk], mt[f][:, blk], start=(f == 0), stop=(f == KB - 1))
            last.then_inc(prep_psum, 1)
            pe.wait_ge(prep_taken, TAKE["kv"] + 1)
            for b in range(KB):
                bank_free(pe, f"g{b}")
                nc.tensor.matmul(bank(f"g{b}"), kvm[:, b, :], woT[:, b, :], start=True, stop=True).then_inc(prep_psum, 1)
            for b in range(KB):
                transposes(f"fv{b}", blocks_of(raw_fv, b))
            for b in range(KB):
                blk = slice(b * P, (b + 1) * P)
                transposes(f"cat{b}", [raw_cat[:, 0, blk], raw_cat[:, 1, blk], raw_cat[0:PV + E, 2, blk]])
            pe.wait_ge(prep_taken, TAKE["cat3"] + 1)
            for b in range(KB):
                j = f"u{b}"
                bank_free(pe, j)
                for d in range(KB):
                    last = nc.tensor.matmul(bank(j)[:, 0:C], raw_fv[:, d, b * P:(b + 1) * P], catT[:, d, :],
                                            start=(d == 0), stop=(d == KB - 1))
                last.then_inc(prep_psum, 1)
            pe.wait_ge(prep_taken, TAKE["u3"] + 1)
            sum_rows("bc", acc_c[:])
            sum_rows("bfv", acc_fv[:])
            for b in range(2):
                transposes(f"w2{b}", [raw_w2[:, d, 4 * b:4 * b + 4, :].rearrange("p e i -> p (e i)") for d in range(KB)])
            pe.wait_ge(weights_ready, 1)

            def out_product(j, h):
                t = 2 * j + h
                pe.wait_ge(qTl_done, t + 1)
                wait_count(pe, x1_done, t)
                three(bank_o, [(qT_hi[:, h, b * P:(b + 1) * P], qT_lo[:, h, b * P:(b + 1) * P],
                                g_hi[:, b, :], g_lo[:, b, :]) for b in range(KB)], True, True).then_inc(o_psum, 1)

            def x2_blocks(h):
                return [(xT_hi[:, h, b * P:(b + 1) * P], xT_lo[:, h, b * P:(b + 1) * P]) for b in range(KB)]

            def fused_product(j, h):
                t = 2 * j + h
                pe.wait_ge(x2Tl_done, t + 1)
                wait_count(pe, zf_done, t)
                three(bank_f[:, 0:C], [(*a, c_hi[:, b, :], c_lo[:, b, :]) for b, a in enumerate(x2_blocks(h))],
                      True, True).then_inc(f_psum, 1)

            def value_product(j, h):
                t = 2 * j + h
                wait_count(pe, fin_done, t - 1)
                three(bank_y(h), [(*a, v_hi[:, b, :], v_lo[:, b, :]) for b, a in enumerate(x2_blocks(h))],
                      True, False).then_inc(y_v_done, 1)

            def expert_product(j, h):
                t = 2 * j + h
                pe.wait_ge(aTl_done, t + 1)
                nc.tensor.matmul(bank_y(h), aT_hi[:, h, 2 * P:3 * P], b2st[:], start=False, stop=False)
                three(bank_y(h), [(aT_hi[:, h, b * P:(b + 1) * P], aT_lo[:, h, b * P:(b + 1) * P],
                                   w2_hi[:, b, :], w2_lo[:, b, :]) for b in range(2)], False, True).then_inc(y_psum, 1)

            def turn(dst, src, n):
                for b in range(n):
                    blk = slice(b * P, (b + 1) * P)
                    last = nc.tensor.transpose(dst[:, blk], src[:, blk], ident[:])
                return last

            def turn_q(j, h):
                t = 2 * j + h
                pe.wait_ge(qz_done, j + 1)
                if h == 0 and live(j - 3, J):
                    pe.wait_ge(aTl_done, 2 * (j - 3) + 2)
                wait_count(pe, qTl_done, t)
                turn(bank_qaT, qz[:, h, :], KB).then_inc(qT_psum, 1)

            def turn_hidden(j, h):
                t = 2 * j + h
                pe.wait_ge(aw_done, j + 1)
                if h == 0 and live(j + 2, J):
                    pe.wait_ge(qTl_done, 2 * (j + 2) + 2)
                wait_count(pe, aTl_done, t)
                turn(bank_qaT, aw[:, h, :], 3).then_inc(aT_psum, 1)

            def turn_x2(j, h):
                t = 2 * j + h
                pe.wait_ge(x2_done, t + 1)
                wait_count(pe, x2Tl_done, t)
                turn(bank_x2T, xn[:, h, :], KB).then_inc(x2T_psum, 1)

            def step_b(j):
                if live(j, J):
                    out_product(j, 0)
                if live(j - 1, J):
                    fused_product(j - 1, 0)
                if live(j - 2, J):
                    turn_hidden(j - 2, 0)
                if live(j, J):
                    out_product(j, 1)
                if live(j - 2, J):
                    expert_product(j - 2, 0)
                    turn_hidden(j - 2, 1)
                if live(j - 1, J):
                    fused_product(j - 1, 1)
                if live(j - 2, J):
                    expert_product(j - 2, 1)
                if live(j + 1, J):
                    turn_q(j + 1, 0)
                if live(j - 1, J):
                    value_product(j - 1, 0)
                if live(j, J):
                    turn_x2(j, 0)
                if live(j + 1, J):
                    turn_q(j + 1, 1)
                if live(j - 1, J):
                    value_product(j - 1, 1)
                if live(j, J):
                    turn_x2(j, 1)

            sweep_pairs(pe, step_b, -1, J + 1, *LOOP_B)


_INS = ["L0_attn_hidden_states", "L0_attn_Wq", "L0_attn_bq", "L0_attn_Wk", "L0_attn_bk", "L0_attn_Wv",
        "L0_attn_bv", "L0_attn_Wo", "L0_attn_bo", "L0_ffn_Wv", "L0_ffn_bv", "L0_ffn_Wg", "L0_ffn_bg",
        "L0_ffn_Wp", "L0_ffn_alpha", "L0_ffn_g_r", "L0_ffn_b_r", "L0_ffn_g_c", "L0_ffn_b_c", "L0_ffn_W1",
        "L0_ffn_b1", "L0_ffn_W2", "L0_ffn_b2", "L0_c", "L0_wmod"]


def kernel(**inputs):
    import numpy as _np
    import concourse.bacc as _bacc
    from concourse import mybir as _mybir
    from concourse.bass_utils import run_bass_kernel_spmd as _run

    nc = _bacc.Bacc("TRN2", target_bir_lowering=False, num_devices=1)
    arrays, args = {}, []
    for name in _INS:
        a = _np.ascontiguousarray(inputs[name])
        if name == "L0_ffn_alpha":
            a = a.reshape(1, 1)
        arrays[f"in_{name}_dram"] = a
        args.append(nc.dram_tensor(f"in_{name}_dram", a.shape, _mybir.dt.from_np(a.dtype), kind="ExternalInput").ap())
    shape = inputs["L0_attn_hidden_states"].shape
    args.append(nc.dram_tensor("out_0_dram", shape, _mybir.dt.float32, kind="ExternalOutput").ap())
    build(nc, *args)
    r = _run(nc, [arrays], core_ids=[0])
    return r.results[0]["out_0_dram"]
```

```python
from contextlib import ExitStack

import concourse.bass as bass
from concourse import mybir

ALU = mybir.AluOpType
ACT = mybir.ActivationFunctionType
AX = mybir.AxisListType
F32 = mybir.dt.float32
F32R = mybir.dt.float32r

P = 128
D = 512
KB = D // P
HEADS = 16
DH = D // HEADS
E = 8
INNER = 32
PD = 8
HID = E * INNER
PV = E * PD
C = HID + PV + E
EPS = 1e-5
SMALL_LOADS = 17
WARM_UP = 28
SENTINEL = -3.0e38
TAKEN = -3.3e38

PREP = {0: ["", "", "bk", "bq"], 3: ["v0", "v1"], 4: ["v2", "v3"], 5: ["bv", ""], 6: ["", "ga"], 7: ["o0", "o1"],
        8: ["o2", "o3"], 9: ["sb", "gb"], 10: ["cat0", ""], 11: ["cat1", "fv0"], 12: ["cat2", "fv1"],
        13: ["cat3", "fv2"], 14: ["", "fv3"], 15: ["u0", "u1"], 16: ["u2", "u3"], 17: ["bc", "w20"],
        18: ["", "bfv"], 19: ["", "w21"]}
PREP_STEPS = 20


def f32(ap):
    return ap.bitcast(F32)


def wait_count(eng, sem, n):
    if not isinstance(n, int) or n > 0:
        eng.wait_ge(sem, n)


def sweep(eng, step, first, last, loop_from, loop_to):
    for i in range(first, loop_from):
        step(i, i % 2)
    with eng.Fori(loop_from, loop_to, 2) as v:
        step(v, 0)
        step(v + 1, 1)
    for i in range(loop_to + 1, last + 1):
        step(i, i % 2)


def sweep_pairs(eng, step, first, last, loop_from, loop_to):
    for j in range(first, loop_from):
        step(j)
    with eng.Fori(loop_from, loop_to + 1) as v:
        step(v)
    for j in range(loop_to + 1, last + 1):
        step(j)


def prep_job(i, n):
    jobs = PREP.get(i, []) if isinstance(i, int) else []
    return [j for j in (jobs[2:] if n == 2 else jobs[n:n + 1]) if j]


def live(t, tiles):
    return not isinstance(t, int) or 0 <= t < tiles


def landed(t, slot):
    return (t - slot) * 8 + 16


def build(nc, x, Wq, bq, Wk, bk, Wv, bv, Wo, bo, fWv, fbv, Wg, bg, Wp, alpha, g_r, b_r, g_c, b_c,
          W1, b1, W2, b2, c, wmod, out):
    T = x.shape[1] // P
    assert T % 2 == 0 and T > 24
    LOOP_A = (PREP_STEPS, T - 5)
    J = T // 2
    LOOP_B = (3, J - 3)
    xt = x.rearrange("a (t p) d -> (a t p) d", p=P)
    ot = out.rearrange("a (t p) d -> (a t p) d", p=P)
    q_dram = nc.dram_tensor("q_scratch", [T * P, D], F32, kind="Internal").ap()

    def rows(i):
        return bass.ds(i * P, P)

    ctx = ExitStack()
    with ctx:
        def sb(name, shape, dt=F32, stack=ctx):
            return stack.enter_context(nc.sbuf_tensor(name, shape, dt))

        def sem(name):
            return ctx.enter_context(nc.semaphore(name))

        ps = ctx.enter_context(nc.psum_tensor("ps", [P, 8, D], F32))

        ident = sb("ident", [P, P])
        headmask = sb("headmask", [P, P])
        ones = sb("ones", [P, P])
        neg_half = sb("neg_half", [P, 8])
        half = sb("half", [P, 8])
        raw_v = sb("raw_v", [P, KB, D])
        raw_o = sb("raw_o", [P, KB, D])
        raw_fv = sb("raw_fv", [P, KB, D])
        raw_cat = sb("raw_cat", [P, 3, D])
        raw_w2 = sb("raw_w2", [P, KB, E, INNER])
        bv_row = sb("bv_row", [P, D])
        bo_ga = sb("bo_ga", [P, D])
        fbv_row = sb("fbv_row", [P, D])
        bias_cols = sb("bias_cols", [P, 2 * KB])
        bvp_col, fbv_col = bias_cols[:, 0:KB], bias_cols[:, KB:2 * KB]
        b2raw = sb("b2raw", [P, D])
        bcat = sb("bcat", [P, C])
        rt = sb("rt", [P, 5, E])
        al = sb("al", [P, 4])
        sa_col = sb("sa_col", [P, KB])
        ca1_col = sb("ca1_col", [P, KB])
        acc_v = sb("acc_v", [P, D])
        ks_acc = sb("ks_acc", [P, D])
        mod2 = sb("mod2", [P, 4, D])
        c_col = sb("c_col", [P, 3, KB])
        wvT = sb("wvT", [P, KB, D])
        woT = raw_v
        catT = raw_o[:, :, 0:C]
        sb_col = sb("sb_col", [P, KB])
        cb1_col = sb("cb1_col", [P, KB])
        small = sb("small", [P, 2])
        wtmp = sb("wtmp", [P, 2, D])
        qf = sb("qf", [P, 2, D])
        out_t = qf
        xin = sb("xin", [P, 2, D])
        stats = sb("stats", [P, 2, 6])
        mv = sb("mv", [P, 2, 2])
        veps = sb("veps", [P, 2])
        rstd = sb("rstd", [P, 2])
        xn = sb("xn", [P, 2, D])
        xT_hi = sb("xT_hi", [P, 2, D], F32R)
        xT_lo = sb("xT_lo", [P, 2, D], F32R)

        first = ExitStack()
        raw_k = sb("raw_k", [P, KB, D], F32, first)
        raw_q = sb("raw_q", [P, KB, D], F32, first)
        mod1 = sb("mod1", [P, 2, D], F32, first)
        acc_k = sb("acc_k", [P, D], F32, first)
        acc_q = sb("acc_q", [P, D], F32, first)
        wm_in = sb("wm_in", [P, 2, KB, D], F32, first)
        first.close()

        v_hi = sb("v_hi", [P, KB, D], F32R)
        v_lo = sb("v_lo", [P, KB, D], F32R)
        c_hi = sb("c_hi", [P, KB, C], F32R)
        c_lo = sb("c_lo", [P, KB, C], F32R)
        w2_hi = sb("w2_hi", [P, 2, D], F32R)
        w2_lo = sb("w2_lo", [P, 2, D], F32R)
        b2st = sb("b2st", [P, 2, D], F32R)
        acc_fv = sb("acc_fv", [P, D])
        bf_row = sb("bf_row", [P, C])
        acc_c = sb("acc_c", [P, C])

        early = ExitStack()
        wq_hi = sb("wq_hi", [P, KB, D], F32R, early)
        wq_lo = sb("wq_lo", [P, KB, D], F32R, early)
        wk_hi = sb("wk_hi", [P, KB, D], F32R, early)
        wk_lo = sb("wk_lo", [P, KB, D], F32R, early)
        bk_row = sb("bk_row", [P, D], F32, early)
        bq_row = sb("bq_row", [P, D], F32, early)
        xn_hi = sb("xn_hi", [P, 2, D], F32R, early)
        xn_lo = sb("xn_lo", [P, 2, D], F32R, early)
        zk = sb("zk", [P, 2, D], F32, early)
        exp_k = sb("exp_k", [P, 2, D], F32, early)
        kf = sb("kf", [P, 2, D], F32, early)
        k_hi = sb("k_hi", [P, 2, D], F32R, early)
        k_lo = sb("k_lo", [P, 2, D], F32R, early)
        zq = sb("zq", [P, 2, D], F32, early)
        exp_q = sb("exp_q", [P, 2, D], F32, early)
        early.close()

        late = ExitStack()
        q_in = sb("q_in", [P, 4 * D], F32, late)
        qks = sb("qks", [P, 2, D], F32, late)
        qz = sb("qz", [P, 2, D], F32, late)
        xb = sb("xb", [P, 2, D], F32, late)
        ks_row = sb("ks_row", [P, D], F32, late)
        g_hi = sb("g_hi", [P, KB, D], F32R, late)
        g_lo = sb("g_lo", [P, KB, D], F32R, late)
        den = sb("den", [P, 2, HEADS], F32, late)
        den_eps = sb("den_eps", [P, 2, HEADS], F32, late)
        zr = sb("zr", [P, 2, HEADS], F32, late)
        qT_hi = sb("qT_hi", [P, 2, D], F32R, late)
        qT_lo = sb("qT_lo", [P, 2, D], F32R, late)
        x1 = sb("x1", [P, 6 * D], F32, late)
        zf = sb("zf", [P, 2, C + E], F32, late)
        sq = sb("sq", [P, 2, PV], F32, late)
        th = sb("th", [P, 2, HID], F32, late)
        hz = sb("hz", [P, 2, HID], F32, late)
        c2 = sb("c2", [P, 2, E], F32, late)
        cn = sb("cn", [P, 2, E], F32, late)
        csum = sb("csum", [P, 2], F32, late)
        rsq = sb("rsq", [P, 2, 2, E], F32, late)
        rvar = sb("rvar", [P, 4], F32, late)
        rve = sb("rve", [P, 4], F32, late)
        rrs = sb("rrs", [P, 2, 2], F32, late)
        s1 = sb("s1", [P, 2, 2, E], F32, late)
        s2 = sb("s2", [P, 2, 2, E], F32, late)
        s3 = sb("s3", [P, 2, E], F32, late)
        sx = sb("sx", [P, 2, 16], F32, late)
        m8 = sb("m8", [P, 2, 8], F32, late)
        top = sb("top", [P, 2, 8], F32, late)
        marked = sb("marked", [P, 2, 16], F32, late)
        mask = sb("mask", [P, 2, E], F32, late)
        sm = sb("sm", [P, 2, E], F32, late)
        ex = sb("ex", [P, 2, E], F32, late)
        wn = sb("wn", [P, 2, E], F32, late)
        wsum = sb("wsum", [P, 2], F32, late)
        winv = sb("winv", [P, 2], F32, late)
        wt = sb("wt", [P, 2, E], F32, late)
        aw = sb("aw", [P, 2, HID], F32, late)
        ws = sb("ws", [P, P], F32, late)
        aT_hi = sb("aT_hi", [P, 2, 2 * P], F32R, late)
        wT_hi = sb("wT_hi", [P, P], F32R, late)
        aT_lo = sb("aT_lo", [P, 2, 2 * P], F32R, late)
        mt = [x1[:, b * D:(b + 1) * D] for b in range(KB)]
        kvm = x1[:, 4 * D:5 * D].rearrange("p (b n) -> p b n", n=P)
        outer = x1[:, 5 * D:6 * D].rearrange("p (b n) -> p b n", n=P)
        late.close()

        c_in = sem("c_in")
        wk_in = sem("wk_in")
        wq_in = sem("wq_in")
        wma_in = [sem(f"wma_in{b}") for b in range(KB)]
        wmv_in = [sem(f"wmv_in{v}") for v in range(4)]
        bias_in = sem("bias_in")
        v_in = sem("v_in")
        o_in = sem("o_in")
        fv_in = sem("fv_in")
        cat_in = sem("cat_in")
        w2_in = sem("w2_in")
        rows_in = sem("rows_in")
        b2_zeroed = sem("b2_zeroed")
        pool_const = sem("pool_const")
        pool_step = sem("pool_step")
        dve_const = sem("dve_const")
        dve_step = sem("dve_step")
        c_exp = sem("c_exp")
        al_exp = sem("al_exp")
        mod1_done = sem("mod1_done")
        mod2_done = sem("mod2_done")
        acc_step = sem("acc_step")
        wlo_done = sem("wlo_done")
        cat_done = sem("cat_done")
        mt_dve = sem("mt_dve")
        mt_act = sem("mt_act")
        kvm_done = sem("kvm_done")
        ks_row_done = sem("ks_row_done")
        b_cleared = sem("b_cleared")
        prep_psum = sem("prep_psum")
        prep_hi = sem("prep_hi")
        prep_taken = sem("prep_taken")
        prep_tmp = sem("prep_tmp")
        weights_ready = sem("weights_ready")
        x_in = [sem("x_in0"), sem("x_in1")]
        stats_done = sem("stats_done")
        mv_done = sem("mv_done")
        veps_done = sem("veps_done")
        rstd_done = sem("rstd_done")
        xn_done = sem("xn_done")
        xnh_done = sem("xnh_done")
        xnl_done = sem("xnl_done")
        xT_psum = sem("xT_psum")
        xTh_done = sem("xTh_done")
        xTl_done = sem("xTl_done")
        k_psum = sem("k_psum")
        zk_done = sem("zk_done")
        rk_done = sem("rk_done")
        ek_done = sem("ek_done")
        kf_done = sem("kf_done")
        kh_done = sem("kh_done")
        kl_done = sem("kl_done")
        ks_done = sem("ks_done")
        m_done = sem("m_done")
        q_psum = sem("q_psum")
        zq_done = sem("zq_done")
        rq_done = sem("rq_done")
        eq_done = sem("eq_done")
        qf_done = sem("qf_done")
        q_out = [sem("q_out0"), sem("q_out1")]
        bx_in = sem("bx_in")
        q_back = sem("q_back")
        qks_done = sem("qks_done")
        den_done = sem("den_done")
        deneps_done = sem("deneps_done")
        zr_done = sem("zr_done")
        qz_done = sem("qz_done")
        xb_done = sem("xb_done")
        bveps_done = sem("bveps_done")
        brstd_done = sem("brstd_done")
        hz_done = sem("hz_done")
        csum_done = sem("csum_done")
        cc_done = sem("cc_done")
        rsq_done = sem("rsq_done")
        rvar_done = sem("rvar_done")
        rve_done = sem("rve_done")
        rrs_done = sem("rrs_done")
        s1_done = sem("s1_done")
        s2_done = sem("s2_done")
        s3_done = sem("s3_done")
        sx_done = sem("sx_done")
        m8_done = sem("m8_done")
        sm_done = sem("sm_done")
        top_done = sem("top_done")
        ex_done = sem("ex_done")
        marked_done = sem("marked_done")
        mask_done = sem("mask_done")
        wn_done = sem("wn_done")
        wsum_done = sem("wsum_done")
        winv_done = sem("winv_done")
        wt_done = sem("wt_done")
        wth_done = sem("wth_done")
        aw_done = sem("aw_done")
        qT_psum = sem("qT_psum")
        qTh_done = sem("qTh_done")
        qTl_done = sem("qTl_done")
        o_psum = sem("o_psum")
        x1_done = sem("x1_done")
        bstats_done = sem("bstats_done")
        bmv_done = sem("bmv_done")
        x2_done = sem("x2_done")
        x2T_psum = sem("x2T_psum")
        x2Th_done = sem("x2Th_done")
        x2Tl_done = sem("x2Tl_done")
        f_psum = sem("f_psum")
        zf_done = sem("zf_done")
        sq_done = sem("sq_done")
        th_done = sem("th_done")
        c2_done = sem("c2_done")
        cn_done = sem("cn_done")
        aT_psum = sem("aT_psum")
        aTh_done = sem("aTh_done")
        aTl_done = sem("aTl_done")
        y_v_done = sem("y_v_done")
        y_psum = sem("y_psum")
        fin_done = sem("fin_done")
        stored = [sem("stored0"), sem("stored1")]

        def q_of(j):
            return q_in[:, bass.ds(j % 2 * (2 * D), 2 * D)]

        def x1_of(j, h):
            return x1[:, bass.ds(j % 3 * (2 * D) + h * D, D)]

        bank_xT = ps[:, 4, :]
        bank_k, bank_q = ps[:, 6, :], ps[:, 7, :]
        bank_qaT, bank_x2T, bank_o, bank_f = ps[:, 4, :], ps[:, 5, :], ps[:, 6, :], ps[:, 7, :]
        def bank_y(h): return ps[:, h, :]

        JOBS = ["sa", "k0", "k1", "k2", "k3", "q0", "q1", "q2", "q3"]
        BANK = dict(zip(JOBS, (0, 4, 2, 3, 1, 6, 7, 5, 0)))
        for step_jobs in PREP.values():
            JOBS += [j for j in step_jobs if j]
            BANK.update({j: 5 for j in step_jobs if j})
        BANK["bq"] = 0
        IN_LOOP = len(JOBS)
        JOBS += ["ks", "kv", "g0", "g1", "g2", "g3"]
        BANK.update(zip(JOBS[IN_LOOP:], (5, 6, 0, 1, 2, 3)))
        JOB = {j: n for n, j in enumerate(JOBS)}
        SUMMED = {j: n for n, j in enumerate(["k0", "q0", "q1", "q2", "k1", "k2", "k3", "q3", "v0", "v1", "v2", "v3"]
                                             + [j for j in JOBS if j[:3] == "cat" or j[:2] == "fv" or j[0] == "u"])}
        TAKE = {j: n for n, j in enumerate([j for j in JOBS if j not in SUMMED or j[0] == "v" or j[0] == "c"])}

        def bank(j):
            return ps[:, BANK[j], :]

        def bank_free(eng, j):
            before = [k for k in JOBS[:JOB[j]] if BANK[k] == BANK[j]]
            if before and before[-1] in TAKE:
                eng.wait_ge(prep_taken, TAKE[before[-1]] + 1)
            elif before:
                eng.wait_ge(acc_step, SUMMED[before[-1]] + 1)

        HI_JOBS = ["k0", "k1", "k2", "k3", "q0", "q1", "q2", "q3",
                   "fv0", "fv1", "fv2", "fv3", "u0", "u1", "u2", "u3", "w20", "w21", "g0", "g1", "g2", "g3"]
        HI = {j: n for n, j in enumerate(HI_JOBS)}
        TMP_JOBS = [j for j in HI_JOBS if j[0] in "fw"]
        TMP = {j: n for n, j in enumerate(TMP_JOBS)}

        block = ctx.enter_context(nc.Block())

        @block.sync
        def _(sp):
            sp.dma_start(c_col[:, 0, :], c.rearrange("a (p b) -> p (a b)", p=P)).then_inc(c_in, 16)
            sp.dma_start(xin[:, 0, :], xt[rows(0), :]).then_inc(x_in[0], 16)
            wm = wmod.rearrange("(p b) (v n) -> p b v n", p=P, n=D)
            for b in range(KB):
                sp.dma_start(wm_in[:, :, b, :], wm[:, b, 0:2, :]).then_inc(wma_in[b], 16)
            sp.dma_start(raw_k[:], Wk.rearrange("(r p) f -> p r f", p=P)).then_inc(wk_in, 16)
            sp.dma_start(xin[:, 1, :], xt[rows(1), :]).then_inc(x_in[1], 16)
            sp.dma_start(raw_q[:], Wq.rearrange("(r p) f -> p r f", p=P)).then_inc(wq_in, 16)

            def row_load(row, src, signal):
                sp.dma_start(row, src.rearrange("(a n) -> a n", a=1).to_broadcast([P, row.shape[1]])).then_inc(signal, 16)

            row_load(bk_row[:], bk, bias_in)
            row_load(bq_row[:], bq, bias_in)

            def loads(i):
                if i in (-1, 1, 3, 5):
                    v = (i + 1) // 2
                    sp.wait_ge(mod1_done, KB)
                    if v >= 2:
                        sp.wait_ge(mod2_done, KB * (v - 1))
                    sp.dma_start(wm_in[:, v % 2, :, :], wm[:, :, v + 2, :]).then_inc(wmv_in[v], 16)
                if i == T:
                    sp.wait_ge(xn_done, T)
                    bx_load(0)
                    sp.wait_ge(q_psum, T)
                    sp.wait_ge(q_out[0], 32)
                    sp.wait_ge(q_out[1], 32)
                    q_load(0)
                    q_load(1)
                if i == 0:
                    sp.dma_start(raw_v[:], Wv.rearrange("(r p) f -> p r f", p=P)).then_inc(v_in, 16)
                if i == 1:
                    for row, src in ((bv_row, bv), (bo_ga, bo), (fbv_row, fbv)):
                        row_load(row[:], src, rows_in)
                if i == 2:
                    sp.dma_start(raw_o[:], Wo.rearrange("(r p) f -> p r f", p=P)).then_inc(o_in, 16)
                if i == 4:
                    sp.dma_start(raw_cat[:, 0:2, :], W1.rearrange("(r e) i d -> (e i) r d", r=2)).then_inc(cat_in, 16)
                    sp.dma_start(raw_cat[0:PV, 2, :], Wp.rearrange("e q d -> (e q) d")).then_inc(cat_in, 16)
                    sp.dma_start(raw_cat[PV:PV + E, 2, :], Wg).then_inc(cat_in, 16)
                if i == 6:
                    sp.dma_start(raw_fv[:], fWv.rearrange("(r p) f -> p r f", p=P)).then_inc(fv_in, 16)
                if i == 7:
                    for b in range(KB):
                        sp.dma_start(raw_w2[:, b, :, :],
                                     W2[:, b * P:(b + 1) * P, :].rearrange("e p i -> p e i")).then_inc(w2_in, 16)
                if i == 8:
                    sp.dma_start(bcat[:, 0:HID],
                                 b1.rearrange("(a e) i -> a (e i)", a=1).to_broadcast([P, HID])).then_inc(w2_in, 16)
                    row_load(bcat[:, HID + PV:C], bg, w2_in)
                    for n, src in enumerate((b_r, g_r, g_c, b_c)):
                        row_load(rt[:, n, :], src, w2_in)
                    sp.dma_start(al[:, 0:1], alpha.to_broadcast([P, 1])).then_inc(w2_in, 16)
                    sp.wait_ge(b2_zeroed, 1)
                    for h in range(2):
                        for r in (0, E, 32):
                            sp.dma_start(b2raw[64 * h + r:64 * h + r + E, :], b2).then_inc(w2_in, 16)

            def pair_rows(j):
                return bass.ds(j * 2 * P, 2 * P)

            def bx_load(j):
                sp.dma_start(xin[:], xt[pair_rows(j), :].rearrange("(h p) d -> p h d", p=P)).then_inc(bx_in, 16)

            def q_load(j):
                wait_count(sp, q_back, 16 * j)
                sp.dma_start(q_of(j).rearrange("p (h d) -> p h d", d=D),
                             q_dram[pair_rows(j), :].rearrange("(h p) d -> p h d", p=P)).then_inc(q_back, 16)

            def step(i, s):
                if live(i + 4, T):
                    wait_count(sp, xn_done, i + 3)
                    sp.dma_start(xin[:, s, :], xt[rows(i + 4), :]).then_inc(x_in[s], 16)
                if isinstance(i, int):
                    loads(i)
                if live(i - 1, T):
                    sp.wait_ge(qf_done, i)
                    sp.dma_start(q_dram[rows(i - 1), :], qf[:, 1 - s, :]).then_inc(q_out[1 - s], 16)

            sweep(sp, step, -2, T, *LOOP_A)
            sp.wait_ge(q_out[0], landed(T - 2, 0))
            sp.wait_ge(q_out[1], landed(T - 1, 1))

            def step_b(j):
                if live(j + 2, J):
                    if not (isinstance(j, int) and j < 0):
                        wait_count(sp, qz_done, j + 1)
                        q_load(j + 2)
                for h in range(2):
                    if live(j - 2, J):
                        sp.wait_ge(fin_done, 2 * (j - 2) + h + 1)
                        sp.dma_start(ot[rows((j - 2) * 2 + h), :], out_t[:, h, :]).then_inc(stored[h], 16)
                if live(j + 2, J):
                    wait_count(sp, xb_done, j + 2)
                    bx_load(j + 2)

            sweep_pairs(sp, step_b, -1, J + 1, *LOOP_B)
            sp.wait_ge(stored[0], landed(T - 2, 0))
            sp.wait_ge(stored[1], landed(T - 1, 1))

        @block.gpsimd
        def _(pool):
            steps = [0]

            def link(ins):
                steps[0] += 1
                ins.then_inc(pool_step, 1)
                pool.wait_ge(pool_step, steps[0])

            link(nc.gpsimd.memset(ident[:], 0.0))
            nc.gpsimd.affine_select(out=ident[:], in_=ident[:], compare_op=ALU.not_equal, fill=1.0,
                                    base=0, pattern=[[-1, P]], channel_multiplier=1).then_inc(pool_const, 1)
            link(nc.gpsimd.memset(headmask[:], 1.0))
            hm = headmask[:].rearrange("p (g d) -> p g d", d=DH)
            link(nc.gpsimd.affine_select(out=hm, in_=hm, compare_op=ALU.is_ge, fill=0.0, base=0,
                                         pattern=[[-DH, P // DH], [0, DH]], channel_multiplier=1))
            nc.gpsimd.affine_select(out=hm, in_=hm, compare_op=ALU.is_ge, fill=0.0, base=DH - 1,
                                    pattern=[[DH, P // DH], [0, DH]], channel_multiplier=-1).then_inc(pool_const, 1)
            link(nc.gpsimd.memset(ks_acc[:], 0.0))
            pool.wait_ge(dve_const, 1)

            def step(i, s):
                if live(i + 2, T):
                    wait_count(pool, veps_done, i + 3)
                    nc.gpsimd.tensor_tensor(rstd[:, s:s + 1], veps[:, s:s + 1], neg_half[:, 0:1],
                                            ALU.pow).then_inc(rstd_done, 1)
                if live(i, T):
                    pool.wait_ge(kf_done, i + 1)
                    wait_count(pool, ks_done, i)
                    nc.gpsimd.tensor_tensor(ks_acc[:], ks_acc[:], kf[:, s, :], ALU.add).then_inc(ks_done, 1)
                if live(i + 1, T):
                    pool.wait_ge(xnh_done, i + 2)
                    pool.wait_ge(xn_done, i + 2)
                    nc.gpsimd.tensor_tensor(xn_lo[:, 1 - s, :], xn[:, 1 - s, :], f32(xn_hi[:, 1 - s, :]),
                                            ALU.subtract).then_inc(xnl_done, 1)

            sweep(pool, step, -2, T - 1, *LOOP_A)

            def biased_x(j):
                pool.wait_ge(bx_in, 16 * (j + 1))
                wait_count(pool, x1_done, 2 * j)
                nc.gpsimd.tensor_tensor(xb[:], xin[:], bo_ga[:].unsqueeze(1).to_broadcast([P, 2, D]),
                                        ALU.add).then_inc(xb_done, 1)

            pool.wait_ge(weights_ready, 1)
            pool.wait_ge(q_psum, T)
            biased_x(0)
            pool.wait_ge(m_done, T)
            pool.wait_ge(qf_done, T)
            pool.wait_ge(ks_done, T)
            nc.gpsimd.memset(sx[:], SENTINEL).then_inc(b_cleared, 1)
            nc.gpsimd.memset(top[:], SENTINEL).then_inc(b_cleared, 1)
            nc.gpsimd.memset(ws[:], 0.0).then_inc(b_cleared, 1)
            pool.wait_ge(ks_row_done, 1)

            def q_times_ks(j):
                pool.wait_ge(q_back, 16 * (j + 1))
                wait_count(pool, den_done, j)
                nc.gpsimd.tensor_tensor(qks[:], q_of(j).rearrange("p (h d) -> p h d", d=D),
                                        ks_row[:].unsqueeze(1).to_broadcast([P, 2, D]), ALU.mult).then_inc(qks_done, 1)

            def step_b(j):
                first = isinstance(j, int) and j == 0
                if live(j + 1, J):
                    pool.wait_ge(zr_done, j + 2)
                    wait_count(pool, qT_psum, 2 * j + 2)
                    nc.gpsimd.tensor_tensor(
                        qz[:].rearrange("p h (n d) -> p (h n) d", d=DH),
                        q_of(j + 1).rearrange("p (n d) -> p n d", d=DH),
                        zr[:].rearrange("p h n -> p (h n)").unsqueeze(2).to_broadcast([P, 2 * HEADS, DH]),
                        ALU.mult).then_inc(qz_done, 1)
                if live(j + 2, J) and not first:
                    q_times_ks(j + 2)
                if live(j - 1, J):
                    pool.wait_ge(c2_done, 2 * j - 1)
                    wait_count(pool, cc_done, j - 1)
                    nc.gpsimd.tensor_tensor(cn[:, 0, :], c2[:, 0, :], half[:], ALU.pow).then_inc(cn_done, 1)
                if live(j, J):
                    pool.wait_ge(bveps_done, j + 1)
                    wait_count(pool, x2_done, 2 * j)
                    nc.gpsimd.tensor_tensor(rstd[:], veps[:], neg_half[:, 0:2], ALU.pow).then_inc(brstd_done, 1)
                if live(j - 1, J):
                    pool.wait_ge(c2_done, 2 * j)
                    nc.gpsimd.tensor_tensor(cn[:, 1, :], c2[:, 1, :], half[:], ALU.pow).then_inc(cn_done, 1)
                    pool.wait_ge(rve_done, j)
                    wait_count(pool, s1_done, j - 1)
                    nc.gpsimd.tensor_tensor(rrs[:].rearrange("p h k -> p (h k)"), rve[:], neg_half[:, 0:4],
                                            ALU.pow).then_inc(rrs_done, 1)
                if live(j + 1, J) and not (isinstance(j, int) and j == -1):
                    biased_x(j + 1)
                if first:
                    q_times_ks(j + 2)

            sweep_pairs(pool, step_b, -2, J, *LOOP_B)

        @block.scalar
        def _(act):
            act.wait_ge(c_in, 16)
            nc.scalar.activation(c_col[:, 1, :], c_col[:, 0, :], ACT.Exp, scale=-1.0).then_inc(c_exp, 1)

            def hi_scaled(j, dst, col):
                act.wait_ge(prep_psum, JOB[j] + 1)
                nc.scalar.activation(dst, bank(j)[:, 0:dst.shape[1]], ACT.Copy, scale=col).then_inc(prep_hi, 1)

            def hi_tmp(j, dst):
                act.wait_ge(prep_tmp, TMP[j] + 1)
                nc.scalar.copy(dst, wtmp[:, TMP[j] % 2, :]).then_inc(prep_hi, 1)

            def prepare(i, n):
                for j in prep_job(i, n):
                    b = int(j[-1]) if j[-1].isdigit() else 0
                    if j in ("v0", "v1", "v2", "v3", "cat0", "cat1", "cat2", "cat3"):
                        act.wait_ge(prep_psum, JOB[j] + 1)
                        dst = wvT[:, b, :] if j[0] == "v" else catT[:, b, :]
                        nc.scalar.copy(dst, bank(j)[:, 0:dst.shape[1]]).then_inc(prep_taken, 1)
                    elif j in ("ga", "gb"):
                        act.wait_ge(prep_psum, JOB[j] + 1)
                        nc.scalar.copy(wtmp[:, 1, :], bank(j)).then_inc(prep_taken, 1)
                    elif j[:2] == "fv":
                        hi_tmp(j, v_hi[:, b, :])
                    elif j[:2] == "w2":
                        hi_tmp(j, w2_hi[:, b, :])
                    elif j[0] == "u":
                        hi_scaled(j, c_hi[:, b, :], cb1_col[:, b:b + 1])
                    elif j == "bc":
                        act.wait_ge(w2_in, 16 * SMALL_LOADS)
                        nc.scalar.activation(al[:, 1:2], al[:, 0:1], ACT.Exp, scale=-1.0).then_inc(al_exp, 1)

            act.wait_ge(prep_taken, TAKE["sa"] + 1)
            for b in range(KB):
                hi_scaled(f"k{b}", wk_hi[:, b, :], ca1_col[:, b:b + 1])
            for b in range(KB):
                hi_scaled(f"q{b}", wq_hi[:, b, :], ca1_col[:, b:b + 1])

            def step(i, s):
                if live(i + 1, T):
                    act.wait_ge(xT_psum, i + 2)
                    wait_count(act, xTl_done, i)
                    wait_count(act, q_psum, i)
                    nc.scalar.copy(xT_hi[:, 1 - s, :], bank_xT).then_inc(xTh_done, 1)
                if live(i - 1, T):
                    act.wait_ge(zq_done, i)
                    wait_count(act, qf_done, i - 2)
                    nc.scalar.activation(exp_q[:, 1 - s, :], zq[:, 1 - s, :], ACT.Relu, scale=-1.0).then_inc(rq_done, 1)
                    act.wait_ge(rq_done, i)
                    nc.scalar.activation(exp_q[:, 1 - s, :], exp_q[:, 1 - s, :], ACT.Exp, scale=-1.0).then_inc(eq_done, 1)
                prepare(i, 0)
                if live(i, T):
                    act.wait_ge(zk_done, i + 1)
                    wait_count(act, kf_done, i - 1)
                    nc.scalar.activation(exp_k[:, s, :], zk[:, s, :], ACT.Relu, scale=-1.0).then_inc(rk_done, 1)
                    act.wait_ge(rk_done, i + 1)
                    nc.scalar.activation(exp_k[:, s, :], exp_k[:, s, :], ACT.Exp, scale=-1.0).then_inc(ek_done, 1)
                    act.wait_ge(kf_done, i + 1)
                    wait_count(act, m_done, i - 1)
                    wait_count(act, kl_done, i - 1)
                    nc.scalar.copy(k_hi[:, s, :], kf[:, s, :]).then_inc(kh_done, 1)
                if live(i + 1, T):
                    act.wait_ge(xn_done, i + 2)
                    wait_count(act, m_done, i)
                    wait_count(act, xnl_done, i)
                    nc.scalar.copy(xn_hi[:, 1 - s, :], xn[:, 1 - s, :]).then_inc(xnh_done, 1)
                prepare(i, 1)

            sweep(act, step, -1, T, *LOOP_A)

            act.wait_ge(m_done, T)
            act.wait_ge(qf_done, T)
            act.wait_ge(ks_done, T)
            for b in (2, 3):
                nc.scalar.activation(mt[b], ps[:, b, :], ACT.Copy, scale=ca1_col[:, b:b + 1]).then_inc(mt_act, 1)
            for b in range(KB):
                act.wait_ge(prep_psum, JOB[f"g{b}"] + 1)
                nc.scalar.copy(g_hi[:, b, :], bank(f"g{b}")).then_inc(prep_hi, 1)

            def x2T_high(j, h):
                t = 2 * j + h
                act.wait_ge(x2T_psum, t + 1)
                wait_count(act, y_v_done, t - 1)
                nc.scalar.copy(xT_hi[:, h, :], bank_x2T).then_inc(x2Th_done, 1)

            def qT_high(j, h):
                t = 2 * j + h
                act.wait_ge(qT_psum, t + 1)
                wait_count(act, o_psum, t - 1)
                wait_count(act, qTl_done, t - 1)
                nc.scalar.copy(qT_hi[:, h, :], bank_qaT).then_inc(qTh_done, 1)

            def aT_high(j, h):
                t = 2 * j + h
                act.wait_ge(aT_psum, t + 1)
                wait_count(act, y_psum, t - 1)
                if h == 0:
                    wait_count(act, y_psum, t)
                    nc.scalar.copy(wT_hi[:], bank_qaT[:, 2 * P:3 * P])
                nc.scalar.copy(aT_hi[:, h, :], bank_qaT[:, 0:2 * P]).then_inc(aTh_done, 1)

            def functions(j, h):
                t = 2 * j + h
                act.wait_ge(zf_done, t + 1)
                wait_count(act, c2_done, t - 1)
                nc.scalar.activation(sq[:, h, :], zf[:, h, HID:HID + PV], ACT.Square,
                                     scale=PD ** -0.5).then_inc(sq_done, 1)
                wait_count(act, hz_done, j)
                nc.scalar.activation(th[:, h, :], zf[:, h, 0:HID], ACT.Tanh, scale=0.5).then_inc(th_done, 1)

            def step_b(j):
                if live(j - 1, J):
                    x2T_high(j - 1, 1)
                if live(j - 2, J):
                    aT_high(j - 2, 0)
                if live(j - 1, J):
                    functions(j - 1, 0)
                if live(j - 2, J):
                    aT_high(j - 2, 1)
                if live(j - 1, J):
                    functions(j - 1, 1)
                if live(j + 1, J):
                    qT_high(j + 1, 0)
                if live(j, J):
                    x2T_high(j, 0)
                if live(j + 1, J):
                    qT_high(j + 1, 1)
                if live(j - 1, J):
                    act.wait_ge(sm_done, j)
                    wait_count(act, wn_done, j - 1)
                    nc.scalar.activation(ex[:], sm[:], ACT.Exp).then_inc(ex_done, 1)

            sweep_pairs(act, step_b, -1, J + 1, *LOOP_B)

        @block.vector
        def _(dve):
            steps = [0]

            def link(ins):
                steps[0] += 1
                ins.then_inc(dve_step, 1)
                dve.wait_ge(dve_step, steps[0])

            def wait_apart(sem, n):
                n = n if isinstance(n, int) else dve.snap(n)
                dve.wait_ge(dve_const, 1)
                dve.wait_ge(sem, n)

            nc.vector.memset(neg_half[:], -0.5)
            nc.vector.memset(half[:], 0.5)
            nc.vector.memset(b2raw[:], 0.0).then_inc(b2_zeroed, 1)
            nc.vector.memset(ones[:], 1.0).then_inc(dve_const, 1)

            def statistics(i, s):
                dve.wait_ge(x_in[s], landed(i, s))
                nc.vector.bn_stats(stats[:, s, :], xin[:, s, :]).then_inc(stats_done, 1)
                dve.wait_ge(stats_done, i + 1)

            def mean_var(i, s):
                nc.vector.bn_aggr(mv[:, s, :], stats[:, s, :]).then_inc(mv_done, 1)

            def var_eps(i, s):
                dve.wait_ge(mv_done, i + 1)
                nc.vector.tensor_scalar(veps[:, s:s + 1], mv[:, s, 1:2], EPS, None, ALU.add).then_inc(veps_done, 1)

            def normed(i, s):
                dve.wait_ge(rstd_done, i + 1)
                wait_count(dve, xT_psum, i - 1)
                wait_count(dve, xnh_done, i - 1)
                wait_count(dve, xnl_done, i - 1)
                nc.vector.tensor_scalar(xn[:, s, :], xin[:, s, :], mv[:, s, 0:1], rstd[:, s:s + 1],
                                        ALU.subtract, ALU.mult).then_inc(xn_done, 1)

            def xT_low(i, s):
                dve.wait_ge(xTh_done, i + 1)
                wait_count(dve, q_psum, i - 1)
                nc.vector.tensor_tensor(xT_lo[:, s, :], bank_xT, f32(xT_hi[:, s, :]), ALU.subtract).then_inc(xTl_done, 1)

            statistics(0, 0)
            mean_var(0, 0)
            var_eps(0, 0)
            dve.wait_ge(c_exp, 1)
            link(nc.vector.tensor_scalar(c_col[:, 2, :], c_col[:, 1, :], 1.0, None, ALU.add))
            link(nc.vector.reciprocal(c_col[:, 1, :], c_col[:, 2, :]))
            link(nc.vector.tensor_tensor(c_col[:, 2, :], c_col[:, 0, :], c_col[:, 1, :], ALU.mult))
            normed(0, 0)
            for b in range(KB):
                dve.wait_ge(wma_in[b], 16)
                if b == 0:
                    ins = nc.vector.tensor_scalar(mod1[:], wm_in[:, :, b, :], c_col[:, 2, b:b + 1], None, ALU.mult)
                else:
                    dve.wait_ge(mod1_done, b)
                    ins = nc.vector.scalar_tensor_tensor(out=mod1[:], in0=wm_in[:, :, b, :], scalar=c_col[:, 2, b:b + 1],
                                                         in1=mod1[:], op0=ALU.mult, op1=ALU.add)
                ins.then_inc(mod1_done, 1)

            def full(j):
                dve.wait_ge(prep_psum, JOB[j] + 1)

            def taken_by(ins, j):
                ins.then_inc(prep_taken, 1)
                dve.wait_ge(prep_taken, TAKE[j] + 1)

            accs = [0]

            def accumulate(acc, src, col, first):
                if accs[0]:
                    dve.wait_ge(acc_step, accs[0])
                if first:
                    ins = nc.vector.tensor_scalar(acc, src, col, None, ALU.mult)
                else:
                    ins = nc.vector.scalar_tensor_tensor(out=acc, in0=src, scalar=col, in1=acc, op0=ALU.mult, op1=ALU.add)
                ins.then_inc(acc_step, 1)
                accs[0] += 1

            dve.wait_ge(pool_const, 1)
            full("sa")
            nc.vector.tensor_copy(sa_col[:], bank("sa")[:, 0:KB])
            taken_by(nc.vector.tensor_scalar(ca1_col[:], bank("sa")[:, KB:2 * KB], 1.0, None, ALU.add), "sa")
            statistics(1, 1)
            mean_var(1, 1)
            var_eps(1, 1)

            def low(j, col, hi, lo):
                full(j)
                dve.wait_ge(prep_hi, HI[j] + 1)
                return nc.vector.scalar_tensor_tensor(out=lo, in0=bank(j)[:, 0:lo.shape[1]], scalar=col, in1=f32(hi),
                                                      op0=ALU.mult, op1=ALU.subtract)

            def low_k(b):
                low(f"k{b}", ca1_col[:, b:b + 1], wk_hi[:, b, :], wk_lo[:, b, :]).then_inc(wlo_done, 1)

            def low_q(b):
                low(f"q{b}", ca1_col[:, b:b + 1], wq_hi[:, b, :], wq_lo[:, b, :]).then_inc(wlo_done, 1)

            def sum_k(b):
                accumulate(acc_k[:], bank(f"k{b}"), sa_col[:, b:b + 1], b == 0)

            def sum_q(b):
                accumulate(acc_q[:], bank(f"q{b}"), sa_col[:, b:b + 1], b == 0)

            low_k(0)
            sum_k(0)
            for b in range(1, KB):
                low_k(b)
            normed(1, 1)
            low_q(0)
            sum_q(0)
            xT_low(0, 0)
            for b in (1, 2):
                low_q(b)
                sum_q(b)
            low_q(3)
            for b in range(1, KB):
                sum_k(b)
            sum_q(3)
            statistics(2, 0)
            mean_var(2, 0)
            var_eps(2, 0)
            dve.wait_ge(bias_in, 32)
            full("bk")
            taken_by(nc.vector.tensor_tensor(bk_row[:], bank("bk"), bk_row[:], ALU.add), "bk")
            normed(2, 0)

            GA, SB, CB, GB = range(4)
            ga, gb = mod2[:, GA, :], mod2[:, GB, :]

            def modulation(v, b):
                dve.wait_ge(wmv_in[v], 16)
                if b == 0:
                    ins = nc.vector.tensor_scalar(mod2[:, v, :], wm_in[:, v % 2, b, :], c_col[:, 2, b:b + 1], None, ALU.mult)
                else:
                    dve.wait_ge(mod2_done, KB * v + b)
                    ins = nc.vector.scalar_tensor_tensor(out=mod2[:, v, :], in0=wm_in[:, v % 2, b, :],
                                                         scalar=c_col[:, 2, b:b + 1], in1=mod2[:, v, :],
                                                         op0=ALU.mult, op1=ALU.add)
                ins.then_inc(mod2_done, 1)

            def gate(j, v):
                dve.wait_ge(prep_taken, TAKE[j] + 1)
                g, sign = wtmp[:, 1, :], wtmp[:, 0, :]
                link(nc.vector.tensor_scalar(sign, g, 0.0, 2.0, ALU.is_ge, ALU.mult))
                link(nc.vector.tensor_scalar(sign, sign, 1.0, None, ALU.subtract))
                link(nc.vector.tensor_tensor(g, g, sign, ALU.mult))
                link(nc.vector.scalar_tensor_tensor(out=mod2[:, v, :], in0=g, scalar=0.25,
                                                    in1=sign, op0=ALU.max, op1=ALU.mult))

            def scaled(i):
                for j in prep_job(i, 1):
                    if j in TMP:
                        scalar = cb1_col[:, int(j[-1]):int(j[-1]) + 1] if j[:2] == "fv" else 0.5
                        full(j)
                        nc.vector.scalar_tensor_tensor(out=wtmp[:, TMP[j] % 2, :], in0=bank(j), scalar=scalar, in1=gb,
                                                       op0=ALU.mult, op1=ALU.mult).then_inc(prep_tmp, 1)

            def tmp_low(j, lo, hi):
                dve.wait_ge(prep_tmp, TMP[j] + 1)
                dve.wait_ge(prep_hi, HI[j] + 1)
                return nc.vector.tensor_tensor(lo, wtmp[:, TMP[j] % 2, :], f32(hi), ALU.subtract)

            LOGITS = slice(HID + PV, C)

            def prepare(i, n):
                for j in prep_job(i, n):
                    b = int(j[-1]) if j[-1].isdigit() else 0
                    if j == "bk":
                        continue
                    if j in ("v0", "v1", "v2", "v3"):
                        dve.wait_ge(prep_taken, TAKE[j] + 1)
                        accumulate(acc_v[:], wvT[:, b, :], sa_col[:, b:b + 1], b == 0)
                        continue
                    if j[:3] == "cat":
                        dve.wait_ge(prep_taken, TAKE[j] + 1)
                        link(nc.vector.tensor_reduce(small[:, 0:1], catT[:, b, LOGITS], AX.X, ALU.add))
                        link(nc.vector.tensor_scalar(small[:, 1:2], small[:, 0:1], 1.0 / E, None, ALU.mult))
                        nc.vector.tensor_scalar(catT[:, b, LOGITS], catT[:, b, LOGITS], small[:, 1:2], None,
                                                ALU.subtract).then_inc(cat_done, 1)
                        dve.wait_ge(cat_done, b + 1)
                        accumulate(acc_c[:], catT[:, b, :], fbv_col[:, b:b + 1], b == 0)
                        continue
                    if j in ("ga", "gb"):
                        gate(j, GA if j == "ga" else GB)
                        if j == "ga":
                            link(nc.vector.tensor_tensor(bo_ga[:], bo_ga[:], ga, ALU.mult))
                        continue
                    full(j)
                    if j == "bq":
                        taken_by(nc.vector.tensor_tensor(bq_row[:], bank(j), bq_row[:], ALU.add), j)
                    elif j == "bv":
                        taken_by(nc.vector.tensor_copy(bias_cols[:], bank(j)[:, 0:2 * KB]), j)
                    elif j[0] == "o":
                        taken_by(nc.vector.tensor_tensor(woT[:, b, :], bank(j), ga, ALU.mult), j)
                    elif j == "sb":
                        nc.vector.tensor_copy(sb_col[:], bank(j)[:, 0:KB])
                        taken_by(nc.vector.tensor_scalar(cb1_col[:], bank(j)[:, KB:2 * KB], 1.0, None, ALU.add), j)
                    elif j[:2] == "fv":
                        tmp_low(j, v_lo[:, b, :], v_hi[:, b, :])
                        accumulate(acc_fv[:], bank(j), sb_col[:, b:b + 1], b == 0)
                    elif j[0] == "u":
                        low(j, cb1_col[:, b:b + 1], c_hi[:, b, :], c_lo[:, b, :])
                        accumulate(acc_c[:], bank(j)[:, 0:C], sb_col[:, b:b + 1], False)
                    elif j == "bc":
                        dve.wait_ge(w2_in, 16 * SMALL_LOADS)
                        link(nc.vector.memset(bcat[:, HID:HID + PV], 0.0))
                        link(nc.vector.tensor_reduce(small[:, 0:1], bcat[:, LOGITS], AX.X, ALU.add))
                        link(nc.vector.tensor_scalar(small[:, 1:2], small[:, 0:1], 1.0 / E, None, ALU.mult))
                        link(nc.vector.tensor_scalar(bcat[:, LOGITS], bcat[:, LOGITS], small[:, 1:2], None, ALU.subtract))
                        taken_by(nc.vector.tensor_tensor(bf_row[:], bank(j)[:, 0:C], bcat[:], ALU.add), j)
                    elif j == "bfv":
                        taken_by(nc.vector.tensor_tensor(b2raw[:], bank(j), b2raw[:], ALU.add), j)
                        link(nc.vector.tensor_tensor(b2raw[:], b2raw[:], gb, ALU.mult))
                        for h in range(2):
                            hi, lo = slice(64 * h, 64 * h + 2 * E), slice(64 * h + 32, 64 * h + 32 + E)
                            nc.vector.tensor_copy(b2st[hi, h, :], b2raw[hi, :])
                            link(nc.vector.tensor_copy(b2st[lo, h, :], b2raw[lo, :]))
                            link(nc.vector.tensor_tensor(b2st[lo, h, :], b2raw[lo, :], f32(b2st[lo, h, :]), ALU.subtract))
                    else:
                        taken_by(tmp_low(j, w2_lo[:, b, :], w2_hi[:, b, :]), j)

            def b2_and_value_bias():
                dve.wait_ge(w2_in, 16 * SMALL_LOADS)
                nc.vector.memset(f32(b2st[:]), 0.0)
                link(nc.vector.tensor_tensor(b2raw[:], b2raw[:], fbv_row[:], ALU.add))

            def router_constants():
                dve.wait_ge(al_exp, 1)
                link(nc.vector.tensor_scalar(al[:, 2:3], al[:, 1:2], 1.0, None, ALU.add))
                link(nc.vector.reciprocal(al[:, 3:4], al[:, 2:3]))
                link(nc.vector.tensor_scalar(rt[:, 2, :], rt[:, 2, :], al[:, 3:4], None, ALU.mult))
                link(nc.vector.scalar_tensor_tensor(out=rt[:, 4, :], in0=rt[:, 3, :], scalar=al[:, 3:4], in1=rt[:, 0, :],
                                                    op0=ALU.mult, op1=ALU.add))
                nc.vector.tensor_copy(small[:, 0:1], bf_row[:, 0:1]).then_inc(weights_ready, 1)

            def step(i, s):
                if live(i - 1, T):
                    dve.wait_ge(q_psum, i)
                    wait_count(dve, eq_done, i - 2)
                    nc.vector.tensor_tensor(zq[:, 1 - s, :], bank_q, bq_row[:], ALU.add).then_inc(zq_done, 1)
                if live(i + 1, T):
                    xT_low(i + 1, 1 - s)
                ahead = live(i + 2, T) and not (isinstance(i, int) and i + 2 <= 2)
                if ahead:
                    statistics(i + 2, s)
                if live(i - 1, T):
                    dve.wait_ge(eq_done, i)
                    wait_count(dve, q_out[1 - s], landed(i - 1, 1 - s) - 16)
                    nc.vector.scalar_tensor_tensor(out=qf[:, 1 - s, :], in0=zq[:, 1 - s, :], scalar=0.0,
                                                   in1=exp_q[:, 1 - s, :], op0=ALU.max, op1=ALU.add).then_inc(qf_done, 1)
                if ahead:
                    mean_var(i + 2, s)
                if live(i, T):
                    dve.wait_ge(k_psum, i + 1)
                    wait_count(dve, ek_done, i - 1)
                    nc.vector.tensor_tensor(zk[:, s, :], bank_k, bk_row[:], ALU.add).then_inc(zk_done, 1)
                prepare(i, 0)
                if ahead:
                    var_eps(i + 2, s)
                    normed(i + 2, s)
                if live(i, T):
                    dve.wait_ge(ek_done, i + 1)
                    wait_count(dve, kh_done, i - 1)
                    wait_count(dve, ks_done, i - 1)
                    nc.vector.scalar_tensor_tensor(out=kf[:, s, :], in0=zk[:, s, :], scalar=0.0,
                                                   in1=exp_k[:, s, :], op0=ALU.max, op1=ALU.add).then_inc(kf_done, 1)
                    scaled(i)
                    dve.wait_ge(kf_done, i + 1)
                    dve.wait_ge(kh_done, i + 1)
                    wait_count(dve, m_done, i - 1)
                    nc.vector.tensor_tensor(k_lo[:, s, :], kf[:, s, :], f32(k_hi[:, s, :]), ALU.subtract).then_inc(kl_done, 1)
                if isinstance(i, int) and 1 <= i <= 2 * KB:
                    for n in (2 * i - 2, 2 * i - 1):
                        modulation(n // KB, n % KB)
                prepare(i, 1)
                prepare(i, 2)
                if isinstance(i, int) and i == 16:
                    b2_and_value_bias()
                if isinstance(i, int) and i == PREP_STEPS - 1:
                    router_constants()

            sweep(dve, step, 0, T, *LOOP_A)

            dve.wait_ge(m_done, T)
            dve.wait_ge(ks_done, T)
            dve.wait_ge(pool_const, 2)
            for b in (0, 1):
                nc.vector.tensor_scalar(mt[b], ps[:, b, :], ca1_col[:, b:b + 1], None, ALU.mult).then_inc(mt_dve, 1)
            full("ks")
            nc.vector.tensor_copy(ks_row[:], bank("ks")).then_inc(ks_row_done, 1)
            dve.wait_ge(ks_row_done, 1)
            for b in range(KB):
                blk = slice(b * P, (b + 1) * P)
                last = nc.vector.scalar_tensor_tensor(out=outer[:, b, :], in0=ks_row[:, blk], scalar=bvp_col[:, b:b + 1],
                                                      in1=headmask[:], op0=ALU.mult, op1=ALU.mult)
            taken_by(last, "ks")
            g_rows, bias_row = rt[:, 1:3, :].rearrange("p k e -> p (k e)"), rt[:, 4, :]

            def over(ap, shape):
                return ap.unsqueeze(2).to_broadcast(shape)

            def denominators(j):
                dve.wait_ge(qks_done, j + 1)
                nc.vector.tensor_reduce(den[:].rearrange("p h n -> p (h n)"),
                                        qks[:].rearrange("p h (n d) -> p (h n) d", d=DH), AX.X, ALU.add).then_inc(den_done, 1)
                dve.wait_ge(den_done, j + 1)
                nc.vector.tensor_scalar(den_eps[:], den[:], 1e-6, None, ALU.add).then_inc(deneps_done, 1)
                dve.wait_ge(deneps_done, j + 1)
                wait_count(dve, qz_done, j)
                nc.vector.reciprocal(zr[:], den_eps[:]).then_inc(zr_done, 1)

            full("kv")
            for b in (0, 2):
                pair = slice(b, b + 2)
                kv = bank("kv")[:, b * P:(b + 2) * P].rearrange("p (b n) -> p b n", n=P)
                link(nc.vector.tensor_tensor(kvm[:, pair, :], kv,
                                             headmask[:].unsqueeze(1).to_broadcast([P, 2, P]), ALU.mult))
                nc.vector.tensor_tensor(kvm[:, pair, :], kvm[:, pair, :], outer[:, pair, :],
                                        ALU.add).then_inc(kvm_done, 1)
            dve.wait_ge(kvm_done, 2)
            nc.vector.tensor_copy(small[:, 0:1], kvm[:, 0, 0:1]).then_inc(prep_taken, 1)
            denominators(0)
            dve.wait_ge(b_cleared, 3)
            for b in range(KB):
                j = f"g{b}"
                dve.wait_ge(prep_hi, HI[j] + 1)
                nc.vector.tensor_tensor(g_lo[:, b, :], bank(j), f32(g_hi[:, b, :]), ALU.subtract).then_inc(prep_taken, 1)

            def residual(j, h):
                t = 2 * j + h
                dve.wait_ge(o_psum, t + 1)
                dve.wait_ge(xb_done, j + 1)
                nc.vector.tensor_tensor(x1_of(j, h), bank_o, xb[:, h, :], ALU.add).then_inc(x1_done, 1)
                wait_apart(x1_done, t + 1)
                nc.vector.bn_stats(stats[:, h, :], x1_of(j, h)).then_inc(bstats_done, 1)

            def moments(j):
                for h in range(2):
                    wait_apart(bstats_done, 2 * j + h + 1)
                    nc.vector.bn_aggr(mv[:, h, :], stats[:, h, :]).then_inc(bmv_done, 1)
                dve.wait_ge(bmv_done, 2 * j + 2)
                nc.vector.tensor_scalar(veps[:], mv[:, :, 1], EPS, None, ALU.add).then_inc(bveps_done, 1)

            def normalised(j, h):
                t = 2 * j + h
                dve.wait_ge(brstd_done, j + 1)
                wait_count(dve, x2T_psum, t - 1)
                nc.vector.tensor_scalar(xn[:, h, :], x1_of(j, h), mv[:, h, 0:1], rstd[:, h:h + 1],
                                        ALU.subtract, ALU.mult).then_inc(x2_done, 1)

            def x2T_low(j, h):
                t = 2 * j + h
                dve.wait_ge(x2Th_done, t + 1)
                nc.vector.tensor_tensor(xT_lo[:, h, :], bank_x2T, f32(xT_hi[:, h, :]), ALU.subtract).then_inc(x2Tl_done, 1)

            def qT_low(j, h):
                t = 2 * j + h
                dve.wait_ge(qTh_done, t + 1)
                nc.vector.tensor_tensor(qT_lo[:, h, :], bank_qaT, f32(qT_hi[:, h, :]), ALU.subtract).then_inc(qTl_done, 1)

            def aT_low(j, h):
                t = 2 * j + h
                dve.wait_ge(aTh_done, t + 1)
                nc.vector.tensor_tensor(aT_lo[:, h, :], bank_qaT[:, 0:2 * P], f32(aT_hi[:, h, :]),
                                        ALU.subtract).then_inc(aTl_done, 1)

            def biased(j, h):
                t = 2 * j + h
                dve.wait_ge(f_psum, t + 1)
                nc.vector.tensor_tensor(zf[:, h, 0:C], bank_f[:, 0:C], bf_row[:], ALU.add).then_inc(zf_done, 1)

            def probes(j, h):
                t = 2 * j + h
                dve.wait_ge(sq_done, t + 1)
                nc.vector.tensor_reduce(c2[:, h, :], sq[:, h, :].rearrange("p (e q) -> p e q", q=PD),
                                        AX.X, ALU.add).then_inc(c2_done, 1)

            def finished(j, h):
                t = 2 * j + h
                dve.wait_ge(y_psum, t + 1)
                if isinstance(j, int) and j == 0:
                    dve.wait_ge(q_out[h], landed(T - 2 + h, h))
                wait_count(dve, stored[h], 16 * j)
                nc.vector.tensor_tensor(out_t[:, h, :], bank_y(h),
                                        x1_of(j, h), ALU.add).then_inc(fin_done, 1)

            def gated(j):
                dve.wait_ge(th_done, 2 * j + 2)
                nc.vector.scalar_tensor_tensor(out=hz[:], in0=th[:], scalar=1.0, in1=zf[:, :, 0:HID],
                                               op0=ALU.add, op1=ALU.mult).then_inc(hz_done, 1)

            def variances(j):
                dve.wait_ge(cn_done, 2 * j + 2)
                nc.vector.tensor_reduce(csum[:], cn[:], AX.X, ALU.add).then_inc(csum_done, 1)
                dve.wait_ge(csum_done, j + 1)
                nc.vector.scalar_tensor_tensor(out=zf[:, :, C:C + E], in0=over(csum[:], [P, 2, E]), scalar=-1.0 / E,
                                               in1=cn[:], op0=ALU.mult, op1=ALU.add).then_inc(cc_done, 1)
                dve.wait_ge(cc_done, j + 1)
                rc = zf[:, :, HID + PV:C + E]
                nc.vector.tensor_tensor(rsq[:].rearrange("p h k e -> p h (k e)"), rc, rc, ALU.mult).then_inc(rsq_done, 1)
                dve.wait_ge(rsq_done, j + 1)
                nc.vector.tensor_reduce(rvar[:], rsq[:].rearrange("p h k e -> p (h k) e"), AX.X, ALU.add).then_inc(rvar_done, 1)
                dve.wait_ge(rvar_done, j + 1)
                nc.vector.tensor_scalar(rve[:], rvar[:], 1.0 / E, EPS, ALU.mult, ALU.add).then_inc(rve_done, 1)

            def scores(j):
                dve.wait_ge(rrs_done, j + 1)
                nc.vector.tensor_tensor(s1[:], zf[:, :, HID + PV:C + E].rearrange("p h (k e) -> p h k e", e=E),
                                        rrs[:].unsqueeze(3).to_broadcast([P, 2, 2, E]), ALU.mult).then_inc(s1_done, 1)
                dve.wait_ge(s1_done, j + 1)
                nc.vector.tensor_tensor(s2[:].rearrange("p h k e -> p h (k e)"), s1[:].rearrange("p h k e -> p h (k e)"),
                                        g_rows.unsqueeze(1).to_broadcast([P, 2, 2 * E]), ALU.mult).then_inc(s2_done, 1)
                dve.wait_ge(s2_done, j + 1)
                nc.vector.tensor_tensor(s3[:], s2[:, :, 0, :], s2[:, :, 1, :], ALU.add).then_inc(s3_done, 1)
                dve.wait_ge(s3_done, j + 1)
                nc.vector.tensor_tensor(sx[:, :, 0:E], s3[:], bias_row.unsqueeze(1).to_broadcast([P, 2, E]),
                                        ALU.add).then_inc(sx_done, 1)
                wait_apart(sx_done, j + 1)
                for h in range(2):
                    nc.vector.max(m8[:, h, :], sx[:, h, 0:E]).then_inc(m8_done, 1)
                dve.wait_ge(m8_done, 2 * j + 2)
                nc.vector.tensor_copy(top[:, :, 0:2], m8[:, :, 0:2]).then_inc(top_done, 1)
                nc.vector.tensor_tensor(sm[:], sx[:, :, 0:E], over(m8[:, :, 0], [P, 2, E]), ALU.subtract).then_inc(sm_done, 1)
                wait_apart(top_done, j + 1)
                for h in range(2):
                    nc.vector.match_replace(marked[:, h, 0:14], top[:, h, :], sx[:, h, 0:14], TAKEN).then_inc(marked_done, 1)
                dve.wait_ge(marked_done, 2 * j + 2)
                nc.vector.tensor_tensor(mask[:], marked[:, :, 0:E], sx[:, :, 0:E], ALU.not_equal).then_inc(mask_done, 1)

            def weights(j):
                dve.wait_ge(ex_done, j + 1)
                dve.wait_ge(mask_done, j + 1)
                nc.vector.tensor_tensor(wn[:], ex[:], mask[:], ALU.mult).then_inc(wn_done, 1)
                dve.wait_ge(wn_done, j + 1)
                nc.vector.tensor_reduce(wsum[:], wn[:], AX.X, ALU.add).then_inc(wsum_done, 1)
                dve.wait_ge(wsum_done, j + 1)
                nc.vector.reciprocal(winv[:], wsum[:]).then_inc(winv_done, 1)
                dve.wait_ge(winv_done, j + 1)
                nc.vector.tensor_tensor(wt[:], wn[:], over(winv[:], [P, 2, E]), ALU.mult).then_inc(wt_done, 1)
                dve.wait_ge(wt_done, j + 1)
                dve.wait_ge(hz_done, j + 1)
                wait_count(dve, aT_psum, 2 * j)
                ws_pair = ws[:].rearrange("p (h r e) -> p h r e", h=2, r=2)
                nc.vector.tensor_copy(ws_pair[:, :, :, 0:E].bitcast(F32R),
                                      wt[:].unsqueeze(2).to_broadcast([P, 2, 2, E])).then_inc(wth_done, 1)
                nc.vector.tensor_tensor(
                    aw[:].rearrange("p h (e i) -> p h e i", i=INNER),
                    hz[:].rearrange("p h (e i) -> p h e i", i=INNER),
                    wt[:].unsqueeze(3).to_broadcast([P, 2, E, INNER]), ALU.mult)
                dve.wait_ge(wth_done, j + 1)
                nc.vector.tensor_tensor(ws_pair[:, :, 0, E:2 * E], wt[:], ws_pair[:, :, 0, 0:E],
                                        ALU.subtract).then_inc(aw_done, 1)

            def step_b(j):
                if live(j - 1, J):
                    x2T_low(j - 1, 1)
                if live(j - 2, J):
                    weights(j - 2)
                if live(j, J):
                    residual(j, 0)
                if isinstance(j, int) and j == 0:
                    denominators(1)
                if live(j - 1, J):
                    biased(j - 1, 0)
                if live(j - 2, J):
                    aT_low(j - 2, 0)
                if live(j - 1, J):
                    probes(j - 1, 0)
                if live(j, J):
                    residual(j, 1)
                    moments(j)
                if live(j - 2, J):
                    aT_low(j - 2, 1)
                    finished(j - 2, 0)
                if live(j, J):
                    normalised(j, 0)
                if live(j - 1, J):
                    biased(j - 1, 1)
                    probes(j - 1, 1)
                if live(j, J):
                    normalised(j, 1)
                if live(j - 1, J):
                    gated(j - 1)
                if live(j - 2, J):
                    finished(j - 2, 1)
                if live(j + 1, J):
                    qT_low(j + 1, 0)
                if isinstance(j, int) and j == -1:
                    qT_low(0, 1)
                if live(j - 1, J):
                    variances(j - 1)
                if live(j + 2, J) and not (isinstance(j, int) and j <= 0):
                    denominators(j + 2)
                if live(j, J):
                    x2T_low(j, 0)
                if live(j - 1, J):
                    scores(j - 1)
                if live(j + 1, J) and not (isinstance(j, int) and j == -1):
                    qT_low(j + 1, 1)
                if isinstance(j, int) and j == 0:
                    denominators(2)

            sweep_pairs(dve, step_b, -1, J + 1, *LOOP_B)

        @block.tensor
        def _(pe):
            pe.wait_ge(dve_const, 1)
            pe.wait_ge(pool_const, 1)

            def three(dst, parts, start, stop, low_ready=None, n_low=0):
                for n, (ah, al_, bh, bl) in enumerate(parts):
                    nc.tensor.matmul(dst, ah, bh, start=start and n == 0, stop=False)
                    nc.tensor.matmul(dst, ah, bl, start=False, stop=False)
                if low_ready is not None:
                    pe.wait_ge(low_ready, n_low)
                for n, (ah, al_, bh, bl) in enumerate(parts):
                    last = nc.tensor.matmul(dst, al_, bh, start=False, stop=stop and n == len(parts) - 1)
                return last

            def transposes(j, srcs):
                bank_free(pe, j)
                col = 0
                for src in srcs:
                    k = src.shape[0]
                    last = nc.tensor.transpose(bank(j)[:, col:col + k], src, ident[0:k, 0:k])
                    col += k
                last.then_inc(prep_psum, 1)

            def blocks_of(raw, fb):
                return [raw[:, r, fb * P:(fb + 1) * P] for r in range(KB)]

            def sum_rows(j, acc):
                bank_free(pe, j)
                nc.tensor.matmul(bank(j)[:, 0:acc.shape[1]], ones[:], acc, start=True, stop=True).then_inc(prep_psum, 1)

            def warm_up(bank, n):
                for _ in range(n):
                    nc.tensor.matmul(ps[:, bank, 0:P], ones[:], ones[:], start=True, stop=True)

            warm_up(5, WARM_UP)
            def columns(j, col, parts):
                for b in range(KB):
                    for n, (part, pick) in enumerate(parts):
                        last = nc.tensor.matmul(bank(j)[:, col + b:col + b + 1], part[:, b * P:(b + 1) * P], pick,
                                                start=(n == 0), stop=(n == len(parts) - 1))
                return last

            all_rows, first_row = ones[:, 0:1], ident[:, 0:1]
            pe.wait_ge(mod1_done, KB)
            columns("sa", 0, [(mod1[:, 0, :], all_rows)])
            columns("sa", KB, [(mod1[:, 1, :], all_rows)]).then_inc(prep_psum, 1)
            pe.wait_ge(wk_in, 16)
            for b in range(KB):
                transposes(f"k{b}", blocks_of(raw_k, b))
            pe.wait_ge(wq_in, 16)
            for b in range(KB):
                transposes(f"q{b}", blocks_of(raw_q, b))
            SUMS = {"ga": 0, "gb": 3}

            def prepare(i, n):
                for j in prep_job(i, n):
                    b = int(j[-1]) if j[-1].isdigit() else 0
                    if j == "bk":
                        pe.wait_ge(acc_step, SUMMED["k3"] + 1)
                        sum_rows(j, acc_k[:])
                    elif j == "bq":
                        pe.wait_ge(acc_step, SUMMED["q3"] + 1)
                        sum_rows(j, acc_q[:])
                    elif j in SUMS:
                        pe.wait_ge(mod2_done, KB * (SUMS[j] + 1))
                        sum_rows(j, mod2[:, SUMS[j], :])
                    elif j == "bv":
                        pe.wait_ge(acc_step, 3 * KB)
                        pe.wait_ge(rows_in, 48)
                        bank_free(pe, j)
                        columns(j, 0, [(acc_v[:], all_rows), (bv_row[:], first_row)])
                        columns(j, KB, [(fbv_row[:], first_row)]).then_inc(prep_psum, 1)
                    elif j == "sb":
                        pe.wait_ge(mod2_done, 3 * KB)
                        bank_free(pe, j)
                        columns(j, 0, [(mod2[:, 1, :], all_rows)])
                        columns(j, KB, [(mod2[:, 2, :], all_rows)]).then_inc(prep_psum, 1)
                    elif j[0] == "v":
                        pe.wait_ge(v_in, 16)
                        transposes(j, blocks_of(raw_v, b))
                    elif j[0] == "o":
                        pe.wait_ge(o_in, 16)
                        transposes(j, blocks_of(raw_o, b))
                    elif j[:3] == "cat":
                        pe.wait_ge(cat_in, 48)
                        blk = slice(b * P, (b + 1) * P)
                        transposes(j, [raw_cat[:, 0, blk], raw_cat[:, 1, blk], raw_cat[0:PV + E, 2, blk]])
                    elif j[:2] == "fv":
                        pe.wait_ge(fv_in, 16)
                        transposes(j, blocks_of(raw_fv, b))
                    elif j[0] == "u":
                        pe.wait_ge(cat_done, KB)
                        bank_free(pe, j)
                        for d in range(KB):
                            last = nc.tensor.matmul(bank(j)[:, 0:C], raw_fv[:, d, b * P:(b + 1) * P], catT[:, d, :],
                                                    start=(d == 0), stop=(d == KB - 1))
                        last.then_inc(prep_psum, 1)
                    elif j == "bc":
                        pe.wait_ge(acc_step, 6 * KB)
                        sum_rows(j, acc_c[:])
                    elif j == "bfv":
                        pe.wait_ge(acc_step, 6 * KB)
                        sum_rows(j, acc_fv[:])
                    else:
                        pe.wait_ge(w2_in, 16 * SMALL_LOADS)
                        transposes(j, [raw_w2[:, d, 4 * b:4 * b + 4, :].rearrange("p e i -> p (e i)") for d in range(KB)])

            def step(i, s):
                if live(i + 1, T):
                    pe.wait_ge(xn_done, i + 2)
                    if isinstance(i, int) and i == -1:
                        pe.wait_ge(acc_step, SUMMED["k0"] + 1)
                    wait_count(pe, xTl_done, i + 1)
                    for b in range(KB):
                        blk = slice(b * P, (b + 1) * P)
                        last = nc.tensor.transpose(bank_xT[:, blk], xn[:, 1 - s, blk], ident[:])
                    last.then_inc(xT_psum, 1)
                if live(i, T):
                    if isinstance(i, int) and i == 0:
                        pe.wait_ge(wlo_done, KB)
                        pe.wait_ge(acc_step, SUMMED["q0"] + 1)
                    pe.wait_ge(xTh_done, i + 1)
                    wait_count(pe, zk_done, i)
                    three(bank_k, [(xT_hi[:, s, b * P:(b + 1) * P], xT_lo[:, s, b * P:(b + 1) * P],
                                    wk_hi[:, b, :], wk_lo[:, b, :]) for b in range(KB)], True, True,
                          xTl_done, i + 1).then_inc(k_psum, 1)
                prepare(i, 0)
                if live(i - 1, T):
                    p = 1 - s
                    first = isinstance(i, int) and i == 1
                    final = isinstance(i, int) and i == T
                    if first:
                        pe.wait_ge(prep_taken, TAKE["bq"] + 1)
                    pe.wait_ge(xnl_done, i)
                    pe.wait_ge(kl_done, i)
                    for b in range(KB):
                        blk = slice(b * P, (b + 1) * P)
                        last = three(ps[:, b, :], [(xn_hi[:, p, blk], xn_lo[:, p, blk], k_hi[:, p, :], k_lo[:, p, :])],
                                     first, final)
                    last.then_inc(m_done, 1)
                prepare(i, 1)
                if live(i, T):
                    if isinstance(i, int) and i == 0:
                        pe.wait_ge(wlo_done, 2 * KB)
                        pe.wait_ge(acc_step, SUMMED["q1"] + 1)
                    wait_count(pe, zq_done, i)
                    three(bank_q, [(xT_hi[:, s, b * P:(b + 1) * P], xT_lo[:, s, b * P:(b + 1) * P],
                                    wq_hi[:, b, :], wq_lo[:, b, :]) for b in range(KB)], True, True).then_inc(q_psum, 1)
                prepare(i, 2)

            sweep(pe, step, -1, T, *LOOP_A)

            pe.wait_ge(ks_done, T)
            sum_rows("ks", ks_acc[:])
            pe.wait_ge(zk_done, T)
            for b in range(KB):
                blk = slice(b * P, (b + 1) * P)
                for f, ready, n in ((0, mt_dve, 1), (2, mt_act, 1), (1, mt_dve, 2), (3, mt_act, 2)):
                    pe.wait_ge(ready, n)
                    last = nc.tensor.matmul(bank("kv")[:, blk], wvT[:, f, blk], mt[f][:, blk],
                                            start=(f == 0), stop=(f == KB - 1))
            last.then_inc(prep_psum, 1)
            for b in range(KB):
                pe.wait_ge(kvm_done, b // 2 + 1)
                nc.tensor.matmul(bank(f"g{b}"), kvm[:, b, :], woT[:, b, :], start=True, stop=True).then_inc(prep_psum, 1)

            def out_product(j, h):
                t = 2 * j + h
                pe.wait_ge(qTh_done, t + 1)
                wait_count(pe, x1_done, t)
                three(bank_o, [(qT_hi[:, h, b * P:(b + 1) * P], qT_lo[:, h, b * P:(b + 1) * P],
                                g_hi[:, b, :], g_lo[:, b, :]) for b in range(KB)], True, True,
                      qTl_done, t + 1).then_inc(o_psum, 1)

            def x2_blocks(h):
                return [(xT_hi[:, h, b * P:(b + 1) * P], xT_lo[:, h, b * P:(b + 1) * P]) for b in range(KB)]

            def fused_product(j, h):
                t = 2 * j + h
                pe.wait_ge(x2Th_done, t + 1)
                wait_count(pe, zf_done, t)
                three(bank_f[:, 0:C], [(*a, c_hi[:, b, :], c_lo[:, b, :]) for b, a in enumerate(x2_blocks(h))],
                      True, True, x2Tl_done, t + 1).then_inc(f_psum, 1)

            def value_product(j, h):
                t = 2 * j + h
                wait_count(pe, fin_done, t - 1)
                three(bank_y(h), [(*a, v_hi[:, b, :], v_lo[:, b, :]) for b, a in enumerate(x2_blocks(h))],
                      True, False).then_inc(y_v_done, 1)

            def expert_product(j, h):
                t = 2 * j + h
                pe.wait_ge(aTh_done, t + 1)
                nc.tensor.matmul(bank_y(h), wT_hi[:], b2st[:, h, :], start=False, stop=False)
                three(bank_y(h), [(aT_hi[:, h, b * P:(b + 1) * P], aT_lo[:, h, b * P:(b + 1) * P],
                                   w2_hi[:, b, :], w2_lo[:, b, :]) for b in range(2)], False, True,
                      aTl_done, t + 1).then_inc(y_psum, 1)

            def turn(dst, src, n):
                for b in range(n):
                    blk = slice(b * P, (b + 1) * P)
                    last = nc.tensor.transpose(dst[:, blk], src[:, blk], ident[:])
                return last

            def turn_q(j, h):
                t = 2 * j + h
                pe.wait_ge(qz_done, j + 1)
                if h == 0 and live(j - 3, J):
                    pe.wait_ge(aTl_done, 2 * (j - 3) + 2)
                wait_count(pe, qTl_done, t)
                turn(bank_qaT, qz[:, h, :], KB).then_inc(qT_psum, 1)

            def turn_hidden(j, h):
                t = 2 * j + h
                pe.wait_ge(aw_done, j + 1)
                if h == 0 and live(j + 2, J):
                    pe.wait_ge(qTl_done, 2 * (j + 2) + 2)
                wait_count(pe, aTl_done, t)
                if h == 0:
                    nc.tensor.transpose(bank_qaT[:, 2 * P:3 * P], ws[:], ident[:])
                turn(bank_qaT, aw[:, h, :], 2).then_inc(aT_psum, 1)

            def turn_x2(j, h):
                t = 2 * j + h
                pe.wait_ge(x2_done, t + 1)
                wait_count(pe, x2Tl_done, t)
                turn(bank_x2T, xn[:, h, :], KB).then_inc(x2T_psum, 1)

            def step_b(j):
                if isinstance(j, int) and j == 0:
                    pe.wait_ge(prep_taken, len(TAKE))
                    pe.wait_ge(weights_ready, 1)
                    pe.wait_ge(zq_done, T)
                if live(j, J):
                    out_product(j, 0)
                if live(j - 1, J):
                    fused_product(j - 1, 0)
                if isinstance(j, int) and j >= J:
                    warm_up(2, 5)
                if live(j - 2, J):
                    turn_hidden(j - 2, 0)
                    if isinstance(j, int) and j >= J:
                        warm_up(2, 3)
                if live(j, J):
                    out_product(j, 1)
                fill_step = isinstance(j, int) and j == 0
                if fill_step:
                    warm_up(2, 6)
                if live(j - 2, J):
                    expert_product(j - 2, 0)
                    turn_hidden(j - 2, 1)
                if live(j - 1, J):
                    fused_product(j - 1, 1)
                if live(j - 2, J):
                    expert_product(j - 2, 1)
                if live(j + 1, J):
                    turn_q(j + 1, 0)
                if fill_step:
                    warm_up(2, 4)
                if live(j - 1, J):
                    value_product(j - 1, 0)
                if live(j, J):
                    turn_x2(j, 0)
                if live(j + 1, J):
                    turn_q(j + 1, 1)
                if live(j - 1, J):
                    value_product(j - 1, 1)
                if live(j, J):
                    turn_x2(j, 1)

            sweep_pairs(pe, step_b, -1, J + 1, *LOOP_B)


_INS = ["L0_attn_hidden_states", "L0_attn_Wq", "L0_attn_bq", "L0_attn_Wk", "L0_attn_bk", "L0_attn_Wv",
        "L0_attn_bv", "L0_attn_Wo", "L0_attn_bo", "L0_ffn_Wv", "L0_ffn_bv", "L0_ffn_Wg", "L0_ffn_bg",
        "L0_ffn_Wp", "L0_ffn_alpha", "L0_ffn_g_r", "L0_ffn_b_r", "L0_ffn_g_c", "L0_ffn_b_c", "L0_ffn_W1",
        "L0_ffn_b1", "L0_ffn_W2", "L0_ffn_b2", "L0_c", "L0_wmod"]


def kernel(**inputs):
    import numpy as _np
    import concourse.bacc as _bacc
    from concourse import mybir as _mybir
    from concourse.bass_utils import run_bass_kernel_spmd as _run

    nc = _bacc.Bacc("TRN2", target_bir_lowering=False, num_devices=1)
    arrays, args = {}, []
    for name in _INS:
        a = _np.ascontiguousarray(inputs[name])
        if name == "L0_ffn_alpha":
            a = a.reshape(1, 1)
        arrays[f"in_{name}_dram"] = a
        args.append(nc.dram_tensor(f"in_{name}_dram", a.shape, _mybir.dt.from_np(a.dtype), kind="ExternalInput").ap())
    shape = inputs["L0_attn_hidden_states"].shape
    args.append(nc.dram_tensor("out_0_dram", shape, _mybir.dt.float32, kind="ExternalOutput").ap())
    build(nc, *args)
    r = _run(nc, [arrays], core_ids=[0])
    return r.results[0]["out_0_dram"]
```
